# Optimizing a Trainium2 kernel written in Bass

```python
import numpy as np
import jax
import jax.numpy as jnp

def _softmax(x, axis=-1):
    return jax.nn.softmax(x, axis=axis)

def _gelu(x):
    return jax.nn.gelu(x, approximate=True)

def _silu(x):
    return jax.nn.silu(x)

def _sigmoid(x):
    return jax.nn.sigmoid(x)

def _layernorm(x, axis=-1, eps=1e-05):
    m = jnp.mean(x, axis=axis, keepdims=True)
    v = jnp.var(x, axis=axis, keepdims=True)
    return (x - m) / jnp.sqrt(v + eps)

def _scatter_add(tgt, idx, src, axis=0):
    return tgt.at[idx].add(src)

def _segment_sum(src, seg, n):
    return jax.ops.segment_sum(src, seg, n)
kernel_name = 'mk_gnn_resnorm_d2_gnn_r64_8a640f'

def setup_inputs(seed: int=0):
    np.random.seed(seed)
    _w = jnp.asarray

    def _rec_inputs():
        import jax
        import jax.numpy as jnp
        _gk = jax.random.key(seed)
        x = -0.0003713 + 1 * jax.random.normal(jax.random.fold_in(_gk, 1), (50000, 256), jnp.float32)
        src = jax.random.randint(jax.random.fold_in(_gk, 2), (12500,), 0, 50000, jnp.int32)
        dst = jax.random.randint(jax.random.fold_in(_gk, 3), (12500,), 0, 50000, jnp.int32)
        _o = jnp.argsort(dst, stable=True)
        src = src[_o]
        dst = dst[_o]
        edge_attr_64 = jax.random.uniform(jax.random.fold_in(_gk, 11), (12500, 64), jnp.float32, 0.0, 1)
        return (x, src, dst, edge_attr_64)
    x, src, dst, edge_attr_64 = _rec_inputs()

    def _L0_gnn_setup():
        import jax, jax.numpy as jnp
        import numpy as np
        N = 50000
        E = 15625
        IN = 256
        H = 4
        D = 64
        OUT = 256
        key = jax.random.key(seed)
        k0, k1, k2, k3, k4 = jax.random.split(key, 5)
        x = jax.random.normal(k0, (N, IN), dtype=jnp.float32)
        edge_index = jax.random.randint(k1, (2, E), 0, N, dtype=jnp.int32)
        W = jax.random.normal(k2, (H, IN, D), dtype=jnp.float32) * 0.05
        attn = jax.random.normal(k3, (H, 2 * D), dtype=jnp.float32) * 0.05
        W_out = jax.random.normal(k4, (H * D, OUT), dtype=jnp.float32) * 0.05
        return {'x': x, 'edge_index': edge_index, 'W': W, 'attn': attn, 'W_out': W_out}
    _L0_gnn_all = _L0_gnn_setup()
    _L0_gnn_in = {k: v for k, v in _L0_gnn_all.items() if k in ('W', 'attn', 'W_out')}
    del _L0_gnn_all

    def _L1_gnn_setup():
        import jax, jax.numpy as jnp
        import numpy as np
        N = 100000
        E = 25000
        D_NODE = 256
        D_MSG = 128
        D_RAD = 64
        HEADS = 4
        OUTC = D_MSG // HEADS

        def _w(key, shape):
            fan_in = shape[-1]
            return jax.random.normal(key, shape, dtype=jnp.float32) / jnp.sqrt(jnp.float32(fan_in))
        key = jax.random.key(seed)
        ks = jax.random.split(key, 16)
        x = jax.random.normal(ks[0], (N, D_NODE), dtype=jnp.float32)
        edge_attr = jax.random.uniform(ks[1], (E, D_RAD), dtype=jnp.float32)
        edge_index = jax.random.randint(ks[2], (2, E), 0, N, dtype=jnp.int64)
        return {'x': x, 'edge_attr': edge_attr, 'edge_index': edge_index, 'W_edge': _w(ks[3], (D_RAD, D_RAD)), 'W_n2m': _w(ks[4], (D_MSG, D_NODE)), 'Wq': _w(ks[5], (D_MSG, D_MSG)), 'bq': jnp.zeros((D_MSG,), jnp.float32), 'Wk': _w(ks[6], (D_MSG, D_MSG)), 'bk': jnp.zeros((D_MSG,), jnp.float32), 'Wv': _w(ks[7], (D_MSG, D_MSG)), 'bv': jnp.zeros((D_MSG,), jnp.float32), 'We': _w(ks[8], (D_MSG, D_RAD)), 'Wskip': _w(ks[9], (D_MSG, D_MSG)), 'bskip': jnp.zeros((D_MSG,), jnp.float32), 'Wbeta': _w(ks[10], (1, 3 * D_MSG)), 'W_m2n': _w(ks[11], (D_NODE, D_MSG))}
    _L1_gnn_all = _L1_gnn_setup()
    _L1_gnn_in = {k: v for k, v in _L1_gnn_all.items() if k in ('W_edge', 'W_n2m', 'Wq', 'bq', 'Wk', 'bk', 'Wv', 'bv', 'We', 'Wskip', 'bskip', 'Wbeta', 'W_m2n')}
    del _L1_gnn_all
    return {'x': x, 'src': src, 'dst': dst, 'edge_attr_64': edge_attr_64, 'L0_gnn_W': _L0_gnn_in['W'], 'L0_gnn_attn': _L0_gnn_in['attn'], 'L0_gnn_W_out': _L0_gnn_in['W_out'], 'L1_gnn_W_edge': _L1_gnn_in['W_edge'], 'L1_gnn_W_n2m': _L1_gnn_in['W_n2m'], 'L1_gnn_Wq': _L1_gnn_in['Wq'], 'L1_gnn_bq': _L1_gnn_in['bq'], 'L1_gnn_Wk': _L1_gnn_in['Wk'], 'L1_gnn_bk': _L1_gnn_in['bk'], 'L1_gnn_Wv': _L1_gnn_in['Wv'], 'L1_gnn_bv': _L1_gnn_in['bv'], 'L1_gnn_We': _L1_gnn_in['We'], 'L1_gnn_Wskip': _L1_gnn_in['Wskip'], 'L1_gnn_bskip': _L1_gnn_in['bskip'], 'L1_gnn_Wbeta': _L1_gnn_in['Wbeta'], 'L1_gnn_W_m2n': _L1_gnn_in['W_m2n']}

def reference(x, src, dst, edge_attr_64, L0_gnn_W, L0_gnn_attn, L0_gnn_W_out, L1_gnn_W_edge, L1_gnn_W_n2m, L1_gnn_Wq, L1_gnn_bq, L1_gnn_Wk, L1_gnn_bk, L1_gnn_Wv, L1_gnn_bv, L1_gnn_We, L1_gnn_Wskip, L1_gnn_bskip, L1_gnn_Wbeta, L1_gnn_W_m2n):
    import jax
    import jax.numpy as jnp

    def _L0_gnn_ref(x, edge_index, W, attn, W_out):
        import jax, jax.numpy as jnp
        import numpy as np
        N = 50000
        E = 15625
        IN = 256
        H = 4
        D = 64
        OUT = 256
        src, dst = (edge_index[0], edge_index[1])
        h = jnp.einsum('ni,hid->nhd', x, W)
        h_src = h[src]
        h_dst = h[dst]
        a_src, a_dst = (attn[:, :D], attn[:, D:])
        e = jnp.einsum('ehd,hd->eh', h_src, a_src) + jnp.einsum('ehd,hd->eh', h_dst, a_dst)
        e = jnp.where(e > 0, e, 0.2 * e)
        e_max = jax.ops.segment_max(e, dst, num_segments=N)
        e_stable = jnp.minimum(e - e_max[dst], 20.0)
        alpha = jnp.exp(e_stable)
        alpha_sum = jax.ops.segment_sum(alpha, dst, num_segments=N)
        alpha_norm = alpha / (alpha_sum[dst] + 1e-08)
        msg = alpha_norm[:, :, None] * h_src
        out_h = jax.ops.segment_sum(msg, dst, num_segments=N)
        return out_h.reshape(N, H * D) @ W_out

    def _L1_gnn_ref(x, edge_attr, edge_index, W_edge, W_n2m, Wq, bq, Wk, bk, Wv, bv, We, Wskip, bskip, Wbeta, W_m2n):
        import jax, jax.numpy as jnp
        import numpy as np
        N = 100000
        E = 25000
        D_NODE = 256
        D_MSG = 128
        D_RAD = 64
        HEADS = 4
        OUTC = D_MSG // HEADS

        def _w(key, shape):
            fan_in = shape[-1]
            return jax.random.normal(key, shape, dtype=jnp.float32) / jnp.sqrt(jnp.float32(fan_in))
        src = edge_index[0]
        dst = edge_index[1]
        n = x.shape[0]
        scale = 1.0 / jnp.sqrt(jnp.float32(OUTC))
        ee = edge_attr @ W_edge.T
        m = x @ W_n2m.T
        q = (m @ Wq.T + bq).reshape(n, HEADS, OUTC)
        k = (m @ Wk.T + bk).reshape(n, HEADS, OUTC)
        v = (m @ Wv.T + bv).reshape(n, HEADS, OUTC)
        e = (ee @ We.T).reshape(-1, HEADS, OUTC)
        kj = k[src] + e
        alpha = jnp.einsum('ehc,ehc->eh', q[dst], kj) * scale
        amax = jax.ops.segment_max(alpha, dst, num_segments=n)
        expa = jnp.exp(alpha - amax[dst])
        asum = jax.ops.segment_sum(expa, dst, num_segments=n)
        alpha = expa / (asum[dst] + 1e-16)
        msg = (v[src] + e) * alpha[..., None]
        out = jax.ops.segment_sum(msg, dst, num_segments=n)
        out = out.reshape(n, D_MSG)
        x_r = m @ Wskip.T + bskip
        beta = jax.nn.sigmoid(jnp.concatenate([out, x_r, out - x_r], axis=-1) @ Wbeta.T)
        out = beta * x_r + (1.0 - beta) * out
        return out @ W_m2n.T
    edge_index = jnp.stack([src, dst])
    x = _layernorm(x + _L0_gnn_ref(x, edge_index, L0_gnn_W, L0_gnn_attn, L0_gnn_W_out), axis=-1)
    x = _layernorm(x + _L1_gnn_ref(x, edge_attr_64, edge_index, L1_gnn_W_edge, L1_gnn_W_n2m, L1_gnn_Wq, L1_gnn_bq, L1_gnn_Wk, L1_gnn_bk, L1_gnn_Wv, L1_gnn_bv, L1_gnn_We, L1_gnn_Wskip, L1_gnn_bskip, L1_gnn_Wbeta, L1_gnn_W_m2n), axis=-1)
    return x

_drawn_inputs = setup_inputs


def setup_inputs(seed=0):
    import zlib

    import numpy as np

    out = dict(_drawn_inputs(seed))
    spreads = {'L1_gnn_bq': (0.0, 0.8),
     'L1_gnn_bk': (0.0, 0.8),
     'L1_gnn_bv': (0.0, 0.465),
     'L1_gnn_bskip': (0.0, 0.1)}
    factors = {'L0_gnn_attn': 5.388}
    for name, (base, spread) in spreads.items():
        noise = np.random.default_rng([zlib.crc32(name.encode()), seed]).standard_normal(out[name].shape)
        drawn = base * np.exp(spread * noise) if base else spread * noise
        out[name] = jnp.asarray(drawn.astype(out[name].dtype))
    for name, factor in factors.items():
        out[name] = (out[name] * factor).astype(out[name].dtype)
    return out
```

```python
from contextlib import ExitStack

import concourse.bass as bass
from concourse import mybir

ALU = mybir.AluOpType
ACT = mybir.ActivationFunctionType
AX = mybir.AxisListType
F32 = mybir.dt.float32
I32 = mybir.dt.int32

P = 128
N, D = 50000, 256
E = 12500
H, HD = 4, 64
DM, RAD = 128, 64
CH = DM // H
EDGES, TILES = 125, 100
G = 5
QS = TILES // G
ROWS = TILES * P
HP = D + H
VP = DM + H
XL = DM + 1
NT = 3
NROWS = NT * P
NFULL = N // NROWS
NSTEPS = NFULL + 1
BIG = 1.0e38
SKIP = 1 << 17
EPS = 1e-5
RSQRT_SEED = 0x5F3759DF


def at_least(eng, sem, value, turn=None):
    if isinstance(value, int):
        if value > 0:
            eng.wait_ge(sem, value)
    else:
        eng.wait_ge(sem, value)
        if turn is not None:
            eng.sem_inc(turn, 1)


class Own:

    def __init__(self, eng, sem, turn):
        self.eng, self.sem, self.turn, self.base, self.n = eng, sem, turn, 0, 0

    def __call__(self, ins):
        self.n += 1
        ins.then_inc(self.sem, 1)

    def upto(self, n, turn=False):
        at_least(self.eng, self.sem, self.base + n, self.turn if turn else None)

    def done(self, turn=False):
        at_least(self.eng, self.sem, self.base + self.n, self.turn if turn else None)

    def loop(self, i, per):
        self.at, self.per = self.n, per
        self.base = i * per

    def looped(self, times):
        assert self.n - self.at == self.per, (self.n - self.at, self.per)
        self.n, self.base = self.at + self.per * times, 0


def steps(eng, own, per, total, unroll, lag, emit, rounds=1, ahead=0):
    peel = unroll * rounds
    times = (total - peel - ahead) // unroll
    for s in range(peel):
        emit(s, s % unroll, None)
    with eng.Fori(0, times) as i:
        own.loop(i, per)
        for j in range(unroll):
            emit(unroll * i + (peel + j), j, i)
    own.looped(times)
    for s in range(peel + times * unroll, total + lag):
        emit(s, s % unroll, None)


def live(s, lag, total):
    return not isinstance(s, int) or 0 <= s - lag < total


def arrivals(s, j, i, unroll, behind, unit=16, rounds=1):
    if i is None:
        return unit * ((s - behind) // unroll + 1) if s >= behind else 0
    return unit * i + unit * (1 + rounds + (j - behind) // unroll)


def rsqrt(own, y, v, t):
    dve = own.eng
    own(dve.tensor_scalar(t.bitcast(I32), v.bitcast(I32), 1, None, ALU.logical_shift_right))
    own.done()
    own(dve.tensor_scalar(y.bitcast(I32), t.bitcast(I32), -1.0, float(RSQRT_SEED), ALU.mult, ALU.add))
    for _ in range(3):
        own.done()
        own(dve.tensor_tensor(t, y, y, ALU.mult))
        own.done()
        own(dve.scalar_tensor_tensor(out=t, in0=t, scalar=-0.5, in1=v, op0=ALU.mult, op1=ALU.mult))
        own.done()
        own(dve.scalar_tensor_tensor(out=y, in0=t, scalar=1.5, in1=y, op0=ALU.add, op1=ALU.mult))
    own.done()


class Core:

    def __init__(self):
        self.passes = 0

    def name(self, name):
        return f"{name}_{self.passes}"


def setup(nc, c, io):
    c.passes += 1
    with ExitStack() as ctx:
        def sb(name, shape, dt=F32):
            return ctx.enter_context(nc.sbuf_tensor(c.name(name), shape, dt))

        def sem(name):
            return ctx.enter_context(nc.semaphore(c.name(name)))

        w_n2m = sb("w_n2m", [P, D])
        w_sq = sb("w_sq", [P, 4, DM])
        w_sqT = sb("w_sqT", [P, 4, DM])
        w_m2n = sb("w_m2n", [P, 2, DM])
        w_skipn = sb("w_skipn", [P, D])
        w_edge = sb("w_edge", [RAD, RAD])
        w_e = sb("w_e", [P, RAD])
        w_eT = sb("w_eT", [RAD, DM])
        attn = sb("attn", [P, H, 2 * HD])
        prod = sb("prod", [P, 2, H, HD])
        beta = sb("beta", [P, 3])
        wb = sb("wb", [P, 1])
        bs_cols = sb("bs_cols", [P, P])
        zero = sb("zero", [P, P])
        mean_w = sb("mean_w", [P, P])
        xlw = sb("xlw", [P, 2])
        qs_raw = sb("qs_raw", [P, 2, D])
        ldd = sem("ldd")
        ident_ready = sem("ident_ready")
        pool_done = sem("pool_done")
        pe_done = sem("pe_done")
        dve_done = sem("dve_done")
        ps = c.psum
        LOADS = 17

        with nc.Block() as block:
            @block.sync
            def _(sp):
                with nc.allow_non_contiguous_dma(reason="a few short weight rows"):
                    sp.dma_start(w_n2m[:, :], io["L1_gnn_W_n2m"]).then_inc(ldd, 16)
                    for k, name in enumerate(("Wq", "Wk", "Wv", "Wskip")):
                        sp.dma_start(w_sq[:, k, :], io["L1_gnn_" + name]).then_inc(ldd, 16)
                    for k in range(2):
                        sp.dma_start(w_m2n[:, k, :], io["L1_gnn_W_m2n"][k * P:(k + 1) * P, :]).then_inc(ldd, 16)
                        sp.dma_start(c.wo[:, k, :], io["L0_gnn_W_out"][k * P:(k + 1) * P, :]).then_inc(ldd, 16)
                        sp.dma_start(c.wh[:, k, 0:D].rearrange("p (h d) -> p h d", h=H),
                                     io["L0_gnn_W"][:, k * P:(k + 1) * P, :].rearrange("h i d -> i h d")).then_inc(ldd, 16)
                    sp.dma_start(w_edge[:, :], io["L1_gnn_W_edge"]).then_inc(ldd, 16)
                    sp.dma_start(w_e[:, :], io["L1_gnn_We"]).then_inc(ldd, 16)
                    sp.dma_start(attn[:, :, :].rearrange("p h d -> p (h d)"),
                                 io["L0_gnn_attn"].rearrange("(a h) d -> a (h d)", a=1).to_broadcast([P, H * 2 * HD])).then_inc(ldd, 16)
                    for k in range(3):
                        sp.dma_start(beta[:, k:k + 1], io["L1_gnn_Wbeta"][:, k * DM:(k + 1) * DM].rearrange("a d -> d a")).then_inc(ldd, 16)

            @block.scalar
            def _(act):
                with nc.allow_non_contiguous_dma(reason="one bias column"):
                    act.dma_start(c.bq_xr[:, 0:DM], io["L1_gnn_bq"].rearrange("(a d) -> a d", a=1).to_broadcast([P, DM])).then_inc(ldd, 16)
                    act.dma_start(c.bq_xr[:, DM:2 * DM], io["L1_gnn_bskip"].rearrange("(a d) -> a d", a=1).to_broadcast([P, DM])).then_inc(ldd, 16)
                    act.dma_start(c.we2[RAD:RAD + 1, 0:DM], io["L1_gnn_bk"].rearrange("(a d) -> a d", a=1)).then_inc(ldd, 16)
                    act.dma_start(c.we2[RAD:RAD + 1, DM:2 * DM], io["L1_gnn_bv"].rearrange("(a d) -> a d", a=1)).then_inc(ldd, 16)
                    act.dma_start(c.wa_row[:, :], io["L1_gnn_Wbeta"][:, 0:DM].to_broadcast([P, DM])).then_inc(ldd, 16)
                    act.dma_start(c.wc_row[:, :], io["L1_gnn_Wbeta"][:, 2 * DM:3 * DM].to_broadcast([P, DM])).then_inc(ldd, 16)
                    act.dma_start(bs_cols[:, 0:1], io["L1_gnn_bskip"].rearrange("(d a) -> d a", a=1)).then_inc(ldd, 16)

            loads = 16 * (1 + 4 + 6 + 2 + 1 + 3 + 7)

            @block.gpsimd
            def _(pool):
                own = Own(pool, pool_done, None)
                own(pool.memset(c.ident[:, :], 0.0))
                own(pool.memset(zero[:, :], 0.0))
                own(pool.memset(mean_w[:, :], 1.0 / D))
                own(pool.memset(xlw[:, :], 0.0))
                own.done()
                pool.affine_select(out=c.ident[:, :], in_=c.ident[:, :], compare_op=ALU.not_equal, fill=1.0,
                                   base=0, pattern=[[-1, P]], channel_multiplier=1).then_inc(ident_ready, 1)

            def bank(b, rows, cols):
                return ps[0:rows, b, 0:cols]

            @block.tensor
            def _(pe):
                pe.wait_ge(ident_ready, 1)
                pe.wait_ge(ldd, loads)
                for k in range(4):
                    pe.transpose(ps[:, 0, k * P:(k + 1) * P], w_sq[:, k, :], c.ident[:, :])
                for k in range(2):
                    pe.transpose(ps[:, 1, k * P:(k + 1) * P], w_m2n[:, k, :], c.ident[:, :])
                pe.transpose(ps[0:RAD, 2, 0:P], w_e[:, :], c.ident[:, :]).then_inc(pe_done, 1)
                pe.wait_ge(dve_done, 9)
                for k in range(2):
                    lhs = w_n2m[:, k * P:(k + 1) * P]
                    for n, w in enumerate((0, 3)):
                        pe.matmul(ps[:, 3, n * DM:(n + 1) * DM] if k == 0 else ps[:, 4, n * DM:(n + 1) * DM], lhs, w_sqT[:, w, :], start=True, stop=True)
                    for n, w in enumerate((1, 2)):
                        pe.matmul(ps[:, 5, n * DM:(n + 1) * DM] if k == 0 else ps[:, 6, n * DM:(n + 1) * DM], lhs, w_sqT[:, w, :], start=True, stop=True)
                pe.matmul(ps[:, 7, 0:D], w_sqT[:, 3, :], w_n2m[:, :], start=True, stop=True)
                pe.matmul(bank(2, RAD, DM), w_edge[:, :], w_eT[:, :], start=True, stop=True).then_inc(pe_done, 1)
                pe.wait_ge(dve_done, 16)
                for k in range(2):
                    pe.matmul(ps[:, 3 + k, 0:D + 1], w_skipn[:, k * P:(k + 1) * P], c.w_out1[:, :], start=True, stop=True)
                    pe.matmul(ps[:, 5 + k, 0:1], w_skipn[:, k * P:(k + 1) * P], wb[:, :], start=True, stop=True)
                pe.matmul(ps[:, 7, 0:D + 1], bs_cols[:, :], c.w_out1[:, :], start=True, stop=True).then_inc(pe_done, 1)
                pe.wait_ge(dve_done, 21)
                for k in range(2):
                    last = pe.matmul(ps[:, 0, 0:D + 1], mean_w[:, :], c.m_ext[:, k, :], start=(k == 0), stop=(k == 1))
                last.then_inc(pe_done, 1)

            @block.vector
            def _(dve):
                own = Own(dve, dve_done, None)
                dve.wait_ge(ldd, loads)
                dve.wait_ge(pool_done, 4)
                own(dve.tensor_tensor(wb[:, :], beta[:, 1:2], beta[:, 2:3], ALU.subtract))
                own(dve.tensor_tensor(c.wa_row[:, :], c.wa_row[:, :], c.wc_row[:, :], ALU.add))
                dve.wait_ge(pe_done, 1)
                own(dve.tensor_copy(w_sqT[:, :, :].rearrange("p k d -> p (k d)"), ps[:, 0, 0:512]))
                own(dve.tensor_copy(c.w_out1[:, 0:D], ps[:, 1, 0:D]))
                own(dve.tensor_copy(w_eT[:, :], ps[0:RAD, 2, 0:DM]))
                own.done()
                own(dve.tensor_copy(c.w_out1[:, D:D + 1], wb[:, :]))
                own(dve.tensor_scalar(bs_cols[:, 1:P], zero[:, 1:P], bs_cols[:, 0:1], None, ALU.add))
                own(dve.memset(c.ones_col[:, :], 1.0))
                own(dve.memset(xlw[:, :], 0.0))
                dve.wait_ge(pe_done, 2)
                for k in range(2):
                    own(dve.tensor_copy(c.w_qs[:, k, 0:2 * DM], ps[:, 3 + k, 0:2 * DM]))
                    own(dve.tensor_copy(c.w_kv[:, k, :], ps[:, 5 + k, 0:2 * DM]))
                own(dve.tensor_copy(w_skipn[:, :], ps[:, 7, 0:D]))
                own(dve.tensor_copy(c.we2[0:RAD, 0:DM], ps[0:RAD, 2, 0:DM]))
                own(dve.tensor_copy(c.we2[0:RAD, DM:2 * DM], ps[0:RAD, 2, 0:DM]))
                dve.wait_ge(pe_done, 3)
                for k in range(2):
                    own(dve.tensor_copy(c.m_ext[:, k, :], ps[:, 3 + k, 0:D + 1]))
                    own(dve.tensor_copy(c.w_qs[:, k, 2 * DM:2 * DM + 1], ps[:, 5 + k, 0:1]))
                own(dve.tensor_copy(c.b_ext[:, :], ps[:, 7, 0:D + 1]))
                own.done()
                own(dve.tensor_copy(c.bq_xr[:, 2 * DM:2 * DM + 1], c.b_ext[:, D:D + 1]))
                dve.wait_ge(pe_done, 4)
                for k in range(2):
                    own(dve.tensor_tensor(c.m_ext[:, k, :], c.m_ext[:, k, :], ps[:, 0, 0:D + 1], ALU.subtract))
                for half, out in ((0, c.wh[:, :, D:HP]), (1, c.w_ad[:, :, :])):
                    for k in range(2):
                        own.done()
                        own(dve.tensor_tensor(prod[:, k, :, :], c.wh[:, k, 0:D].rearrange("p (h d) -> p h d", h=H),
                                              attn[:, :, half * HD:(half + 1) * HD], ALU.mult))
                    own.done()
                    for k in range(2):
                        own(dve.tensor_reduce(out[:, k, :], prod[:, k, :, :], AX.X, ALU.add))
                own.done()


def index_pass(nc, c, io):
    c.passes += 1
    dst, src = io["dst"], io["src"]
    rows = dst.rearrange("(t e) -> t e", e=EDGES)
    with ExitStack() as ctx:
        def sb(name, shape, dt=F32):
            return ctx.enter_context(nc.sbuf_tensor(c.name(name), shape, dt))

        def sem(name):
            return ctx.enter_context(nc.semaphore(c.name(name)))

        dsti = sb("dsti", [TILES, EDGES], I32)
        srci = sb("srci", [TILES, EDGES], I32)
        previ = sb("previ", [TILES, 1], I32)
        nexti = sb("nexti", [TILES, 1], I32)
        edgei = sb("edgei", [H, 2, TILES], I32)
        edgef = sb("edgef", [H, 2, TILES])
        dstf = sb("dstf", [TILES, EDGES])
        prevf = sb("prevf", [TILES, 1])
        nextf = sb("nextf", [TILES, 1])
        row = sb("row", [TILES, 5, P])
        islast = sb("islast", [TILES, EDGES])
        posi = sb("posi", [TILES, EDGES], I32)
        posf = sb("posf", [TILES, EDGES])
        fill = sb("fill", [80, N // 80], I32)
        idx_loads = sem("idx_loads")
        own_sem = sem("own_sem")
        minus = sem("minus")
        table = sem("table")
        turned = sem("turned")
        pool_ready = sem("pool_ready")
        LD = 16 * 6
        with nc.Block() as block:
            @block.sync
            def _(sp):
                with nc.allow_non_contiguous_dma(reason="400 first and last dst of the tiles, once"):
                    sp.dma_start(dsti[:, :], rows).then_inc(idx_loads, 16)
                    sp.dma_start(srci[:, :], src.rearrange("(t e) -> t e", e=EDGES)).then_inc(idx_loads, 16)
                    sp.dma_start(edgei[:, 0, :], dst.rearrange("(a t e) -> a t e", a=1, e=EDGES)[:, :, 0].to_broadcast([H, TILES])).then_inc(idx_loads, 16)
                    sp.dma_start(edgei[:, 1, :], dst.rearrange("(a t e) -> a t e", a=1, e=EDGES)[:, :, EDGES - 1].to_broadcast([H, TILES])).then_inc(idx_loads, 16)
                    sp.wait_ge(minus, 1)
                    sp.dma_start(previ[1:TILES, :], rows[0:TILES - 1, EDGES - 1:EDGES]).then_inc(idx_loads, 16)
                    sp.dma_start(nexti[0:TILES - 1, :], rows[1:TILES, 0:1]).then_inc(idx_loads, 16)
                sp.wait_ge(pool_ready, 1)
                sp.dma_start(c.pos_table.rearrange("(p n) a -> p (n a)", p=80), fill[:, :]).then_inc(table, 16)
                sp.wait_ge(own_sem, 17)
                sp.dma_start(c.col_ids, row[:, 4, :]).then_inc(table, 16)
                sp.wait_ge(table, 32)

            @block.gpsimd
            def _(pool):
                pool.iota(posi[:, :], [[1, EDGES]], base=1, channel_multiplier=P).then_inc(pool_ready, 1)
                pool.iota(c.own_pos[:, :], [[P, TILES]], base=0, channel_multiplier=1).then_inc(pool_ready, 1)

            @block.vector
            def _(dve):
                own = Own(dve, own_sem, None)
                own(dve.memset(previ[:, :], -1))
                own(dve.memset(nexti[:, :], -1))
                own(dve.memset(row[:, 0:2, :], 0.0))
                own(dve.memset(row[:, 2, :], float(SKIP)))
                own(dve.memset(row[:, 3, :], -2.0))
                own(dve.memset(row[:, 4, :], -3.0))
                dve.memset(fill[:, :], SKIP).then_inc(minus, 1)
                dve.wait_ge(idx_loads, LD)
                dve.wait_ge(minus, 1)
                dve.wait_ge(pool_ready, 2)
                for out, into in ((dstf, dsti), (prevf, previ), (nextf, nexti), (posf, posi)):
                    own(dve.tensor_copy(out[:, :], into[:, :]))
                own(dve.tensor_copy(edgef[:, :, :], edgei[:, :, :]))
                own(dve.tensor_copy(row[:, 0, 1:1 + EDGES], srci[:, :]))
                own(dve.tensor_copy(row[:, 1, 1:1 + EDGES], dsti[:, :]))
                own.done()
                own(dve.tensor_copy(row[:, 3, 0:1], prevf[:, :]))
                own(dve.tensor_copy(row[:, 3, 1:1 + EDGES], dstf[:, :]))
                own(dve.tensor_copy(row[:, 4, 0:1], dstf[:, EDGES - 1:EDGES]))
                own(dve.tensor_copy(row[:, 4, 1:1 + EDGES], dstf[:, :]))
                own(dve.tensor_tensor(islast[:, 0:EDGES - 1], dstf[:, 0:EDGES - 1], dstf[:, 1:EDGES], ALU.not_equal))
                own(dve.tensor_tensor(islast[:, EDGES - 1:EDGES], dstf[:, EDGES - 1:EDGES], nextf[:, :], ALU.not_equal))
                own.done()
                own(dve.memset(c.cut[:, :, :, :], -BIG))
                own.done()
                for h in range(H):
                    own(dve.tensor_scalar(c.cut[:, 0, h, 1:EDGES], islast[:, 0:EDGES - 1], -BIG, None, ALU.mult))
                    own(dve.tensor_scalar(c.cut[:, 1, h, 0:EDGES - 1], islast[:, 0:EDGES - 1], -BIG, None, ALU.mult))
                for k, end in ((0, prevf), (1, nextf)):
                    own(dve.tensor_scalar(c.open_[:, k, :], dstf[:, :], end[:, :], None, ALU.is_equal))
                own.done()
                own(dve.tensor_scalar(c.open_[:, :, :], c.open_[:, :, :], -1.0, BIG, ALU.add, ALU.mult))
                own(dve.memset(c.whole[:, :, :], -BIG))
                own.done()
                own(dve.tensor_tensor(c.whole[:, 0, 1:TILES], edgef[:, 1, 0:TILES - 1], edgef[:, 1, 1:TILES], ALU.is_equal))
                own(dve.tensor_tensor(c.whole[:, 1, 0:TILES - 1], edgef[:, 0, 0:TILES - 1], edgef[:, 0, 1:TILES], ALU.is_equal))
                own.done()
                own(dve.tensor_scalar(c.whole[:, 0, 1:TILES], c.whole[:, 0, 1:TILES], -1.0, BIG, ALU.add, ALU.mult))
                own(dve.tensor_scalar(c.whole[:, 1, 0:TILES - 1], c.whole[:, 1, 0:TILES - 1], -1.0, BIG, ALU.add, ALU.mult))
                own(dve.tensor_scalar(row[:, 2, 1:1 + EDGES], dstf[:, :], -float(SKIP), None, ALU.add))
                own.done()
                own(dve.tensor_tensor(row[:, 2, 1:1 + EDGES], row[:, 2, 1:1 + EDGES], islast[:, :], ALU.mult))
                own.done()
                own(dve.tensor_scalar(row[:, 2, 1:1 + EDGES], row[:, 2, 1:1 + EDGES], float(SKIP), None, ALU.add))
                for h in range(H):
                    own(dve.tensor_copy(c.val[:, h, :], posf[:, :]))
                own.done()

            @block.tensor
            def _(pe):
                pe.wait_ge(own_sem, 43)
                for k in range(4):
                    last = pe.transpose(c.psum[:, k // 2, (k % 2) * 256:(k % 2) * 256 + TILES], row[:, k, :], c.ident[0:TILES, 0:TILES])
                last.then_inc(turned, 1)

            @block.scalar
            def _(act):
                act.wait_ge(turned, 1)
                for k, out in enumerate((c.src_col, c.dst_col, c.last_col, c.row_ids)):
                    act.activation(out[:, :], c.psum[:, k // 2, (k % 2) * 256:(k % 2) * 256 + TILES], ACT.Copy).then_inc(turned, 1)
                act.wait_ge(turned, 5)


def max_of_segments(nc, c, dve, own, asks, answers, n):
    flat = "p h e -> p (h e)"
    val, fwd, bwd = (x[:, :, :].rearrange(flat) for x in (c.val, c.fwd, c.bwd))
    own(dve.tensor_tensor_scan(fwd, c.cut[:, 0, :, :].rearrange(flat), val, -BIG, ALU.add, ALU.max))
    own(dve.tensor_tensor_scan(bwd[:, ::-1], c.cut[:, 1, :, :].rearrange(flat)[:, ::-1], val[:, ::-1], -BIG, ALU.add, ALU.max))
    own.done()
    own(dve.tensor_copy(c.ends[:, 0, :], c.fwd[:, :, EDGES - 1]))
    own(dve.tensor_copy(c.ends[:, 1, :], c.bwd[:, :, 0]))
    own.done()
    own(dve.tensor_tensor(c.top[:, :, :], c.fwd[:, :, :], c.bwd[:, :, :], ALU.max))
    own.done()
    dve.sem_inc(asks, 1)
    dve.wait_ge(answers, 2 * n + 1)
    own(dve.tensor_copy(c.run[:, 0, :], c.psum[0:H, 0, 0:TILES]))
    own(dve.tensor_copy(c.run[:, 1, :], c.psum[0:H, 0, 256:256 + TILES]))
    own.done()
    own(dve.tensor_tensor_scan(c.run2[:, 0, 1:TILES + 1], c.whole[:, 0, :], c.run[:, 0, :], -BIG, ALU.add, ALU.max))
    own(dve.tensor_tensor_scan(c.run2[:, 1, 0:TILES][:, ::-1], c.whole[:, 1, :][:, ::-1], c.run[:, 1, :][:, ::-1], -BIG, ALU.add, ALU.max))
    own(dve.memset(c.run2[:, 0, 0:1], -BIG))
    own(dve.memset(c.run2[:, 1, TILES:TILES + 1], -BIG))
    own.done()
    dve.sem_inc(asks, 1)
    dve.wait_ge(answers, 2 * n + 2)
    own(dve.tensor_copy(c.carried[:, 0, :], c.psum[0:TILES, 1, 0:H]))
    own(dve.tensor_copy(c.carried[:, 1, :], c.psum[0:TILES, 1, 256:256 + H]))
    for k in range(2):
        own.done()
        for h in range(H):
            own(dve.scalar_tensor_tensor(out=c.top[:, h, :], in0=c.open_[:, k, :], scalar=c.carried[:, k, h:h + 1],
                                         in1=c.top[:, h, :], op0=ALU.add, op1=ALU.max))
    own.done()


def turns_for_max(pe, c, asks, answers, n):
    pe.wait_ge(asks, 2 * n + 1)
    for k in range(2):
        last = pe.transpose(c.psum[0:H, 0, 256 * k:256 * k + TILES], c.ends[:, k, :], c.ident[0:TILES, 0:TILES])
    last.then_inc(answers, 1)
    pe.wait_ge(asks, 2 * n + 2)
    pe.transpose(c.psum[0:TILES, 1, 0:H], c.run2[:, 0, 0:TILES], c.ident[0:H, 0:H])
    pe.transpose(c.psum[0:TILES, 1, 256:256 + H], c.run2[:, 1, 1:TILES + 1], c.ident[0:H, 0:H]).then_inc(answers, 1)


def position_pass(nc, c):
    c.passes += 1
    with ExitStack() as ctx:
        own_sem, asks, answers, turned, ready = (ctx.enter_context(nc.semaphore(c.name(n))) for n in ("own_sem", "asks", "answers", "turned", "ready"))
        padded = ctx.enter_context(nc.sbuf_tensor(c.name("padded"), [TILES, P], F32))
        with nc.Block() as block:
            @block.vector
            def _(dve):
                own = Own(dve, own_sem, None)
                max_of_segments(nc, c, dve, own, asks, answers, 0)
                own(dve.memset(padded[:, :], 0.0))
                own.done()
                dve.tensor_copy(padded[:, 1:1 + EDGES], c.top[:, 0, :]).then_inc(ready, 1)

            @block.tensor
            def _(pe):
                turns_for_max(pe, c, asks, answers, 0)
                pe.wait_ge(ready, 1)
                pe.transpose(c.psum[:, 2, 0:TILES], padded[:, :], c.ident[0:TILES, 0:TILES]).then_inc(turned, 1)

            @block.scalar
            def _(act):
                act.wait_ge(turned, 1)
                act.activation(c.last_pos[:, :], c.psum[:, 2, 0:TILES], ACT.Copy).then_inc(ready, 1)
                act.wait_ge(ready, 2)


def weights_pass(nc, c, score_of, leaky, out):
    c.passes += 1
    with ExitStack() as ctx:
        own_sem, asks, answers, turned, ready, back = (ctx.enter_context(nc.semaphore(c.name(n))) for n in ("own_sem", "asks", "answers", "turned", "ready", "back"))
        raw = ctx.enter_context(nc.sbuf_tensor(c.name("raw"), [TILES, H, EDGES], F32))
        weights = ctx.enter_context(nc.sbuf_tensor(c.name("weights"), [TILES, H, P], F32))
        with nc.Block() as block:
            @block.tensor
            def _(pe):
                for h in range(H):
                    last = pe.transpose(c.psum[0:TILES, 3, h * P:(h + 1) * P], score_of(h), c.ident[:, :])
                last.then_inc(turned, 1)
                turns_for_max(pe, c, asks, answers, 0)
                pe.wait_ge(ready, 2)
                for h in range(H):
                    last = pe.transpose(c.psum[:, 4, h * P:h * P + TILES], weights[:, h, :], c.ident[0:TILES, 0:TILES])
                last.then_inc(back, 1)

            @block.vector
            def _(dve):
                own = Own(dve, own_sem, None)
                dve.wait_ge(turned, 1)
                scores = c.psum[0:TILES, 3, :].rearrange("p (h e) -> p h e", h=H)[:, :, 1:1 + EDGES]
                own(dve.tensor_copy(raw[:, :, :], scores))
                own(dve.memset(weights[:, :, :], 0.0))
                own.done()
                if leaky:
                    own(dve.scalar_tensor_tensor(out=c.val[:, :, :].rearrange("p h e -> p (h e)"), in0=raw[:, :, :].rearrange("p h e -> p (h e)"), scalar=0.2,
                                                 in1=raw[:, :, :].rearrange("p h e -> p (h e)"), op0=ALU.mult, op1=ALU.max))
                else:
                    own(dve.tensor_scalar(c.val[:, :, :], raw[:, :, :], 1.0 / float(CH) ** 0.5, None, ALU.mult))
                own.done()
                max_of_segments(nc, c, dve, own, asks, answers, 0)
                own(dve.tensor_tensor(raw[:, :, :], c.val[:, :, :], c.top[:, :, :], ALU.subtract))
                own.done()
                dve.tensor_scalar(raw[:, :, :], raw[:, :, :], 20.0 if leaky else BIG, None, ALU.min).then_inc(ready, 1)

            @block.scalar
            def _(act):
                act.wait_ge(ready, 1)
                act.activation(weights[:, :, 1:1 + EDGES], raw[:, :, :], ACT.Exp).then_inc(ready, 1)
                act.wait_ge(back, 1)
                act.activation(out.rearrange("p t h -> p h t"), c.psum[:, 4, :].rearrange("p (h t) -> p h t", h=H)[:, :, 0:TILES], ACT.Copy).then_inc(ready, 1)
                act.wait_ge(ready, 3)


def node_pass(nc, c, io, out):
    c.passes += 1
    x = io["x"]
    U = 4
    xv = x[0:NFULL * NROWS, :].rearrange("(s p j) d -> s p (j d)", p=P, j=NT)
    ov = out[0:NFULL * NROWS, :].rearrange("(s p j) d -> s p (j d)", p=P, j=NT)

    def rows_of(view, whole, s):
        if isinstance(s, int) and s == NFULL:
            return whole[N - NROWS:N, :].rearrange("(p j) d -> p (j d)", j=NT)
        return view[bass.ds(s, 1), :, :].rearrange("s p n -> (s p) n")

    with ExitStack() as ctx:
        def sb(name, shape, dt=F32):
            return ctx.enter_context(nc.sbuf_tensor(c.name(name), shape, dt))

        def sem(name):
            return ctx.enter_context(nc.semaphore(c.name(name)))

        X = sb("X", [P, U, NT, D])
        XB = sb("XB", [P, U, NT, D])
        TB = sb("TB", [P, 2, NT, D])
        XT = sb("XT", [P, 2, D])
        st = sb("st", [P, 2, NT, 6])
        mv = sb("mv", [P, 2, NT, 2])
        vv = sb("vv", [P, U, 2 * NT])
        r = sb("r", [P, U, 2 * NT])
        sd = sb("sd", [P, U, NT])
        lg = sb("lg", [P, U, NT])
        be = sb("be", [P, U, NT])
        bs = sb("bs", [P, U, NT])
        nm = sb("nm", [P, U, NT])
        tmp = sb("tmp", [P, 2 * NT])
        loaded = [sem(f"loaded{j}") for j in range(U)]
        stored = [sem(f"stored{j}") for j in range(U)]
        turned, xt_ready, product, logit, beta_ready, bs_ready, tb_ready, xb_ready, u_ready, normed, dve_own, turn_a, turn_d, turn_p, turn_s, act_own, bank_free, pos_done, pos_own = (
            sem(n) for n in ("turned", "xt_ready", "product", "logit", "beta_ready", "bs_ready", "tb_ready", "xb_ready", "u_ready",
                             "normed", "dve_own", "turn_a", "turn_d", "turn_p", "turn_s", "act_own", "bank_free", "pos_done", "pos_own"))
        ps = c.psum

        with nc.Block() as block:
            @block.sync
            def _(sp):
                own = Own(sp, turn_s, None)

                def emit(s, j, i):
                    if live(s, 0, NSTEPS):
                        at_least(sp, bank_free, s - U + 1)
                        sp.dma_start(X[:, j, :, :].rearrange("p j d -> p (j d)"), rows_of(xv, x, s)).then_inc(loaded[j], 16)
                steps(sp, own, 0, NSTEPS, U, 0, emit, 2)

            @block.scalar
            def _(act):
                own = Own(act, act_own, turn_a)

                def emit(s, j, i):
                    if live(s, 1, NSTEPS):
                        o = (j - 1) % U
                        at_least(act, logit, s)
                        act.activation(be[:, o, :], lg[:, o, :], ACT.Sigmoid, bias=c.b_ext[:, D:D + 1]).then_inc(beta_ready, 1)
                    for k in range(NT):
                        if live(s, 0, NSTEPS):
                            n = NT * s + k
                            at_least(act, turned, n + 1)
                            at_least(act, product, n - 1)
                            kk = (NT * j + k) % 2
                            act.activation(XT[:, kk, :], ps[:, 6 + kk, 0:D], ACT.Copy).then_inc(xt_ready, 1)
                    if live(s, 1, NSTEPS):
                        at_least(act, bs_ready, s)
                        at_least(act, xb_ready, s - 2)
                        for k in range(NT):
                            last = act.activation(TB[:, (j - 1) % 2, k, :], c.b_ext[:, 0:D], ACT.Copy, scale=bs[:, (j - 1) % U, k:k + 1])
                        last.then_inc(tb_ready, 1)
                    if live(s, 4, NSTEPS):
                        o, w = (j - 4) % U, (j - 1) % U
                        at_least(act, u_ready, s - 3)
                        for k in range(NT):
                            last = act.activation(XB[:, o, k, :], XB[:, o, k, :], ACT.Identity, bias=nm[:, w, k:k + 1], scale=r[:, w, NT + k:NT + k + 1])
                        last.then_inc(normed, 1)
                        at_least(act, normed, s - 3, turn_a)
                        if isinstance(s, int) and s - 4 == NFULL:
                            act.wait_ge(stored[(NFULL - 1) % U], 16 * ((NFULL - 1) // U + 1))
                        act.dma_start(rows_of(ov, out, s - 4), XB[:, o, :, :].rearrange("p j d -> p (j d)")).then_inc(stored[o], 16)
                steps(act, own, 0, NSTEPS, U, 4, emit, 2)
                for j in range(U):
                    act.wait_ge(stored[j], 16 * ((NSTEPS - 1 - j) // U + 1))

            @block.tensor
            def _(pe):
                own = Own(pe, turn_d, None)

                def emit(s, j, i):
                    if not live(s, 0, NSTEPS):
                        return

                    def turn(k):
                        n = NT * s + k
                        kk = (NT * j + k) % 2
                        if k == 0:
                            at_least(pe, loaded[j], arrivals(s, j, i, U, 0, rounds=2))
                        at_least(pe, xt_ready, n - 1)
                        for q in range(2):
                            last = pe.transpose(ps[:, 6 + kk, q * P:(q + 1) * P], X[:, j, k, q * P:(q + 1) * P], c.ident[:, :])
                        last.then_inc(turned, 1)
                    turn(0)
                    for k in range(NT):
                        if k + 1 < NT:
                            turn(k + 1)
                        at_least(pe, xt_ready, NT * s + k + 1)
                        if k == 0:
                            at_least(pe, bank_free, s - 1)
                        kk = (NT * j + k) % 2
                        for q in range(2):
                            last = pe.matmul(ps[:, NT * (j % 2) + k, 0:D + 1], XT[:, kk, q * P:(q + 1) * P], c.m_ext[:, q, :],
                                             start=(q == 0), stop=(q == 1))
                        last.then_inc(product, 1)
                steps(pe, own, 0, NSTEPS, U, 0, emit, 2)

            @block.vector
            def _(dve):
                own = Own(dve, dve_own, turn_d)
                BIGS = 3 * NT + 2 * NT

                def emit(s, j, i):
                    chain = []
                    if live(s, 0, NSTEPS) or live(s, 3, NSTEPS):
                        chain = roots(s, j)
                    if live(s, 1, NSTEPS):
                        o, b = (j - 1) % U, NT * ((j - 1) % 2)
                        at_least(dve, product, NT * s)
                        dve.tensor_tensor(lg[:, o, :], ps[:, b:b + NT, D], r[:, o, 0:NT], ALU.mult).then_inc(logit, 1)
                    next(chain, None) if chain else None
                    if live(s, 2, NSTEPS):
                        o, b = (j - 2) % U, NT * (j % 2)
                        at_least(dve, xb_ready, s - 1)
                        for k in range(NT):
                            ins = dve.scalar_tensor_tensor(out=XB[:, o, k, :], in0=ps[:, b + k, 0:D], scalar=be[:, o, k:k + 1],
                                                           in1=XB[:, o, k, :], op0=ALU.mult, op1=ALU.add)
                            if k < NT - 1:
                                own(ins)
                            else:
                                ins.then_inc(bank_free, 1)
                            next(chain, None) if chain else None
                    if live(s, 1, NSTEPS):
                        o = (j - 1) % U
                        at_least(dve, beta_ready, s)
                        dve.tensor_tensor(bs[:, o, :], be[:, o, :], sd[:, o, :], ALU.mult).then_inc(bs_ready, 1)
                    marks = []
                    if live(s, -1, NSTEPS):
                        x_stats((j + 1) % U, lambda: at_least(dve, loaded[(j + 1) % U], arrivals(s, j, i, U, -1, rounds=2)), chain, marks)
                    if live(s, 2, NSTEPS):
                        at_least(dve, bank_free, s - 1)
                        for k in range(NT):
                            own(dve.bn_stats(st[:, 1, k, :], XB[:, o2(j), k, :]))
                            marks.append(own.n)
                            next(chain, None) if chain else None
                    for _ in chain or ():
                        pass
                    own.upto(own.n, True)
                    for side in range(2):
                        if live(s, -1, NSTEPS) if side == 0 else live(s, 2, NSTEPS):
                            for k in range(NT):
                                own(dve.bn_aggr(mv[:, side, k, :], st[:, side, k, :]))
                    own.done()

                def o2(j):
                    return (j - 2) % U

                def x_stats(slot, arrived, chain, marks):
                    arrived()
                    for k in range(NT):
                        own(dve.bn_stats(st[:, 0, k, :], X[:, slot, k, :]))
                        marks.append(own.n)
                        next(chain, None) if chain else None

                def roots(s, j):
                    first, last = live(s, 0, NSTEPS), live(s, 3, NSTEPS)
                    lo, hi = (0 if first else NT), (2 * NT if last else NT)
                    v, y, t = vv[:, j, lo:hi], r[:, j, lo:hi], tmp[:, lo:hi]
                    if first:
                        own(dve.tensor_scalar(vv[:, j, 0:NT], mv[:, 0, :, 1], EPS, None, ALU.add))
                    if last:
                        own(dve.scalar_tensor_tensor(out=vv[:, j, NT:2 * NT], in0=vv[:, (j - 3) % U, 0:NT], scalar=EPS, in1=mv[:, 1, :, 1], op0=ALU.mult, op1=ALU.add))
                    n = own.n
                    yield
                    own.upto(n)
                    own(dve.tensor_scalar(t.bitcast(I32), v.bitcast(I32), 1, None, ALU.logical_shift_right))
                    n = own.n
                    yield
                    own.upto(n)
                    at_least(dve, normed, s - U - 2)
                    own(dve.tensor_scalar(y.bitcast(I32), t.bitcast(I32), -1.0, float(RSQRT_SEED), ALU.mult, ALU.add))
                    for _ in range(3):
                        n = own.n
                        yield
                        own.upto(n)
                        own(dve.tensor_tensor(t, y, y, ALU.mult))
                        n = own.n
                        yield
                        own.upto(n)
                        own(dve.scalar_tensor_tensor(out=t, in0=t, scalar=-0.5, in1=v, op0=ALU.mult, op1=ALU.mult))
                        n = own.n
                        yield
                        own.upto(n)
                        own(dve.scalar_tensor_tensor(out=y, in0=t, scalar=1.5, in1=y, op0=ALU.add, op1=ALU.mult))
                    n = own.n
                    yield
                    own.upto(n)
                    if last:
                        dve.scalar_tensor_tensor(out=nm[:, j, :], in0=mv[:, 1, :, 0], scalar=-1.0, in1=r[:, j, NT:2 * NT],
                                                 op0=ALU.mult, op1=ALU.mult).then_inc(u_ready, 1)
                    if first:
                        own(dve.tensor_tensor(sd[:, j, :], vv[:, j, 0:NT], r[:, j, 0:NT], ALU.mult))
                    else:
                        at_least(dve, u_ready, s - 2)

                x_stats(0, lambda: at_least(dve, loaded[0], 16), None, [])
                own.done()
                for k in range(NT):
                    own(dve.bn_aggr(mv[:, 0, k, :], st[:, 0, k, :]))
                own.done()
                steps(dve, own, U * (NT - 1 + 2 * NT + 2 * NT + 2 + 11 + 1), NSTEPS, U, 3, emit, 2)

            @block.gpsimd
            def _(pool):
                own = Own(pool, turn_p, turn_p)

                def emit(s, j, i):
                    if live(s, 1, NSTEPS):
                        o = (j - 1) % U
                        at_least(pool, tb_ready, s, turn_p)
                        at_least(pool, stored[o], arrivals(s, j, i, U, 1 + U, rounds=2), turn_p)
                        for k in range(NT):
                            last = pool.tensor_tensor(XB[:, o, k, :], X[:, o, k, :], TB[:, (j - 1) % 2, k, :], ALU.add)
                        last.then_inc(xb_ready, 1)

                steps(pool, own, 0, NSTEPS, U, 1, emit, 2)


def score_pass(nc, c, io):
    c.passes += 1
    x, U = io["x"], 2 * G
    with ExitStack() as ctx:
        def sb(name, shape, dt=F32):
            return ctx.enter_context(nc.sbuf_tensor(c.name(name), shape, dt))

        def sem(name):
            return ctx.enter_context(nc.semaphore(c.name(name)))

        XS = sb("XS", [P, 2, G, D])
        XD = sb("XD", [P, 2, G, D])
        XT = sb("XT", [P, 2, 2 * D])
        isrc = [sb(f"isrc{b}", [P, G], I32) for b in range(2)]
        idst = [sb(f"idst{b}", [P, G], I32) for b in range(2)]
        gathered = [sem(f"gathered{b}") for b in range(2)]
        turned, xt_ready, product, h_ready, copied, turn_p, turn_e, turn_a, turn_d = (
            sem(n) for n in ("turned", "xt_ready", "product", "h_ready", "copied", "turn_p", "turn_e", "turn_a", "turn_d"))
        ps = c.psum
        with nc.Block() as block:
            @block.gpsimd
            def _(pool):
                own = Own(pool, copied, turn_p)

                def emit(q, b, i):
                    at_least(pool, turned, G * (q - 1), turn_p)
                    own(pool.tensor_copy(isrc[b][:, :], c.src_col[:, bass.ds(G * q, G)]))
                    own(pool.tensor_copy(idst[b][:, :], c.dst_col[:, bass.ds(G * q, G)]))
                    own.done(True)
                    for k in range(G):
                        for out, idx in ((XS, isrc), (XD, idst)):
                            pool.indirect_dma_start(out=out[:, b, k, :], out_offset=None, in_=x,
                                                    in_offset=bass.IndirectOffsetOnAxis(ap=idx[b][:, k:k + 1], axis=0)).then_inc(gathered[b], 16)
                steps(pool, own, 4, QS, 2, 0, emit)

            @block.tensor
            def _(pe):
                own = Own(pe, turn_e, None)

                def emit(t, j, i):
                    if live(t, 0, TILES):
                        b, k = j // G, j % G
                        if k == 0:
                            at_least(pe, gathered[b], arrivals(t, j, i, U, 0, 32 * G))
                        at_least(pe, xt_ready, t - 1)
                        for side, x_ in enumerate((XS, XD)):
                            for q in range(2):
                                last = pe.transpose(ps[:, j % 2, (2 * side + q) * P:(2 * side + q + 1) * P], x_[:, b, k, q * P:(q + 1) * P], c.ident[:, :])
                        last.then_inc(turned, 1)
                    if live(t, 1, TILES):
                        o = (j - 1) % 2
                        at_least(pe, xt_ready, t)
                        at_least(pe, h_ready, t - 2)
                        for q in range(2):
                            pe.matmul(ps[:, 2 + o, 0:HP], XT[:, o, q * P:(q + 1) * P], c.wh[:, q, :], start=(q == 0), stop=(q == 1))
                        for q in range(2):
                            last = pe.matmul(ps[:, 2 + o, D:HP], XT[:, o, (2 + q) * P:(3 + q) * P], c.w_ad[:, q, :], start=False, stop=(q == 1), skip_group_check=True)
                        last.then_inc(product, 1)
                steps(pe, own, 0, TILES, U, 1, emit)

            @block.scalar
            def _(act):
                own = Own(act, turn_a, None)

                def emit(t, j, i):
                    at_least(act, turned, t + 1)
                    at_least(act, product, t - 1)
                    act.activation(XT[:, j % 2, :], ps[:, j % 2, :], ACT.Copy).then_inc(xt_ready, 1)
                steps(act, own, 0, TILES, U, 0, emit)

            @block.vector
            def _(dve):
                own = Own(dve, turn_d, None)

                def emit(t, j, i):
                    at_least(dve, product, t + 1, turn_d)
                    dve.tensor_copy(c.store[:, bass.ds(t, 1), 0:HP].rearrange("p a d -> p (a d)"), ps[:, 2 + j % 2, 0:HP]).then_inc(h_ready, 1)
                steps(dve, own, 0, TILES, U, 0, emit)
                dve.wait_ge(h_ready, TILES)


def gather_pass(nc, c, io):
    c.passes += 1
    x, U = io["x"], 2 * G
    with ExitStack() as ctx:
        def sb(name, shape, dt=F32):
            return ctx.enter_context(nc.sbuf_tensor(c.name(name), shape, dt))

        def sem(name):
            return ctx.enter_context(nc.semaphore(c.name(name)))

        XD = sb("XD", [P, 2, G, D])
        MB = sb("MB", [P, 2, G, P])
        S = sb("S", [P, G, P])
        MSG = sb("MSG", [P, G, HP])
        AG = sb("AG", [P, 2, D])
        AT = sb("AT", [P, 2, D])
        rec = sb("rec", [P, 2, H])
        idst = [sb(f"idst{b}", [P, G], I32) for b in range(2)]
        gathered = [sem(f"gathered{b}") for b in range(2)]
        ids = [sem(f"ids{b}") for b in range(2)]
        stored = [sem(f"stored{b}") for b in range(2)]
        made, summed, carried, scaled, turned, at_ready, product, z_ready, copied, dve_own, turn_p, turn_e, turn_a, turn_d, turn_s = (
            sem(n) for n in ("made", "summed", "carried", "scaled", "turned", "at_ready", "product", "z_ready", "copied", "dve_own",
                             "turn_p", "turn_e", "turn_a", "turn_d", "turn_s"))
        ps = c.psum
        ids_v = c.col_ids.rearrange("(q k) m -> q (k m)", k=G)
        rows_v = c.rows0.rearrange("(q k p) d -> q p k d", k=G, p=P)
        with nc.Block() as block:
            @block.gpsimd
            def _(pool):
                own = Own(pool, copied, turn_p)

                def emit(q, b, i):
                    at_least(pool, stored[b], arrivals(q, b, i, 2, 2), turn_p)
                    own(pool.tensor_copy(idst[b][:, :], c.dst_col[:, bass.ds(G * q, G)]))
                    own.done(True)
                    for k in range(G):
                        pool.indirect_dma_start(out=XD[:, b, k, :], out_offset=None, in_=x,
                                                in_offset=bass.IndirectOffsetOnAxis(ap=idst[b][:, k:k + 1], axis=0)).then_inc(gathered[b], 16)
                steps(pool, own, 2, QS, 2, 0, emit)

            @block.sync
            def _(sp):
                own = Own(sp, turn_s, None)

                def emit(q, b, i):
                    if live(q, 0, QS):
                        at_least(sp, made, G * (q - 1), turn_s)
                        sp.dma_start(MB[:, b, :, :].rearrange("p k m -> p (k m)"), ids_v[bass.ds(q, 1), :].to_broadcast([P, G * P])).then_inc(ids[b], 16)
                    if live(q, 1, QS):
                        at_least(sp, z_ready, G * q, turn_s)
                        sp.dma_start(rows_v[bass.ds(q - 1, 1), :, :, :].rearrange("q p k d -> (q p) k d"), XD[:, (b - 1) % 2, :, :]).then_inc(stored[(b - 1) % 2], 16)
                steps(sp, own, 0, QS, 2, 1, emit)
                for b in range(2):
                    sp.wait_ge(stored[b], 16 * (QS // 2))

            @block.tensor
            def _(pe):
                own = Own(pe, turn_e, None)

                def emit(t, j, i):
                    if live(t, 0, TILES):
                        at_least(pe, made, t + 1)
                        at_least(pe, carried, t + 1)
                        at_least(pe, scaled, t - 1)
                        pe.matmul(ps[:, j % 2, 0:HP], S[:, j % G, :], MSG[:, j % G, :], start=True, stop=True).then_inc(summed, 1)
                    if live(t, 1, TILES):
                        o = (j - 1) % 2
                        at_least(pe, scaled, t)
                        at_least(pe, at_ready, t - 2)
                        for q in range(2):
                            last = pe.transpose(ps[:, 2 + o, q * P:(q + 1) * P], AG[:, o, q * P:(q + 1) * P], c.ident[:, :])
                        last.then_inc(turned, 1)
                    if live(t, 2, TILES):
                        o = j % 2
                        at_least(pe, at_ready, t - 1)
                        at_least(pe, z_ready, t - 3)
                        for q in range(2):
                            last = pe.matmul(ps[:, 4 + o, 0:D], AT[:, o, q * P:(q + 1) * P], c.wo[:, q, :], start=(q == 0), stop=(q == 1))
                        last.then_inc(product, 1)
                steps(pe, own, 0, TILES, U, 2, emit)

            @block.scalar
            def _(act):
                own = Own(act, turn_a, None)

                def emit(t, j, i):
                    if live(t, 0, TILES - 1):
                        at_least(act, made, t + 2)
                        at_least(act, summed, t + 1)
                        act.activation(MSG[0:1, (j + 1) % G, :], ps[0:1, j % 2, 0:HP], ACT.Copy).then_inc(carried, 1)
                    if live(t, 1, TILES):
                        o = (j - 1) % 2
                        at_least(act, turned, t)
                        at_least(act, product, t - 2)
                        act.activation(AT[:, o, :], ps[:, 2 + o, 0:D], ACT.Copy).then_inc(at_ready, 1)
                steps(act, own, 0, TILES, U, 1, emit, ahead=1)

            @block.vector
            def _(dve):
                own = Own(dve, dve_own, turn_d)

                def make(t, j, i):
                    k = j % G
                    if k == 0:
                        at_least(dve, ids[j // G], arrivals(t, j, i, U, 0))
                    at_least(dve, summed, t - G + 1, turn_d)
                    own(dve.tensor_scalar(S[:, k, :], MB[:, j // G, k, :], c.row_ids[:, bass.ds(t, 1)], None, ALU.is_equal))
                    w = c.weights[:, bass.ds(t, 1), :].rearrange("p a h -> p (a h)")
                    own(dve.tensor_tensor(MSG[:, k, 0:D].rearrange("p (h d) -> p h d", h=H),
                                          c.store[:, bass.ds(t, 1), 0:D].rearrange("p a (h d) -> p (a h) d", h=H),
                                          w.unsqueeze(2).to_broadcast([P, H, HD]), ALU.mult))
                    dve.tensor_copy(MSG[:, k, D:HP], w).then_inc(made, 1)

                def emit(t, j, i):
                    if isinstance(t, int) and t == 0:
                        make(0, 0, None)
                        dve.wait_ge(made, 1)
                        dve.memset(MSG[0:1, 0, :], 0.0).then_inc(carried, 1)
                    if live(t, -1, TILES):
                        make(t + 1, (j + 1) % U, i if j + 1 < U or i is None else i + 1)
                    if live(t, 0, TILES):
                        o = j % 2
                        if isinstance(t, int) and t == TILES - 1:
                            dve.wait_ge(summed, TILES)
                        else:
                            at_least(dve, carried, t + 2)
                        at_least(dve, turned, t - 1)
                        own(dve.tensor_scalar(rec[:, o, :], ps[:, o, D:HP], 1e-8, None, ALU.add))
                        own.done()
                        own(dve.reciprocal(rec[:, o, :], rec[:, o, :]))
                        own.done()
                        dve.tensor_tensor(AG[:, o, :].rearrange("p (h d) -> p h d", h=H), ps[:, o, 0:D].rearrange("p (h d) -> p h d", h=H),
                                          rec[:, o, :].unsqueeze(2).to_broadcast([P, H, HD]), ALU.mult).then_inc(scaled, 1)
                    if live(t, 3, TILES):
                        b, k = ((j - 3) % U) // G, (j - 3) % G
                        if k == 0:
                            at_least(dve, gathered[b], arrivals(t, j, i, U, 3, 16 * G))
                        at_least(dve, product, t - 2)
                        dve.tensor_tensor(XD[:, b, k, :], ps[:, 4 + (j - 3) % 2, 0:D], XD[:, b, k, :], ALU.add).then_inc(z_ready, 1)
                steps(dve, own, U * 4, TILES, U, 3, emit, ahead=1)


def source_pass(nc, c):
    c.passes += 1
    B = 2 * G
    with ExitStack() as ctx:
        def sem(name):
            return ctx.enter_context(nc.semaphore(c.name(name)))

        idx = [ctx.enter_context(nc.sbuf_tensor(c.name(f"idx{b}"), [P, B], I32)) for b in range(2)]
        val = [ctx.enter_context(nc.sbuf_tensor(c.name(f"val{b}"), [P, B], I32)) for b in range(2)]
        moved = [sem(f"moved{b}") for b in range(2)]
        found = [sem(f"found{b}") for b in range(2)]
        copied, turn_p = sem("copied"), sem("turn_p")
        with nc.Block() as block:
            @block.gpsimd
            def _(pool):
                own = Own(pool, copied, turn_p)
                for q in range(TILES // B):
                    b = q % 2
                    at_least(pool, moved[b], 16 * B * (q // 2))
                    own(pool.tensor_copy(idx[b][:, :], c.last_col[:, q * B:(q + 1) * B]))
                    own(pool.tensor_copy(val[b][:, :], c.own_pos[:, q * B:(q + 1) * B]))
                    own.done()
                    for k in range(B):
                        pool.indirect_dma_start(out=c.pos_table, out_offset=bass.IndirectOffsetOnAxis(ap=idx[b][:, k:k + 1], axis=0),
                                                in_=val[b][:, k:k + 1], in_offset=None, bounds_check=N - 1, oob_is_err=False).then_inc(moved[b], 16)
                for b in range(2):
                    pool.wait_ge(moved[b], 16 * TILES // 2)
                for q in range(TILES // B + 1):
                    b = q % 2
                    if q < TILES // B:
                        own(pool.tensor_copy(idx[b][:, :], c.src_col[:, q * B:(q + 1) * B]))
                        own.done()
                        for k in range(B):
                            pool.indirect_dma_start(out=val[b][:, k:k + 1], out_offset=None, in_=c.pos_table,
                                                    in_offset=bass.IndirectOffsetOnAxis(ap=idx[b][:, k:k + 1], axis=0)).then_inc(found[b], 16)
                    if q > 0:
                        pool.wait_ge(found[1 - b], 16 * B * ((q - 1) // 2 + 1))
                        own(pool.tensor_copy(c.src_pos[:, (q - 1) * B:q * B], val[1 - b][:, :]))
                own.done()


def message_pass(nc, c, io):
    c.passes += 1
    x, R = io["x"], 4
    U = R * G
    with ExitStack() as ctx:
        def sb(name, shape, dt=F32):
            return ctx.enter_context(nc.sbuf_tensor(c.name(name), shape, dt))

        def sem(name):
            return ctx.enter_context(nc.semaphore(c.name(name)))

        Z = sb("Z", [P, R, G, 2, D])
        AT = sb("AT", [P, R, G, RAD + 1])
        XT = sb("XT", [P, 2, 2 * D])
        ET = sb("ET", [RAD + 1, 2, P])
        st = sb("st", [P, G * 2, 6])
        mv = sb("mv", [P, G * 2, 2])
        vv = sb("vv", [P, G * 2])
        r = sb("r", [P, 2, G * 2])
        nm = sb("nm", [P, 2, G * 2])
        tmp = sb("tmp", [P, G * 2])
        QK = sb("QK", [P, 2, DM])
        sc = sb("sc", [P, 2, H])
        icol = [[sb(f"icol{b}{n}", [P, G], I32) for n in range(3)] for b in range(R)]
        gathered = [sem(f"gathered{b}") for b in range(R)]
        overlaid = [sem(f"overlaid{b}") for b in range(R)]
        attrs = [sem(f"attrs{b}") for b in range(R)]
        padded, roots, normed, turned, xt_ready, product, scored, v_ready, copied, dve_own, turn_e, turn_a, turn_d, turn_s, turn_p = (
            sem(n) for n in ("padded", "roots", "normed", "turned", "xt_ready", "product", "scored", "v_ready", "copied", "dve_own",
                             "turn_e", "turn_a", "turn_d", "turn_s", "turn_p"))
        ps = c.psum
        attr_v = io["edge_attr_64"].rearrange("(q k e) a -> q e k a", k=G, e=EDGES)
        with nc.Block() as block:
            @block.gpsimd
            def _(pool):
                own = Own(pool, copied, turn_p)

                def emit(q, b, i):
                    if live(q, 0, QS):
                        at_least(pool, turned, G * (q - R + 1), turn_p)
                        for n, col in enumerate((c.src_col, c.last_pos, c.src_pos)):
                            own(pool.tensor_copy(icol[b][n][:, :], col[:, bass.ds(G * q, G)]))
                        own.done(True)
                        for k in range(G):
                            pool.indirect_dma_start(out=Z[:, b, k, 0, :], out_offset=None, in_=x,
                                                    in_offset=bass.IndirectOffsetOnAxis(ap=icol[b][0][:, k:k + 1], axis=0)).then_inc(gathered[b], 16)
                            pool.indirect_dma_start(out=Z[:, b, k, 1, :], out_offset=None, in_=c.rows0,
                                                    in_offset=bass.IndirectOffsetOnAxis(ap=icol[b][1][:, k:k + 1], axis=0)).then_inc(gathered[b], 16)
                    if live(q, 1, QS):
                        o = (b - 1) % R
                        at_least(pool, gathered[o], arrivals(q, b, i, R, 1, 32 * G), turn_p)
                        for k in range(G):
                            pool.indirect_dma_start(out=Z[:, o, k, 0, :], out_offset=None, in_=c.rows0,
                                                    in_offset=bass.IndirectOffsetOnAxis(ap=icol[o][2][:, k:k + 1], axis=0),
                                                    bounds_check=ROWS - 1, oob_is_err=False).then_inc(overlaid[o], 16)
                steps(pool, own, 3 * R, QS, R, 1, emit)

            @block.sync
            def _(sp):
                own = Own(sp, turn_s, None)

                def emit(q, b, i):
                    at_least(sp, turned, G * (q - R + 1), turn_s)
                    if isinstance(q, int) and q == 0:
                        sp.wait_ge(padded, 2)
                    sp.dma_start(AT[1:1 + EDGES, b, :, 0:RAD], attr_v[bass.ds(q, 1), :, :, :].rearrange("q e k a -> (q e) k a")).then_inc(attrs[b], 16)
                steps(sp, own, 0, QS, R, 0, emit)

            @block.tensor
            def _(pe):
                own = Own(pe, turn_e, None)

                def emit(t, j, i):
                    if live(t, 0, TILES):
                        b, k, o = j // G, j % G, j % 2
                        if k == 0:
                            at_least(pe, attrs[b], arrivals(t, j, i, U, 0))
                        at_least(pe, normed, t + 1)
                        at_least(pe, xt_ready, t - 1)
                        for side in range(2):
                            for q in range(2):
                                pe.transpose(ps[:, o, (2 * side + q) * P:(2 * side + q + 1) * P], Z[:, b, k, side, q * P:(q + 1) * P], c.ident[:, :])
                        pe.transpose(ps[0:RAD + 1, 2 + o, 0:P], AT[:, b, k, :], c.ident[:, :]).then_inc(turned, 1)
                    if live(t, 1, TILES):
                        o = (j - 1) % 2
                        at_least(pe, xt_ready, t)
                        at_least(pe, scored, t - 2)
                        at_least(pe, v_ready, t - 2)
                        for q in range(2):
                            pe.matmul(ps[:, 4 + o, 0:2 * DM], XT[:, o, q * P:(q + 1) * P], c.w_kv[:, q, :], start=(q == 0), stop=False)
                        pe.matmul(ps[:, 4 + o, 0:2 * DM], ET[:, o, :], c.we2[:, :], start=False, stop=True)
                        for q in range(2):
                            last = pe.matmul(ps[:, 6 + o, 0:2 * DM + 1], XT[:, o, (2 + q) * P:(3 + q) * P], c.w_qs[:, q, :], start=(q == 0), stop=(q == 1))
                        last.then_inc(product, 1)
                steps(pe, own, 0, TILES, U, 1, emit)

            @block.scalar
            def _(act):
                own = Own(act, turn_a, turn_a)

                def emit(t, j, i):
                    if live(t, 0, TILES) and j % G == 0:
                        b = j // G
                        at_least(act, roots, (t // G if isinstance(t, int) else R * i + R + b) + 1)
                        for k in range(G):
                            for side in range(2):
                                n = 2 * k + side
                                last = act.activation(Z[:, b, k, side, :], Z[:, b, k, side, :], ACT.Identity, bias=nm[:, b % 2, n:n + 1], scale=r[:, b % 2, n:n + 1])
                            last.then_inc(normed, 1)
                    if live(t, 1, TILES):
                        o = (j - 1) % 2
                        at_least(act, turned, t)
                        at_least(act, product, t - 2)
                        act.activation(ET[:, o, :], ps[0:RAD + 1, 2 + o, 0:P], ACT.Copy)
                        act.activation(XT[:, o, :], ps[:, o, :], ACT.Copy).then_inc(xt_ready, 1)
                    if live(t, 4, TILES):
                        at_least(act, scored, t - 3, turn_a)
                        act.activation(c.store[:, bass.ds(t - 4, 1), 0:DM].rearrange("p a d -> p (a d)"), ps[:, 4 + j % 2, DM:2 * DM], ACT.Copy).then_inc(v_ready, 1)
                steps(act, own, 0, TILES, U, 4, emit)
                act.wait_ge(v_ready, TILES)

            @block.vector
            def _(dve):
                own = Own(dve, dve_own, turn_d)
                own(dve.memset(AT[:, :, :, :], 0.0))
                own.done()
                dve.memset(AT[:, :, :, RAD:RAD + 1], 1.0).then_inc(padded, 2)

                def statistics(b, arrived, overlay, free):
                    at_least(dve, gathered[b], arrived)
                    at_least(dve, overlaid[b], overlay)
                    for k in range(G):
                        for side in range(2):
                            own(dve.bn_stats(st[:, 2 * k + side, :], Z[:, b, k, side, :]))
                    own.done(True)
                    for n in range(2 * G):
                        own(dve.bn_aggr(mv[:, n, :], st[:, n, :]))
                    own.done()
                    own(dve.tensor_scalar(vv[:, :], mv[:, :, 1], EPS, None, ALU.add))
                    own.done()
                    at_least(dve, normed, free)
                    rsqrt(own, r[:, b % 2, :], vv[:, :], tmp[:, :])
                    dve.scalar_tensor_tensor(out=nm[:, b % 2, :], in0=mv[:, :, 0], scalar=-1.0, in1=r[:, b % 2, :], op0=ALU.mult, op1=ALU.mult).then_inc(roots, 1)

                def emit(t, j, i):
                    if live(t, -G, TILES) and j % G == 0:
                        b = ((j + G) % U) // G
                        at_least(dve, roots, t // G + 1 if isinstance(t, int) else R * i + R + j // G + 1, turn_d)
                        statistics(b, arrivals(t, j, i, U, -G, 32 * G), arrivals(t, j, i, U, -G, 16 * G), t - G)
                    if live(t, 2, TILES):
                        n, o = t - 2, j % 2
                        at_least(dve, product, t - 1)
                        own(dve.tensor_tensor(c.store[:, bass.ds(n, 1), 0:2 * DM + 1].rearrange("p a d -> p (a d)"),
                                              ps[:, 6 + o, 0:2 * DM + 1], c.bq_xr[:, :], ALU.add))
                        own.done()
                        own(dve.tensor_tensor(QK[:, o, :], c.store[:, bass.ds(n, 1), 0:DM].rearrange("p a d -> p (a d)"), ps[:, 4 + o, 0:DM], ALU.mult))
                        own.done(True)
                        dve.tensor_reduce(c.scores[:, bass.ds(n, 1), :].rearrange("p a h -> p (a h)"), QK[:, o, :].rearrange("p (h d) -> p h d", h=H), AX.X, ALU.add).then_inc(scored, 1)
                statistics(0, 32 * G, 16 * G, 0)
                steps(dve, own, U * 2 + R * (4 * G + 1 + 11), TILES, U, 2, emit, ahead=G)
                dve.wait_ge(scored, TILES)


def out_pass(nc, c, out):
    c.passes += 1
    R = 4
    U = R * G
    with ExitStack() as ctx:
        def sb(name, shape, dt=F32):
            return ctx.enter_context(nc.sbuf_tensor(c.name(name), shape, dt))

        def sem(name):
            return ctx.enter_context(nc.semaphore(c.name(name)))

        Z = sb("Z", [P, R, G, D])
        MB = sb("MB", [P, R, G, P])
        S = sb("S", [P, G, P])
        MSG = sb("MSG", [P, G, VP])
        O = sb("O", [P, 2, DM])
        DF = sb("DF", [P, 2, DM])
        OW = sb("OW", [P, 2, DM])
        MX = sb("MX", [P, 2, DM])
        MT = sb("MT", [P, 2, DM])
        rec = sb("rec", [P, 2, H])
        lg = sb("lg", [P, 2, 1])
        be = sb("be", [P, 2, 1])
        st = sb("st", [P, G, 6])
        mv = sb("mv", [P, G, 2])
        vv = sb("vv", [P, G])
        r = sb("r", [P, 2, 2, G])
        nm = sb("nm", [P, 2, 2, G])
        tmp = sb("tmp", [P, G])
        icol = [sb(f"icol{b}", [P, G], I32) for b in range(R)]
        rows = [sem(f"rows{b}") for b in range(R)]
        ids = [sem(f"ids{b}") for b in range(R)]
        scattered = [sem(f"scattered{b}") for b in range(R)]
        roots, x1_ready, made, summed, carried, logit, beta_ready, mixed, turned, mt_ready, product, z_ready, z_roots, normed, copied, dve_own, turn_p, turn_e, turn_a, turn_d, turn_s = (
            sem(n) for n in ("roots", "x1_ready", "made", "summed", "carried", "logit", "beta_ready", "mixed", "turned", "mt_ready",
                             "product", "z_ready", "z_roots", "normed", "copied", "dve_own", "turn_p", "turn_e", "turn_a", "turn_d", "turn_s"))
        ps = c.psum
        ids_v = c.col_ids.rearrange("(q k) m -> q (k m)", k=G)
        rows_v = c.rows0.rearrange("(q k p) d -> q p k d", k=G, p=P)

        def step_of(t, j, i):
            return t // G if isinstance(t, int) else R * i + R + j // G

        with nc.Block() as block:
            @block.sync
            def _(sp):
                own = Own(sp, turn_s, None)

                def emit(q, b, i):
                    at_least(sp, scattered[b], arrivals(q, b, i, R, R, 16 * G), turn_s)
                    at_least(sp, made, G * (q - R + 1), turn_s)
                    sp.dma_start(Z[:, b, :, :], rows_v[bass.ds(q, 1), :, :, :].rearrange("q p k d -> (q p) k d")).then_inc(rows[b], 16)
                    sp.dma_start(MB[:, b, :, :].rearrange("p k m -> p (k m)"), ids_v[bass.ds(q, 1), :].to_broadcast([P, G * P])).then_inc(ids[b], 16)
                steps(sp, own, 0, QS, R, 0, emit)

            @block.gpsimd
            def _(pool):
                own = Own(pool, copied, turn_p)

                def emit(q, b, i):
                    at_least(pool, scattered[b], arrivals(q, b, i, R, R, 16 * G), turn_p)
                    own(pool.tensor_copy(icol[b][:, :], c.last_col[:, bass.ds(G * q, G)]))
                    own.done(True)
                    at_least(pool, normed, q + 1, turn_p)
                    for k in range(G):
                        pool.indirect_dma_start(out=out, out_offset=bass.IndirectOffsetOnAxis(ap=icol[b][:, k:k + 1], axis=0),
                                                in_=Z[:, b, k, :], in_offset=None, bounds_check=N - 1, oob_is_err=False).then_inc(scattered[b], 16)
                steps(pool, own, R, QS, R, 0, emit)
                for b in range(R):
                    pool.wait_ge(scattered[b], 16 * G * QS // R)

            @block.tensor
            def _(pe):
                own = Own(pe, turn_e, None)

                def emit(t, j, i):
                    if live(t, 0, TILES):
                        at_least(pe, made, t + 1)
                        at_least(pe, carried, t + 1)
                        at_least(pe, logit, t - 1)
                        pe.matmul(ps[:, j % 2, 0:VP], S[:, j % G, :], MSG[:, j % G, :], start=True, stop=True).then_inc(summed, 1)
                    if live(t, 2, TILES):
                        at_least(pe, mixed, t - 1)
                        at_least(pe, mt_ready, t - 3)
                        pe.transpose(ps[:, 2 + j % 2, 0:DM], MX[:, j % 2, :], c.ident[:, :]).then_inc(turned, 1)
                    if live(t, 3, TILES):
                        o = (j - 3) % 2
                        at_least(pe, mt_ready, t - 2)
                        at_least(pe, z_ready, t - 4)
                        pe.matmul(ps[:, 4 + o, 0:D], MT[:, o, :], c.w_out1[:, 0:D], start=True, stop=True).then_inc(product, 1)
                steps(pe, own, 0, TILES, U, 3, emit)

            @block.scalar
            def _(act):
                own = Own(act, turn_a, turn_a)

                def normalise(b, side, done, ready, count):
                    at_least(act, ready, count)
                    for k in range(G):
                        last = act.activation(Z[:, b, k, :], Z[:, b, k, :], ACT.Identity, bias=nm[:, side, b % 2, k:k + 1], scale=r[:, side, b % 2, k:k + 1])
                    last.then_inc(done, 1)

                def emit(t, j, i):
                    k = j % G
                    if k == 2 and live(t, 2 - G, TILES):
                        normalise(((j + G - 2) % U) // G, 0, x1_ready, roots, step_of(t, j, i) + 2)
                    if live(t, 0, TILES - 1):
                        at_least(act, made, t + 2)
                        at_least(act, summed, t + 1)
                        act.activation(MSG[0:1, (j + 1) % G, :], ps[0:1, j % 2, 0:VP], ACT.Copy).then_inc(carried, 1)
                    if live(t, 0, TILES):
                        at_least(act, logit, t + 1)
                        at_least(act, mixed, t - 1)
                        act.activation(be[:, j % 2, :], lg[:, j % 2, :], ACT.Sigmoid).then_inc(beta_ready, 1)
                    if live(t, 2, TILES):
                        at_least(act, turned, t - 1)
                        at_least(act, product, t - 3)
                        act.activation(MT[:, j % 2, :], ps[:, 2 + j % 2, 0:DM], ACT.Copy).then_inc(mt_ready, 1)
                    if k == 4 and live(t, 4 + G, TILES):
                        normalise(((j - G) % U) // G, 1, normed, z_roots, step_of(t, j, i))
                normalise(0, 0, x1_ready, roots, 1)
                steps(act, own, 0, TILES, U, 9 + 1, emit, ahead=G)

            @block.vector
            def _(dve):
                own = Own(dve, dve_own, turn_d)

                def statistics(b, side, ready, used):
                    for k in range(G):
                        own(dve.bn_stats(st[:, k, :], Z[:, b, k, :]))
                    own.done(True)
                    for n in range(G):
                        own(dve.bn_aggr(mv[:, n, :], st[:, n, :]))
                    own.done()
                    own(dve.tensor_scalar(vv[:, :], mv[:, :, 1], EPS, None, ALU.add))
                    own.done()
                    at_least(dve, *used)
                    rsqrt(own, r[:, side, b % 2, :], vv[:, :], tmp[:, :])
                    dve.scalar_tensor_tensor(out=nm[:, side, b % 2, :], in0=mv[:, :, 0], scalar=-1.0, in1=r[:, side, b % 2, :], op0=ALU.mult, op1=ALU.mult).then_inc(ready, 1)

                def make(t, j, i):
                    k = j % G
                    if k == 0:
                        at_least(dve, ids[j // G], arrivals(t, j, i, U, 0))
                    at_least(dve, summed, t - G + 1, turn_d)
                    own(dve.tensor_scalar(S[:, k, :], MB[:, j // G, k, :], c.row_ids[:, bass.ds(t, 1)], None, ALU.is_equal))
                    w = c.weights[:, bass.ds(t, 1), :].rearrange("p a h -> p (a h)")
                    own(dve.tensor_tensor(MSG[:, k, 0:DM].rearrange("p (h d) -> p h d", h=H),
                                          c.store[:, bass.ds(t, 1), 0:DM].rearrange("p a (h d) -> p (a h) d", h=H),
                                          w.unsqueeze(2).to_broadcast([P, H, CH]), ALU.mult))
                    dve.tensor_copy(MSG[:, k, DM:VP], w).then_inc(made, 1)

                def emit(t, j, i):
                    k, o = j % G, j % 2
                    if k == 0 and live(t, -G, TILES):
                        b = ((j + G) % U) // G
                        at_least(dve, rows[b], arrivals(t, j, i, U, -G))
                        q = step_of(t, j, i)
                        at_least(dve, roots, q + 1)
                        statistics(b, 0, roots, (x1_ready, q))
                    if live(t, -1, TILES):
                        make(t + 1, (j + 1) % U, i if j + 1 < U or i is None else i + 1)
                    if live(t, 0, TILES):
                        if isinstance(t, int) and t == TILES - 1:
                            dve.wait_ge(summed, TILES)
                        else:
                            at_least(dve, carried, t + 2)
                        own(dve.tensor_scalar(rec[:, o, :], ps[:, o, DM:VP], 1e-16, None, ALU.add))
                        own.done()
                        own(dve.reciprocal(rec[:, o, :], rec[:, o, :]))
                        own.done()
                        own(dve.tensor_tensor(O[:, o, :].rearrange("p (h d) -> p h d", h=H), ps[:, o, 0:DM].rearrange("p (h d) -> p h d", h=H),
                                              rec[:, o, :].unsqueeze(2).to_broadcast([P, H, CH]), ALU.mult))
                        own.done()
                        own(dve.tensor_tensor(DF[:, o, :], c.store[:, bass.ds(t, 1), DM:2 * DM].rearrange("p a d -> p (a d)"), O[:, o, :], ALU.subtract))
                        own(dve.tensor_tensor(OW[:, o, :], O[:, o, :], c.wa_row[:, :], ALU.mult))
                        own.done()
                        at_least(dve, beta_ready, t - 1)
                        own(dve.tensor_reduce(lg[:, o, :], OW[:, o, :], AX.X, ALU.add))
                        own.done()
                        dve.tensor_tensor(lg[:, o, :], lg[:, o, :], c.store[:, bass.ds(t, 1), 2 * DM:XL + DM].rearrange("p a d -> p (a d)"), ALU.add).then_inc(logit, 1)
                    if live(t, 1, TILES):
                        o = (j - 1) % 2
                        at_least(dve, beta_ready, t)
                        at_least(dve, turned, t - 2)
                        dve.scalar_tensor_tensor(out=MX[:, o, :], in0=DF[:, o, :], scalar=be[:, o, :], in1=O[:, o, :], op0=ALU.mult, op1=ALU.add).then_inc(mixed, 1)
                    if live(t, 4, TILES):
                        b, n = ((j - 4) % U) // G, (j - 4) % G
                        if n == 0:
                            at_least(dve, x1_ready, step_of(t, j, i) + 1 if j % G == 4 else None)
                        at_least(dve, product, t - 3)
                        dve.tensor_tensor(Z[:, b, n, :], ps[:, 4 + j % 2, 0:D], Z[:, b, n, :], ALU.add).then_inc(z_ready, 1)
                        if n == G - 1:
                            at_least(dve, z_ready, t - 3)
                            q = step_of(t, j, i)
                            if not (isinstance(q, int) and q == 1):
                                at_least(dve, z_roots, q - 1)
                            statistics(b, 1, z_roots, (normed, q - 2))
                dve.wait_ge(rows[0], 16)
                statistics(0, 0, roots, (x1_ready, 0))
                make(0, 0, None)
                dve.wait_ge(made, 1)
                dve.memset(MSG[0:1, 0, :], 0.0).then_inc(carried, 1)
                steps(dve, own, U * (2 + 3 + 2 + 1) + R * 2 * (2 * G + 1 + 11), TILES, U, 4, emit, ahead=G)


def build(nc, io, out):
    with ExitStack() as ctx:
        c = Core()

        def sb(name, shape, dt=F32):
            return ctx.enter_context(nc.sbuf_tensor(name, shape, dt))

        c.psum = ctx.enter_context(nc.psum_tensor("banks", [P, 8, 512], F32))
        c.ident = sb("ident", [P, P])
        c.ones_col = sb("ones_col", [P, 1])
        c.wh = sb("wh", [P, 2, HP])
        c.w_ad = sb("w_ad", [P, 2, H])
        c.wo = sb("wo", [P, 2, D])
        c.w_kv = sb("w_kv", [P, 2, 2 * DM])
        c.w_qs = sb("w_qs", [P, 2, 2 * DM + 1])
        c.bq_xr = sb("bq_xr", [P, 2 * DM + 1])
        c.we2 = sb("we2", [RAD + 1, 2 * DM])
        c.wa_row = sb("wa_row", [P, DM])
        c.wc_row = sb("wc_row", [P, DM])
        c.w_out1 = sb("w_out1", [P, D + 1])
        c.m_ext = sb("m_ext", [P, 2, D + 1])
        c.b_ext = sb("b_ext", [P, D + 1])
        c.src_col = sb("src_col", [P, TILES], I32)
        c.dst_col = sb("dst_col", [P, TILES], I32)
        c.last_col = sb("last_col", [P, TILES], I32)
        c.own_pos = sb("own_pos", [P, TILES], I32)
        c.last_pos = sb("last_pos", [P, TILES], I32)
        c.src_pos = sb("src_pos", [P, TILES], I32)
        c.row_ids = sb("row_ids", [P, TILES])
        c.cut = sb("cut", [TILES, 2, H, EDGES])
        c.open_ = sb("open_", [TILES, 2, EDGES])
        c.whole = sb("whole", [H, 2, TILES])
        c.val = sb("val", [TILES, H, EDGES])
        c.fwd = sb("fwd", [TILES, H, EDGES])
        c.bwd = sb("bwd", [TILES, H, EDGES])
        c.top = sb("top", [TILES, H, EDGES])
        c.ends = sb("ends", [TILES, 2, H])
        c.run = sb("run", [H, 2, TILES])
        c.run2 = sb("run2", [H, 2, TILES + 1])
        c.carried = sb("carried", [TILES, 2, H])
        c.pos_table = nc.dram_tensor("pos_table", (N, 1), I32, kind="Internal").ap()
        c.col_ids = nc.dram_tensor("col_ids", (TILES, P), F32, kind="Internal").ap()
        c.rows0 = nc.dram_tensor("rows0", (ROWS, D), F32, kind="Internal").ap()

        c.weights = sb("weights", [P, TILES, H])
        c.scores = sb("scores", [P, TILES, H])
        setup(nc, c, io)
        index_pass(nc, c, io)
        position_pass(nc, c)
        source_pass(nc, c)
        node_pass(nc, c, io, out)
        c.store = sb("store", [P, TILES, HP])
        score_pass(nc, c, io)
        weights_pass(nc, c, lambda h: c.store[:, :, D + h], True, c.weights[:, :, :])
        gather_pass(nc, c, io)
        message_pass(nc, c, io)
        weights_pass(nc, c, lambda h: c.scores[:, :, h], False, c.weights[:, :, :])
        out_pass(nc, c, out)


INS = ["x", "src", "dst", "edge_attr_64", "L0_gnn_W", "L0_gnn_attn", "L0_gnn_W_out", "L1_gnn_W_edge", "L1_gnn_W_n2m",
       "L1_gnn_Wq", "L1_gnn_bq", "L1_gnn_Wk", "L1_gnn_bk", "L1_gnn_Wv", "L1_gnn_bv", "L1_gnn_We", "L1_gnn_Wskip",
       "L1_gnn_bskip", "L1_gnn_Wbeta", "L1_gnn_W_m2n"]


def kernel(**inputs):
    import numpy as np
    import concourse.bacc as bacc
    from concourse.bass_utils import run_bass_kernel_spmd

    nc = bacc.Bacc("TRN2", target_bir_lowering=False, num_devices=1)
    arrays, io = {}, {}
    for name in INS:
        a = np.ascontiguousarray(inputs[name])
        arrays[f"in_{name}"] = a
        io[name] = nc.dram_tensor(f"in_{name}", a.shape, mybir.dt.from_np(a.dtype), kind="ExternalInput").ap()
    out = nc.dram_tensor("out", (N, D), F32, kind="ExternalOutput").ap()
    build(nc, io, out)
    return run_bass_kernel_spmd(nc, [arrays], core_ids=[0]).results[0]["out"]
```

```python
from contextlib import ExitStack

import concourse.bass as bass
from concourse import mybir

ALU = mybir.AluOpType
ACT = mybir.ActivationFunctionType
AX = mybir.AxisListType
F32 = mybir.dt.float32
I32 = mybir.dt.int32

P = 128
N, D = 50000, 256
E = 12500
H, HD = 4, 64
DM, RAD = 128, 64
CH = DM // H
EDGES, TILES = 125, 100
G = 5
QS = TILES // G
ROWS = TILES * P
HP = D + H
VP = DM + H
XL = DM + 1
NT = 2
NROWS = NT * P
NFULL = N // NROWS
NSTEPS = NFULL + 1
BIG = 1.0e38
SKIP = 1 << 17
EPS = 1e-5
RSQRT_SEED = 0x5F3759DF


def at_least(eng, sem, value, turn=None):
    if isinstance(value, int):
        if value > 0:
            eng.wait_ge(sem, value)
    else:
        eng.wait_ge(sem, value)
        if turn is not None:
            eng.sem_inc(turn, 1)


class Own:

    def __init__(self, eng, sem, turn):
        self.eng, self.sem, self.turn, self.base, self.n = eng, sem, turn, 0, 0

    def __call__(self, ins):
        self.n += 1
        ins.then_inc(self.sem, 1)

    def upto(self, n, turn=False):
        at_least(self.eng, self.sem, self.base + n, self.turn if turn else None)

    def done(self, turn=False):
        at_least(self.eng, self.sem, self.base + self.n, self.turn if turn else None)

    def loop(self, i, per):
        self.at, self.per = self.n, per
        self.base = i * per

    def looped(self, times):
        assert self.n - self.at == self.per, (self.n - self.at, self.per)
        self.n, self.base = self.at + self.per * times, 0


def clear_semaphores(nc, c):
    with nc.Block() as block:
        @block.gpsimd
        def _(pool):
            pool.sem_clear(range(min(c.semaphores), max(c.semaphores) + 1))


class Part:

    def __init__(self, total, unroll, lag, ahead=0, rounds=1, per=1):
        self.total, self.unroll, self.lag, self.ahead, self.rounds, self.per = total, unroll, lag, ahead, rounds, per
        self.peeled = unroll * rounds
        self.loops = (total - self.peeled - ahead) // (unroll * per)


def blend(lists):
    spread = [((2 * k + 1) / (2 * len(x)), n, entry) for n, x in enumerate(lists) for k, entry in enumerate(x)]
    return [(n, entry) for _, n, entry in sorted(spread, key=lambda e: e[:2])]


def steps(eng, own, per, parts, emits, cuts=()):
    times = min(p.loops for p in parts)
    split = isinstance(per, (list, tuple))
    pers, emitted = (per, emits) if split else ([per], [emits])

    def straight(entries, emit):
        for n, s in blend(entries):
            emit[n](s, s % parts[n].unroll, s // parts[n].unroll)

    straight([list(range(p.peeled)) for p in parts], emitted[0])
    bounds = [0, *cuts, times]
    for lo, hi, count, emit in zip(bounds[:-1], bounds[1:], pers, emitted):
        with eng.Fori(lo, hi) as i:
            own.loop(i - lo if lo else i, count)
            for n, j in blend([list(range(p.unroll * p.per)) for p in parts]):
                p = parts[n]
                q = p.per * i + (p.rounds + j // p.unroll)
                emit[n](p.unroll * p.per * i + (p.peeled + j), j % p.unroll, q)
            own.looped(hi - lo)
    straight([list(range(p.peeled + times * p.unroll * p.per, p.total + p.lag)) for p in parts], emitted[-1])


def idle(s, j, q):
    pass


def live(s, lag, total):
    return not isinstance(s, int) or 0 <= s - lag < total


def arrivals(j, q, unroll, behind, unit=16):
    rounds = q + (1 + (j - behind) // unroll)
    return unit * (max(0, rounds) if isinstance(q, int) else rounds)


def rsqrt(own, y, v, t):
    dve = own.eng
    own(dve.tensor_scalar(t.bitcast(I32), v.bitcast(I32), 1, None, ALU.logical_shift_right))
    own.done()
    own(dve.tensor_scalar(y.bitcast(I32), t.bitcast(I32), -1.0, float(RSQRT_SEED), ALU.mult, ALU.add))
    for _ in range(3):
        own.done()
        own(dve.tensor_tensor(t, y, y, ALU.mult))
        own.done()
        own(dve.scalar_tensor_tensor(out=t, in0=t, scalar=-0.5, in1=v, op0=ALU.mult, op1=ALU.mult))
        own.done()
        own(dve.scalar_tensor_tensor(out=y, in0=t, scalar=1.5, in1=y, op0=ALU.add, op1=ALU.mult))
    own.done()


class Core:

    def __init__(self):
        self.passes = 0
        self.semaphores = set()

    def name(self, name):
        return f"{name}_{self.passes}"

    def semaphore(self, nc, ctx, name):
        sem = ctx.enter_context(nc.semaphore(self.name(name)))
        self.semaphores.add(sem.num)
        return sem


def setup(nc, c, io):
    c.passes += 1
    with ExitStack() as ctx:
        def sb(name, shape, dt=F32):
            return ctx.enter_context(nc.sbuf_tensor(c.name(name), shape, dt))

        def sem(name):
            return c.semaphore(nc, ctx, name)

        w_n2m = sb("w_n2m", [P, D])
        w_sq = sb("w_sq", [P, 4, DM])
        w_sqT = sb("w_sqT", [P, 4, DM])
        w_m2n = sb("w_m2n", [P, 2, DM])
        w_skipn = sb("w_skipn", [P, D])
        w_edge = sb("w_edge", [RAD, RAD])
        w_e = sb("w_e", [P, RAD])
        w_eT = sb("w_eT", [RAD, DM])
        attn = sb("attn", [P, H, 2 * HD])
        prod = sb("prod", [P, 2, H, HD])
        beta = sb("beta", [P, 3])
        wb = sb("wb", [P, 1])
        bs_cols = sb("bs_cols", [P, P])
        zero = sb("zero", [P, P])
        mean_w = sb("mean_w", [P, P])
        xlw = sb("xlw", [P, 2])
        qs_raw = sb("qs_raw", [P, 2, D])
        ldd = sem("ldd")
        ident_ready = sem("ident_ready")
        pool_done = sem("pool_done")
        pe_done = sem("pe_done")
        dve_done = sem("dve_done")
        ps = c.psum
        LOADS = 17

        with nc.Block() as block:
            @block.sync
            def _(sp):
                with nc.allow_non_contiguous_dma(reason="a few short weight rows"):
                    sp.dma_start(w_n2m[:, :], io["L1_gnn_W_n2m"]).then_inc(ldd, 16)
                    for k, name in enumerate(("Wq", "Wk", "Wv", "Wskip")):
                        sp.dma_start(w_sq[:, k, :], io["L1_gnn_" + name]).then_inc(ldd, 16)
                    for k in range(2):
                        sp.dma_start(w_m2n[:, k, :], io["L1_gnn_W_m2n"][k * P:(k + 1) * P, :]).then_inc(ldd, 16)
                        sp.dma_start(c.wo[:, k, :], io["L0_gnn_W_out"][k * P:(k + 1) * P, :]).then_inc(ldd, 16)
                        sp.dma_start(c.wh[:, k, 0:D].rearrange("p (h d) -> p h d", h=H),
                                     io["L0_gnn_W"][:, k * P:(k + 1) * P, :].rearrange("h i d -> i h d")).then_inc(ldd, 16)
                    sp.dma_start(w_edge[:, :], io["L1_gnn_W_edge"]).then_inc(ldd, 16)
                    sp.dma_start(w_e[:, :], io["L1_gnn_We"]).then_inc(ldd, 16)
                    sp.dma_start(attn[:, :, :].rearrange("p h d -> p (h d)"),
                                 io["L0_gnn_attn"].rearrange("(a h) d -> a (h d)", a=1).to_broadcast([P, H * 2 * HD])).then_inc(ldd, 16)
                    for k in range(3):
                        sp.dma_start(beta[:, k:k + 1], io["L1_gnn_Wbeta"][:, k * DM:(k + 1) * DM].rearrange("a d -> d a")).then_inc(ldd, 16)

            @block.scalar
            def _(act):
                with nc.allow_non_contiguous_dma(reason="one bias column"):
                    act.dma_start(c.bq_xr[:, 0:DM], io["L1_gnn_bq"].rearrange("(a d) -> a d", a=1).to_broadcast([P, DM])).then_inc(ldd, 16)
                    act.dma_start(c.bq_xr[:, DM:2 * DM], io["L1_gnn_bskip"].rearrange("(a d) -> a d", a=1).to_broadcast([P, DM])).then_inc(ldd, 16)
                    act.dma_start(c.we2[RAD:RAD + 1, 0:DM], io["L1_gnn_bk"].rearrange("(a d) -> a d", a=1)).then_inc(ldd, 16)
                    act.dma_start(c.we2[RAD:RAD + 1, DM:2 * DM], io["L1_gnn_bv"].rearrange("(a d) -> a d", a=1)).then_inc(ldd, 16)
                    act.dma_start(c.wa_row[:, :], io["L1_gnn_Wbeta"][:, 0:DM].to_broadcast([P, DM])).then_inc(ldd, 16)
                    act.dma_start(c.wc_row[:, :], io["L1_gnn_Wbeta"][:, 2 * DM:3 * DM].to_broadcast([P, DM])).then_inc(ldd, 16)
                    act.dma_start(bs_cols[:, 0:1], io["L1_gnn_bskip"].rearrange("(d a) -> d a", a=1)).then_inc(ldd, 16)

            loads = 16 * (1 + 4 + 6 + 2 + 1 + 3 + 7)

            @block.gpsimd
            def _(pool):
                own = Own(pool, pool_done, None)
                own(pool.memset(c.ident[:, :], 0.0))
                own(pool.memset(zero[:, :], 0.0))
                own(pool.memset(mean_w[:, :], 1.0 / D))
                own(pool.memset(xlw[:, :], 0.0))
                own.done()
                pool.affine_select(out=c.ident[:, :], in_=c.ident[:, :], compare_op=ALU.not_equal, fill=1.0,
                                   base=0, pattern=[[-1, P]], channel_multiplier=1).then_inc(ident_ready, 1)

            def bank(b, rows, cols):
                return ps[0:rows, b, 0:cols]

            @block.tensor
            def _(pe):
                pe.wait_ge(ident_ready, 1)
                pe.wait_ge(ldd, loads)
                for k in range(4):
                    pe.transpose(ps[:, 0, k * P:(k + 1) * P], w_sq[:, k, :], c.ident[:, :])
                for k in range(2):
                    pe.transpose(ps[:, 1, k * P:(k + 1) * P], w_m2n[:, k, :], c.ident[:, :])
                pe.transpose(ps[0:RAD, 2, 0:P], w_e[:, :], c.ident[:, :]).then_inc(pe_done, 1)
                pe.wait_ge(dve_done, 9)
                for k in range(2):
                    lhs = w_n2m[:, k * P:(k + 1) * P]
                    for n, w in enumerate((0, 3)):
                        pe.matmul(ps[:, 3, n * DM:(n + 1) * DM] if k == 0 else ps[:, 4, n * DM:(n + 1) * DM], lhs, w_sqT[:, w, :], start=True, stop=True)
                    for n, w in enumerate((1, 2)):
                        pe.matmul(ps[:, 5, n * DM:(n + 1) * DM] if k == 0 else ps[:, 6, n * DM:(n + 1) * DM], lhs, w_sqT[:, w, :], start=True, stop=True)
                pe.matmul(ps[:, 7, 0:D], w_sqT[:, 3, :], w_n2m[:, :], start=True, stop=True)
                pe.matmul(bank(2, RAD, DM), w_edge[:, :], w_eT[:, :], start=True, stop=True).then_inc(pe_done, 1)
                pe.wait_ge(dve_done, 16)
                for k in range(2):
                    pe.matmul(ps[:, 3 + k, 0:D + 1], w_skipn[:, k * P:(k + 1) * P], c.w_out1[:, :], start=True, stop=True)
                    pe.matmul(ps[:, 5 + k, 0:1], w_skipn[:, k * P:(k + 1) * P], wb[:, :], start=True, stop=True)
                pe.matmul(ps[:, 7, 0:D + 1], bs_cols[:, :], c.w_out1[:, :], start=True, stop=True).then_inc(pe_done, 1)
                pe.wait_ge(dve_done, 21)
                for k in range(2):
                    last = pe.matmul(ps[:, 0, 0:D + 1], mean_w[:, :], c.m_ext[:, k, :], start=(k == 0), stop=(k == 1))
                last.then_inc(pe_done, 1)

            @block.vector
            def _(dve):
                own = Own(dve, dve_done, None)
                dve.wait_ge(ldd, loads)
                dve.wait_ge(pool_done, 4)
                own(dve.tensor_tensor(wb[:, :], beta[:, 1:2], beta[:, 2:3], ALU.subtract))
                own(dve.tensor_tensor(c.wa_row[:, :], c.wa_row[:, :], c.wc_row[:, :], ALU.add))
                dve.wait_ge(pe_done, 1)
                own(dve.tensor_copy(w_sqT[:, :, :].rearrange("p k d -> p (k d)"), ps[:, 0, 0:512]))
                own(dve.tensor_copy(c.w_out1[:, 0:D], ps[:, 1, 0:D]))
                own(dve.tensor_copy(w_eT[:, :], ps[0:RAD, 2, 0:DM]))
                own.done()
                own(dve.tensor_copy(c.w_out1[:, D:D + 1], wb[:, :]))
                own(dve.tensor_scalar(bs_cols[:, 1:P], zero[:, 1:P], bs_cols[:, 0:1], None, ALU.add))
                own(dve.memset(c.ones_col[:, :], 1.0))
                own(dve.memset(xlw[:, :], 0.0))
                dve.wait_ge(pe_done, 2)
                for k in range(2):
                    own(dve.tensor_copy(c.w_qs[:, k, 0:2 * DM], ps[:, 3 + k, 0:2 * DM]))
                    own(dve.tensor_copy(c.w_kv[:, k, :], ps[:, 5 + k, 0:2 * DM]))
                own(dve.tensor_copy(w_skipn[:, :], ps[:, 7, 0:D]))
                own(dve.tensor_copy(c.we2[0:RAD, 0:DM], ps[0:RAD, 2, 0:DM]))
                own(dve.tensor_copy(c.we2[0:RAD, DM:2 * DM], ps[0:RAD, 2, 0:DM]))
                dve.wait_ge(pe_done, 3)
                for k in range(2):
                    own(dve.tensor_copy(c.m_ext[:, k, :], ps[:, 3 + k, 0:D + 1]))
                    own(dve.tensor_copy(c.w_qs[:, k, 2 * DM:2 * DM + 1], ps[:, 5 + k, 0:1]))
                own(dve.tensor_copy(c.b_ext[:, :], ps[:, 7, 0:D + 1]))
                own.done()
                own(dve.tensor_copy(c.bq_xr[:, 2 * DM:2 * DM + 1], c.b_ext[:, D:D + 1]))
                dve.wait_ge(pe_done, 4)
                own.done()
                own(dve.scalar_tensor_tensor(out=c.b_ext[:, :], in0=c.b_ext[:, :], scalar=1.0 / D, in1=ps[:, 0, 0:D + 1], op0=ALU.mult, op1=ALU.subtract))
                own.done()
                for k in range(2):
                    own(dve.tensor_tensor(c.m_ext[:, k, :], c.m_ext[:, k, :], c.b_ext[:, :], ALU.add))
                for half, out in ((0, c.wh[:, :, D:HP]), (1, c.w_ad[:, :, :])):
                    for k in range(2):
                        own.done()
                        own(dve.tensor_tensor(prod[:, k, :, :], c.wh[:, k, 0:D].rearrange("p (h d) -> p h d", h=H),
                                              attn[:, :, half * HD:(half + 1) * HD], ALU.mult))
                    own.done()
                    for k in range(2):
                        own(dve.tensor_reduce(out[:, k, :], prod[:, k, :, :], AX.X, ALU.add))
                own.done()


def index_pass(nc, c, io):
    c.passes += 1
    dst, src = io["dst"], io["src"]
    rows = dst.rearrange("(t e) -> t e", e=EDGES)
    with ExitStack() as ctx:
        def sb(name, shape, dt=F32):
            return ctx.enter_context(nc.sbuf_tensor(c.name(name), shape, dt))

        def sem(name):
            return c.semaphore(nc, ctx, name)

        dsti = sb("dsti", [TILES, EDGES], I32)
        srci = sb("srci", [TILES, EDGES], I32)
        previ = sb("previ", [TILES, 1], I32)
        nexti = sb("nexti", [TILES, 1], I32)
        edgei = sb("edgei", [H, 2, TILES], I32)
        edgef = sb("edgef", [H, 2, TILES])
        dstf = sb("dstf", [TILES, EDGES])
        prevf = sb("prevf", [TILES, 1])
        nextf = sb("nextf", [TILES, 1])
        row = sb("row", [TILES, 5, P])
        islast = sb("islast", [TILES, EDGES])
        posi = sb("posi", [TILES, EDGES], I32)
        posf = sb("posf", [TILES, EDGES])
        fill = sb("fill", [80, N // 80], I32)
        idx_loads = sem("idx_loads")
        own_sem = sem("own_sem")
        minus = sem("minus")
        table = sem("table")
        turned = sem("turned")
        pool_ready = sem("pool_ready")
        LD = 16 * 6
        with nc.Block() as block:
            @block.sync
            def _(sp):
                with nc.allow_non_contiguous_dma(reason="400 first and last dst of the tiles, once"):
                    sp.dma_start(dsti[:, :], rows).then_inc(idx_loads, 16)
                    sp.dma_start(srci[:, :], src.rearrange("(t e) -> t e", e=EDGES)).then_inc(idx_loads, 16)
                    sp.dma_start(edgei[:, 0, :], dst.rearrange("(a t e) -> a t e", a=1, e=EDGES)[:, :, 0].to_broadcast([H, TILES])).then_inc(idx_loads, 16)
                    sp.dma_start(edgei[:, 1, :], dst.rearrange("(a t e) -> a t e", a=1, e=EDGES)[:, :, EDGES - 1].to_broadcast([H, TILES])).then_inc(idx_loads, 16)
                    sp.wait_ge(minus, 1)
                    sp.dma_start(previ[1:TILES, :], rows[0:TILES - 1, EDGES - 1:EDGES]).then_inc(idx_loads, 16)
                    sp.dma_start(nexti[0:TILES - 1, :], rows[1:TILES, 0:1]).then_inc(idx_loads, 16)
                sp.wait_ge(pool_ready, 1)
                sp.dma_start(c.pos_table.rearrange("(p n) a -> p (n a)", p=80), fill[:, :]).then_inc(table, 16)
                sp.wait_ge(own_sem, 17)
                sp.dma_start(c.col_ids, row[:, 4, :]).then_inc(table, 16)
                sp.wait_ge(table, 32)

            @block.gpsimd
            def _(pool):
                pool.iota(posi[:, :], [[1, EDGES]], base=1, channel_multiplier=P).then_inc(pool_ready, 1)
                pool.iota(c.own_pos[:, :], [[P, TILES]], base=0, channel_multiplier=1).then_inc(pool_ready, 1)

            @block.vector
            def _(dve):
                own = Own(dve, own_sem, None)
                own(dve.memset(previ[:, :], -1))
                own(dve.memset(nexti[:, :], -1))
                own(dve.memset(row[:, 0:2, :], 0.0))
                own(dve.memset(row[:, 2, :], float(SKIP)))
                own(dve.memset(row[:, 3, :], -2.0))
                own(dve.memset(row[:, 4, :], -3.0))
                dve.memset(fill[:, :], SKIP).then_inc(minus, 1)
                dve.wait_ge(idx_loads, LD)
                dve.wait_ge(minus, 1)
                dve.wait_ge(pool_ready, 2)
                for out, into in ((dstf, dsti), (prevf, previ), (nextf, nexti), (posf, posi)):
                    own(dve.tensor_copy(out[:, :], into[:, :]))
                own(dve.tensor_copy(edgef[:, :, :], edgei[:, :, :]))
                own(dve.tensor_copy(row[:, 0, 1:1 + EDGES], srci[:, :]))
                own(dve.tensor_copy(row[:, 1, 1:1 + EDGES], dsti[:, :]))
                own.done()
                own(dve.tensor_copy(row[:, 3, 0:1], prevf[:, :]))
                own(dve.tensor_copy(row[:, 3, 1:1 + EDGES], dstf[:, :]))
                own(dve.tensor_copy(row[:, 4, 0:1], dstf[:, EDGES - 1:EDGES]))
                own(dve.tensor_copy(row[:, 4, 1:1 + EDGES], dstf[:, :]))
                own(dve.tensor_tensor(islast[:, 0:EDGES - 1], dstf[:, 0:EDGES - 1], dstf[:, 1:EDGES], ALU.not_equal))
                own(dve.tensor_tensor(islast[:, EDGES - 1:EDGES], dstf[:, EDGES - 1:EDGES], nextf[:, :], ALU.not_equal))
                own.done()
                own(dve.memset(c.cut[:, :, :, :], -BIG))
                own.done()
                for h in range(H):
                    own(dve.tensor_scalar(c.cut[:, 0, h, 1:EDGES], islast[:, 0:EDGES - 1], -BIG, None, ALU.mult))
                    own(dve.tensor_scalar(c.cut[:, 1, h, 0:EDGES - 1], islast[:, 0:EDGES - 1], -BIG, None, ALU.mult))
                for k, end in ((0, prevf), (1, nextf)):
                    own(dve.tensor_scalar(c.open_[:, k, :], dstf[:, :], end[:, :], None, ALU.is_equal))
                own.done()
                own(dve.tensor_scalar(c.open_[:, :, :], c.open_[:, :, :], -1.0, BIG, ALU.add, ALU.mult))
                own(dve.memset(c.whole[:, :, :], -BIG))
                own.done()
                own(dve.tensor_tensor(c.whole[:, 0, 1:TILES], edgef[:, 1, 0:TILES - 1], edgef[:, 1, 1:TILES], ALU.is_equal))
                own(dve.tensor_tensor(c.whole[:, 1, 0:TILES - 1], edgef[:, 0, 0:TILES - 1], edgef[:, 0, 1:TILES], ALU.is_equal))
                own.done()
                own(dve.tensor_scalar(c.whole[:, 0, 1:TILES], c.whole[:, 0, 1:TILES], -1.0, BIG, ALU.add, ALU.mult))
                own(dve.tensor_scalar(c.whole[:, 1, 0:TILES - 1], c.whole[:, 1, 0:TILES - 1], -1.0, BIG, ALU.add, ALU.mult))
                own(dve.tensor_scalar(row[:, 2, 1:1 + EDGES], dstf[:, :], -float(SKIP), None, ALU.add))
                own.done()
                own(dve.tensor_tensor(row[:, 2, 1:1 + EDGES], row[:, 2, 1:1 + EDGES], islast[:, :], ALU.mult))
                own.done()
                own(dve.tensor_scalar(row[:, 2, 1:1 + EDGES], row[:, 2, 1:1 + EDGES], float(SKIP), None, ALU.add))
                for h in range(H):
                    own(dve.tensor_copy(c.val[:, h, :], posf[:, :]))
                own.done()

            @block.tensor
            def _(pe):
                pe.wait_ge(own_sem, 43)
                for k in range(4):
                    last = pe.transpose(c.psum[:, k // 2, (k % 2) * 256:(k % 2) * 256 + TILES], row[:, k, :], c.ident[0:TILES, 0:TILES])
                last.then_inc(turned, 1)

            @block.scalar
            def _(act):
                act.wait_ge(turned, 1)
                for k, out in enumerate((c.src_col, c.dst_col, c.last_col, c.row_ids)):
                    act.activation(out[:, :], c.psum[:, k // 2, (k % 2) * 256:(k % 2) * 256 + TILES], ACT.Copy).then_inc(turned, 1)
                act.wait_ge(turned, 5)


def scratch_for_max(nc, c, ctx):
    def sb(name, shape):
        return ctx.enter_context(nc.sbuf_tensor(c.name(name), shape, F32))

    c.val, c.fwd, c.bwd, c.top = (sb(name, [TILES, H, EDGES]) for name in ("val", "fwd", "bwd", "top"))
    c.ends = sb("ends", [TILES, 2, H])
    c.run = sb("run", [H, 2, TILES])
    c.run2 = sb("run2", [H, 2, TILES + 1])
    c.carried = sb("carried", [TILES, 2, H])


def max_of_segments(nc, c, dve, own, asks, answers, n):
    flat = "p h e -> p (h e)"
    val, fwd, bwd = (x[:, :, :].rearrange(flat) for x in (c.val, c.fwd, c.bwd))
    own(dve.tensor_tensor_scan(fwd, c.cut[:, 0, :, :].rearrange(flat), val, -BIG, ALU.add, ALU.max))
    own(dve.tensor_tensor_scan(bwd[:, ::-1], c.cut[:, 1, :, :].rearrange(flat)[:, ::-1], val[:, ::-1], -BIG, ALU.add, ALU.max))
    own.done()
    own(dve.tensor_copy(c.ends[:, 0, :], c.fwd[:, :, EDGES - 1]))
    own(dve.tensor_copy(c.ends[:, 1, :], c.bwd[:, :, 0]))
    own.done()
    own(dve.tensor_tensor(c.top[:, :, :], c.fwd[:, :, :], c.bwd[:, :, :], ALU.max))
    own.done()
    dve.sem_inc(asks, 1)
    dve.wait_ge(answers, 2 * n + 1)
    own(dve.tensor_copy(c.run[:, 0, :], c.psum[0:H, 0, 0:TILES]))
    own(dve.tensor_copy(c.run[:, 1, :], c.psum[0:H, 0, 256:256 + TILES]))
    own.done()
    own(dve.tensor_tensor_scan(c.run2[:, 0, 1:TILES + 1], c.whole[:, 0, :], c.run[:, 0, :], -BIG, ALU.add, ALU.max))
    own(dve.tensor_tensor_scan(c.run2[:, 1, 0:TILES][:, ::-1], c.whole[:, 1, :][:, ::-1], c.run[:, 1, :][:, ::-1], -BIG, ALU.add, ALU.max))
    own(dve.memset(c.run2[:, 0, 0:1], -BIG))
    own(dve.memset(c.run2[:, 1, TILES:TILES + 1], -BIG))
    own.done()
    dve.sem_inc(asks, 1)
    dve.wait_ge(answers, 2 * n + 2)
    own(dve.tensor_copy(c.carried[:, 0, :], c.psum[0:TILES, 1, 0:H]))
    own(dve.tensor_copy(c.carried[:, 1, :], c.psum[0:TILES, 1, 256:256 + H]))
    for k in range(2):
        own.done()
        for h in range(H):
            own(dve.scalar_tensor_tensor(out=c.top[:, h, :], in0=c.open_[:, k, :], scalar=c.carried[:, k, h:h + 1],
                                         in1=c.top[:, h, :], op0=ALU.add, op1=ALU.max))
    own.done()


def turns_for_max(pe, c, asks, answers, n):
    pe.wait_ge(asks, 2 * n + 1)
    for k in range(2):
        last = pe.transpose(c.psum[0:H, 0, 256 * k:256 * k + TILES], c.ends[:, k, :], c.ident[0:TILES, 0:TILES])
    last.then_inc(answers, 1)
    pe.wait_ge(asks, 2 * n + 2)
    pe.transpose(c.psum[0:TILES, 1, 0:H], c.run2[:, 0, 0:TILES], c.ident[0:H, 0:H])
    pe.transpose(c.psum[0:TILES, 1, 256:256 + H], c.run2[:, 1, 1:TILES + 1], c.ident[0:H, 0:H]).then_inc(answers, 1)


def position_pass(nc, c):
    c.passes += 1
    with ExitStack() as ctx:
        own_sem, asks, answers, turned, ready = (c.semaphore(nc, ctx, n) for n in ("own_sem", "asks", "answers", "turned", "ready"))
        padded = ctx.enter_context(nc.sbuf_tensor(c.name("padded"), [TILES, P], F32))
        with nc.Block() as block:
            @block.vector
            def _(dve):
                own = Own(dve, own_sem, None)
                max_of_segments(nc, c, dve, own, asks, answers, 0)
                own(dve.memset(padded[:, :], 0.0))
                own.done()
                dve.tensor_copy(padded[:, 1:1 + EDGES], c.top[:, 0, :]).then_inc(ready, 1)

            @block.tensor
            def _(pe):
                turns_for_max(pe, c, asks, answers, 0)
                pe.wait_ge(ready, 1)
                pe.transpose(c.psum[:, 2, 0:TILES], padded[:, :], c.ident[0:TILES, 0:TILES]).then_inc(turned, 1)

            @block.scalar
            def _(act):
                act.wait_ge(turned, 1)
                act.activation(c.last_pos[:, :], c.psum[:, 2, 0:TILES], ACT.Copy).then_inc(ready, 1)
                act.wait_ge(ready, 2)


def weights_pass(nc, c, score_of, leaky, out):
    c.passes += 1
    with ExitStack() as ctx:
        own_sem, asks, answers, turned, ready, back = (c.semaphore(nc, ctx, n) for n in ("own_sem", "asks", "answers", "turned", "ready", "back"))
        scratch_for_max(nc, c, ctx)
        raw = ctx.enter_context(nc.sbuf_tensor(c.name("raw"), [TILES, H, EDGES], F32))
        weights = ctx.enter_context(nc.sbuf_tensor(c.name("weights"), [TILES, H, P], F32))
        with nc.Block() as block:
            @block.tensor
            def _(pe):
                for h in range(H):
                    last = pe.transpose(c.psum[0:TILES, 3, h * P:(h + 1) * P], score_of(h), c.ident[:, :])
                last.then_inc(turned, 1)
                turns_for_max(pe, c, asks, answers, 0)
                pe.wait_ge(ready, 2)
                for h in range(H):
                    last = pe.transpose(c.psum[:, 4, h * P:h * P + TILES], weights[:, h, :], c.ident[0:TILES, 0:TILES])
                last.then_inc(back, 1)

            @block.vector
            def _(dve):
                own = Own(dve, own_sem, None)
                dve.wait_ge(turned, 1)
                scores = c.psum[0:TILES, 3, :].rearrange("p (h e) -> p h e", h=H)[:, :, 1:1 + EDGES]
                own(dve.tensor_copy(raw[:, :, :], scores))
                own(dve.memset(weights[:, :, :], 0.0))
                own.done()
                if leaky:
                    own(dve.scalar_tensor_tensor(out=c.val[:, :, :].rearrange("p h e -> p (h e)"), in0=raw[:, :, :].rearrange("p h e -> p (h e)"), scalar=0.2,
                                                 in1=raw[:, :, :].rearrange("p h e -> p (h e)"), op0=ALU.mult, op1=ALU.max))
                else:
                    own(dve.tensor_scalar(c.val[:, :, :], raw[:, :, :], 1.0 / float(CH) ** 0.5, None, ALU.mult))
                own.done()
                max_of_segments(nc, c, dve, own, asks, answers, 0)
                own(dve.tensor_tensor(raw[:, :, :], c.val[:, :, :], c.top[:, :, :], ALU.subtract))
                own.done()
                dve.tensor_scalar(raw[:, :, :], raw[:, :, :], 20.0 if leaky else BIG, None, ALU.min).then_inc(ready, 1)

            @block.scalar
            def _(act):
                act.wait_ge(ready, 1)
                act.activation(weights[:, :, 1:1 + EDGES], raw[:, :, :], ACT.Exp).then_inc(ready, 1)
                act.wait_ge(back, 1)
                act.activation(out.rearrange("p t h -> p h t"), c.psum[:, 4, :].rearrange("p (h t) -> p h t", h=H)[:, :, 0:TILES], ACT.Copy).then_inc(ready, 1)
                act.wait_ge(ready, 3)


NODE_PARTS = (80, 80, NSTEPS - 160)


class NodePart:
    U = 8
    LAG = 6
    DVE = 8 * (2 * NT + (NT - 1) + 2 * NT + 1 + 11 + 1)

    def __init__(self, nc, c, ctx, x, out, first, count):
        U = self.U
        self.nc, self.c, self.x, self.out, self.first = nc, c, x, out, first
        self.xv = x[0:NFULL * NROWS, :].rearrange("(s p j) d -> s p (j d)", p=P, j=NT)
        self.ov = out[0:NFULL * NROWS, :].rearrange("(s p j) d -> s p (j d)", p=P, j=NT)
        self.part = Part(count, U, self.LAG, 2)

        def sb(name, shape, dt=F32):
            return ctx.enter_context(nc.sbuf_tensor(c.name("node_" + name), shape, dt))

        def sem(name):
            return c.semaphore(nc, ctx, "node_" + name)

        self.X = sb("X", [P, U, NT, D])
        self.Y = sb("Y", [P, 2, NT, D])
        self.XT = sb("XT", [P, 2, NT * D])
        self.st = sb("st", [P, 2, NT, 6])
        self.mv = sb("mv", [P, 2, NT, 2])
        self.vv = sb("vv", [P, 2, NT])
        self.r = sb("r", [P, 4, 2, NT])
        self.nm = sb("nm", [P, 4, 2, NT])
        self.be = sb("be", [P, 4, NT])
        self.tmp = sb("tmp", [P, 2, NT])
        self.loaded = [sem(f"loaded{j}") for j in range(U)]
        self.stored = [sem(f"stored{j}") for j in range(U)]
        self.roots_ready, self.x1_ready, self.turned, self.xt_ready, self.product, self.beta_ready, self.updated, self.normed = (
            sem(n) for n in ("roots_ready", "x1_ready", "turned", "xt_ready", "product", "beta_ready", "updated", "normed"))

    def rows_of(self, view, whole, s):
        if isinstance(s, int) and s + self.first == NFULL:
            return whole[N - NROWS:N, :].rearrange("(p j) d -> p (j d)", j=NT)
        return view[bass.ds(s + self.first, 1), :, :].rearrange("s p n -> (s p) n")

    def load(self, sp, s, j):
        sp.dma_start(self.X[:, j, :, :].rearrange("p j d -> p (j d)"), self.rows_of(self.xv, self.x, s)).then_inc(self.loaded[j], 16)

    def sync_start(self, own):
        for s in range(2):
            self.load(own.eng, s, s)

    def sync(self, own):
        sp, U = own.eng, self.U

        def emit(s, j, q):
            if live(s, -2, self.part.total):
                at_least(sp, self.normed, s - U + 3, own.turn)
                self.load(sp, s + 2, (j + 2) % U)
        return emit

    def scalar(self, own):
        act, c, U, total, X = own.eng, self.c, self.U, self.part.total, self.X

        def emit(s, j, q):
            if live(s, 4, total):
                o, b = j % 4, NT * (j % 2)
                at_least(act, self.product, s - 3)
                at_least(act, self.updated, s - 7)
                act.activation(self.be[:, o, :], c.psum[:, b:b + NT, D], ACT.Sigmoid).then_inc(self.beta_ready, 1)
            if live(s, 1, total):
                o, w = (j - 1) % U, (j - 1) % 4
                at_least(act, self.roots_ready, s)
                for k in range(NT):
                    last = act.activation(X[:, o, k, :], X[:, o, k, :], ACT.Identity, bias=self.nm[:, w, 0, k:k + 1], scale=self.r[:, w, 0, k:k + 1])
                last.then_inc(self.x1_ready, 1)
            if live(s, 6, total):
                o, w = (j - 6) % U, (j - 1) % 4
                at_least(act, self.roots_ready, s)
                at_least(act, self.stored[(j - 8) % U], arrivals(j, q, U, 8))
                for k in range(NT):
                    last = act.activation(self.Y[:, j % 2, k, :], X[:, o, k, :], ACT.Identity, bias=self.nm[:, w, 1, k:k + 1], scale=self.r[:, w, 1, k:k + 1])
                last.then_inc(self.normed, 1)
            if live(s, 2, total):
                at_least(act, self.turned, s - 1)
                at_least(act, self.product, s - 3)
                act.activation(self.XT[:, j % 2, :], c.psum[:, 4, 0:NT * D], ACT.Copy).then_inc(self.xt_ready, 1)
            if live(s, 6, total):
                at_least(act, self.normed, s - 5, own.turn)
                if isinstance(s, int) and s - 6 + self.first == NFULL:
                    act.wait_ge(self.stored[(total - 2) % U], 16 * ((total - 2) // U + 1))
                act.dma_start(self.rows_of(self.ov, self.out, s - 6), self.Y[:, j % 2, :, :].rearrange("p j d -> p (j d)")).then_inc(self.stored[(j - 6) % U], 16)
        return emit

    def scalar_end(self, act):
        for j in range(self.U):
            act.wait_ge(self.stored[j], 16 * ((self.part.total - 1 - j) // self.U + 1))

    def tensor(self, own):
        pe, c, U, total, ps = own.eng, self.c, self.U, self.part.total, self.c.psum

        def emit(s, j, q):
            if live(s, 2, total):
                at_least(pe, self.x1_ready, s - 1)
                at_least(pe, self.xt_ready, s - 2)
                for k in range(NT):
                    for h in range(2):
                        last = pe.transpose(ps[:, 4, k * D + h * P:k * D + (h + 1) * P], self.X[:, (j - 2) % U, k, h * P:(h + 1) * P], c.ident[:, :])
                last.then_inc(self.turned, 1)
            if live(s, 3, total):
                at_least(pe, self.xt_ready, s - 2)
                at_least(pe, self.updated, s - 4)
                o = (j - 3) % 2
                for k in range(NT):
                    for h in range(2):
                        last = pe.matmul(ps[:, NT * o + k, 0:D + 1], self.XT[:, o, k * D + h * P:k * D + (h + 1) * P], c.m_ext[:, h, :],
                                         start=(h == 0), stop=(h == 1))
                last.then_inc(self.product, 1)
        return emit

    def vector(self, own):
        dve, c, U, total, ps = own.eng, self.c, self.U, self.part.total, self.c.psum
        X, st, mv, vv, tmp, r, nm = self.X, self.st, self.mv, self.vv, self.tmp, self.r, self.nm

        def emit(s, j, q):
            chain = roots(s, j) if live(s, 0, total) or live(s, 5, total) else iter(())
            next(chain, None)
            if live(s, -1, total):
                at_least(dve, self.loaded[(j + 1) % U], arrivals(j, q, U, -1))
                for k in range(NT):
                    own(dve.bn_stats(st[:, 0, k, :], X[:, (j + 1) % U, k, :]))
                    next(chain, None)
            if live(s, 4, total):
                o, b = (j - 4) % U, NT * (j % 2)
                at_least(dve, self.beta_ready, s - 3)
                for k in range(NT):
                    ins = dve.scalar_tensor_tensor(out=X[:, o, k, :], in0=ps[:, b + k, 0:D], scalar=self.be[:, j % 4, k:k + 1],
                                                   in1=X[:, o, k, :], op0=ALU.mult, op1=ALU.add)
                    if k < NT - 1:
                        own(ins)
                    else:
                        ins.then_inc(self.updated, 1)
                    next(chain, None)
                at_least(dve, self.updated, s - 3)
                for k in range(NT):
                    own(dve.bn_stats(st[:, 1, k, :], X[:, o, k, :]))
                    next(chain, None)
            for _ in chain:
                pass
            own.done(True)
            for side, lag in ((0, -1), (1, 4)):
                if live(s, lag, total):
                    for k in range(NT):
                        own(dve.bn_aggr(mv[:, side, k, :], st[:, side, k, :]))
            own.done()

        def roots(s, j):
            first, last = live(s, 0, total), live(s, 5, total)
            lo, hi = (0 if first else 1), (2 if last else 1)
            w = j % 4
            v, y, t = vv[:, lo:hi, :], r[:, w, lo:hi, :], tmp[:, lo:hi, :]
            own(dve.tensor_scalar(v, mv[:, lo:hi, :, 1], EPS, None, ALU.add))
            n = own.n
            yield
            own.upto(n)
            own(dve.tensor_scalar(t.bitcast(I32), v.bitcast(I32), 1, None, ALU.logical_shift_right))
            n = own.n
            yield
            own.upto(n)
            at_least(dve, self.x1_ready, s - 2) if first else dve.wait_ge(self.normed, min(s - 8, total))
            own(dve.tensor_scalar(y.bitcast(I32), t.bitcast(I32), -1.0, float(RSQRT_SEED), ALU.mult, ALU.add))
            for _ in range(3):
                n = own.n
                yield
                own.upto(n)
                own(dve.tensor_tensor(t, y, y, ALU.mult))
                n = own.n
                yield
                own.upto(n)
                own(dve.scalar_tensor_tensor(out=t, in0=t, scalar=-0.5, in1=v, op0=ALU.mult, op1=ALU.mult))
                n = own.n
                yield
                own.upto(n)
                own(dve.scalar_tensor_tensor(out=y, in0=t, scalar=1.5, in1=y, op0=ALU.add, op1=ALU.mult))
            n = own.n
            yield
            own.upto(n)
            ins = dve.scalar_tensor_tensor(out=nm[:, w, lo:hi, :], in0=mv[:, lo:hi, :, 0], scalar=-1.0, in1=y, op0=ALU.mult, op1=ALU.mult)
            if first:
                own(ins)
                n = own.n
                yield
                own.upto(n)
                ins = dve.tensor_scalar(nm[:, w, 0, :], nm[:, w, 0, :], 1.0, None, ALU.add)
            ins.then_inc(self.roots_ready, 1)
            at_least(dve, self.roots_ready, s + 1)
        return emit

    def vector_start(self, own):
        dve = own.eng
        dve.wait_ge(self.loaded[0], 16)
        for k in range(NT):
            own(dve.bn_stats(self.st[:, 0, k, :], self.X[:, 0, k, :]))
        own.done()
        for k in range(NT):
            own(dve.bn_aggr(self.mv[:, 0, k, :], self.st[:, 0, k, :]))
        own.done()


def score_pass(nc, c, io, out):
    x, U = io["x"], 2 * G
    c.passes += 1
    with ExitStack() as ctx:
        def sb(name, shape, dt=F32):
            return ctx.enter_context(nc.sbuf_tensor(c.name(name), shape, dt))

        def sem(name):
            return c.semaphore(nc, ctx, name)

        XS = sb("XS", [P, 2, G, D])
        XD = sb("XD", [P, 2, G, D])
        ST = sb("ST", [P, 2, 2 * D])
        isrc = [sb(f"isrc{b}", [P, G], I32) for b in range(2)]
        idst = [sb(f"idst{b}", [P, G], I32) for b in range(2)]
        gathered = [sem(f"gathered{b}") for b in range(2)]
        kept = [sem(f"kept{b}") for b in range(2)]
        e_turned, st_ready, e_product, h_ready, copied, dve_own, turn_p, turn_e, turn_a, turn_d, turn_s = (
            sem(n) for n in ("e_turned", "st_ready", "e_product", "h_ready", "copied", "dve_own", "turn_p", "turn_e", "turn_a", "turn_d", "turn_s"))
        ps = c.psum
        dst_rows = c.rows[0:ROWS, :].rearrange("(q k p) d -> q p k d", k=G, p=P)
        src_rows = c.rows[ROWS:2 * ROWS, :].rearrange("(q k p) d -> q p k d", k=G, p=P)
        node = NodePart(nc, c, ctx, x, out, 0, NODE_PARTS[0])
        parts = (node.part, Part(TILES, U, 2))
        with nc.Block() as block:
            @block.gpsimd
            def _(pool):
                own = Own(pool, copied, turn_p)

                def gather(q, b):
                    own(pool.tensor_copy(isrc[b][:, :], c.src_col[:, bass.ds(G * q, G)]))
                    own(pool.tensor_copy(idst[b][:, :], c.dst_col[:, bass.ds(G * q, G)]))
                    own.done(True)
                    for k in range(G):
                        for rows, idx in ((XS, isrc), (XD, idst)):
                            pool.indirect_dma_start(out=rows[:, b, k, :], out_offset=None, in_=x,
                                                    in_offset=bass.IndirectOffsetOnAxis(ap=idx[b][:, k:k + 1], axis=0)).then_inc(gathered[b], 16)

                def emit(t, j, q):
                    if j % G == 0 and live(t, -G, TILES):
                        n, b = 2 * q + j // G, (j // G + 1) % 2
                        at_least(pool, e_turned, t, turn_p)
                        at_least(pool, kept[b], arrivals(j, q, U, G, 32), turn_p)
                        gather(n + 1, b)
                gather(0, 0)
                steps(pool, own, 4, parts, (idle, emit))

            @block.sync
            def _(sp):
                own = Own(sp, turn_s, turn_s)

                def emit(t, j, q):
                    if j % G == 0 and live(t, 0, TILES):
                        b = j // G
                        at_least(sp, gathered[b], arrivals(j, q, U, 0, 32 * G), turn_s)
                        for rows, into in ((XD, dst_rows), (XS, src_rows)):
                            sp.dma_start(into[bass.ds(2 * q + b, 1), :, :, :].rearrange("q p k d -> (q p) k d"), rows[:, b, :, :]).then_inc(kept[b], 16)
                node.sync_start(own)
                steps(sp, own, 0, parts, (node.sync(own), emit))
                for b in range(2):
                    sp.wait_ge(kept[b], 32 * QS // 2)

            @block.tensor
            def _(pe):
                own = Own(pe, turn_e, None)

                def emit(t, j, q):
                    if live(t, 0, TILES + 1):
                        at_least(pe, st_ready, t)
                    if live(t, 0, TILES):
                        if j % G == 0:
                            at_least(pe, gathered[j // G], arrivals(j, q, U, 0, 32 * G))
                        for side, rows in enumerate((XS, XD)):
                            for h in range(2):
                                last = pe.transpose(ps[:, 5, (2 * side + h) * P:(2 * side + h + 1) * P], rows[:, j // G, j % G, h * P:(h + 1) * P], c.ident[:, :])
                        last.then_inc(e_turned, 1)
                    if live(t, 1, TILES):
                        o = (j - 1) % 2
                        at_least(pe, h_ready, t - 2)
                        for h in range(2):
                            pe.matmul(ps[:, 6 + o, 0:HP], ST[:, o, h * P:(h + 1) * P], c.wh[:, h, :], start=(h == 0), stop=(h == 1))
                        for h in range(2):
                            last = pe.matmul(ps[:, 6 + o, D:HP], ST[:, o, (2 + h) * P:(3 + h) * P], c.w_ad[:, h, :], start=False, stop=(h == 1), skip_group_check=True)
                        last.then_inc(e_product, 1)
                steps(pe, own, 0, parts, (node.tensor(own), emit))

            @block.scalar
            def _(act):
                own = Own(act, turn_a, turn_a)

                def emit(t, j, q):
                    if live(t, 0, TILES):
                        at_least(act, e_turned, t + 1)
                        at_least(act, e_product, t - 1)
                        act.activation(ST[:, j % 2, :], ps[:, 5, :], ACT.Copy).then_inc(st_ready, 1)
                steps(act, own, 0, parts, (node.scalar(own), emit))
                node.scalar_end(act)

            @block.vector
            def _(dve):
                own = Own(dve, dve_own, turn_d)

                def emit(t, j, q):
                    if live(t, 2, TILES):
                        at_least(dve, e_product, t - 1, turn_d)
                        dve.tensor_copy(c.store[:, bass.ds(t - 2, 1), 0:HP].rearrange("p a d -> p (a d)"), ps[:, 6 + j % 2, 0:HP]).then_inc(h_ready, 1)
                node.vector_start(own)
                steps(dve, own, node.DVE, parts, (node.vector(own), emit))
                dve.wait_ge(h_ready, TILES)


def gather_pass(nc, c, io, out):
    U, Q = 2 * G, 4
    c.passes += 1
    with ExitStack() as ctx:
        def sb(name, shape, dt=F32):
            return ctx.enter_context(nc.sbuf_tensor(c.name(name), shape, dt))

        def sem(name):
            return c.semaphore(nc, ctx, name)

        XD = sb("XD", [P, 2, G, D])
        MB = sb("MB", [P, 2, G, P])
        S = sb("S", [P, G, P])
        MSG = sb("MSG", [P, G, HP])
        AG = sb("AG", [P, 2, D])
        AT = sb("AT", [P, 2, D])
        rec = sb("rec", [P, 2, H])
        idx = [sb(f"idx{b}", [P, G], I32) for b in range(Q)]
        val = [sb(f"val{b}", [P, G], I32) for b in range(Q)]
        moved = [sem(f"moved{b}") for b in range(Q)]
        found = [sem(f"found{b}") for b in range(Q)]
        rows_in = [sem(f"rows_in{b}") for b in range(2)]
        ids = [sem(f"ids{b}") for b in range(2)]
        kept = [sem(f"kept{b}") for b in range(2)]
        made, matched, summed, carried, scaled, e_turned, at_ready, e_product, z_ready, copied, dve_own, turn_p, turn_e, turn_a, turn_d, turn_s = (
            sem(n) for n in ("made", "matched", "summed", "carried", "scaled", "e_turned", "at_ready", "e_product", "z_ready", "copied", "dve_own",
                             "turn_p", "turn_e", "turn_a", "turn_d", "turn_s"))
        ps = c.psum
        ids_v = c.col_ids.rearrange("(q k) m -> q (k m)", k=G)
        rows_v = c.rows[0:ROWS, :].rearrange("(q k p) d -> q p k d", k=G, p=P)
        node = NodePart(nc, c, ctx, io["x"], out, NODE_PARTS[0], NODE_PARTS[1])
        tiles = Part(TILES, U, 4, 2)
        parts = (node.part, tiles)
        loops = min(node.part.loops, tiles.loops)
        with nc.Block() as block:
            @block.gpsimd
            def _(pool):
                own = Own(pool, copied, turn_p)
                table = Part(2 * QS, Q, 0)
                half = (QS - Q) // Q

                def write(s, j, q):
                    at_least(pool, moved[j], arrivals(j, q, Q, Q, 16 * G), turn_p)
                    own(pool.tensor_copy(idx[j][:, :], c.last_col[:, bass.ds(G * s, G)]))
                    own(pool.tensor_copy(val[j][:, :], c.own_pos[:, bass.ds(G * s, G)]))
                    own.done(True)
                    for k in range(G):
                        pool.indirect_dma_start(out=c.pos_table, out_offset=bass.IndirectOffsetOnAxis(ap=idx[j][:, k:k + 1], axis=0),
                                                in_=val[j][:, k:k + 1], in_offset=None, bounds_check=N - 1, oob_is_err=False).then_inc(moved[j], 16)

                def read(s, j, q):
                    n = s - QS
                    if isinstance(s, int) and s < 2 * QS or not isinstance(s, int):
                        if j == 0:
                            for b in range(Q):
                                pool.wait_ge(moved[b], 16 * G * QS // Q)
                        own(pool.tensor_copy(idx[j][:, :], c.src_col[:, bass.ds(G * n, G)]))
                        own.done(True)
                        for k in range(G):
                            pool.indirect_dma_start(out=val[j][:, k:k + 1], out_offset=None, in_=c.pos_table,
                                                    in_offset=bass.IndirectOffsetOnAxis(ap=idx[j][:, k:k + 1], axis=0)).then_inc(found[j], 16)
                    if j == Q - 1:
                        for b in range(Q):
                            at_least(pool, found[b], 16 * G * (q - QS // Q + 1), turn_p)
                            own(pool.tensor_copy(c.src_pos[:, bass.ds(G * (n - Q + 1 + b), G)], val[b][:, :]))
                        own.done(True)

                def make(t, j):
                    k = j % G
                    at_least(pool, summed, t - G + 1, turn_p)
                    w = c.weights[:, bass.ds(t, 1), :].rearrange("p a h -> p (a h)")
                    pool.tensor_tensor(MSG[:, k, 0:D].rearrange("p (h d) -> p h d", h=H),
                                       c.store[:, bass.ds(t, 1), 0:D].rearrange("p a (h d) -> p (a h) d", h=H),
                                       w.unsqueeze(2).to_broadcast([P, H, HD]), ALU.mult)
                    pool.tensor_copy(MSG[:, k, D:HP], w).then_inc(made, 1)

                def emit(t, j, q):
                    if live(t, -2, TILES):
                        make(t + 2, (j + 2) % U)

                for t in range(2):
                    make(t, t)
                pool.wait_ge(made, 2)
                pool.memset(MSG[0:1, 0, :], 0.0).then_inc(carried, 1)
                steps(pool, own, (2 * Q, 2 * Q), (node.part, tiles, table), ((idle, emit, write), (idle, emit, read)), (half,))

            @block.sync
            def _(sp):
                own = Own(sp, turn_s, turn_s)

                def load_ids(n, b):
                    sp.dma_start(MB[:, b, :, :].rearrange("p k m -> p (k m)"), ids_v[bass.ds(n, 1), :].to_broadcast([P, G * P])).then_inc(ids[b], 16)

                def load_rows(n, b):
                    sp.dma_start(XD[:, b, :, :], rows_v[bass.ds(n, 1), :, :, :].rearrange("q p k d -> (q p) k d")).then_inc(rows_in[b], 16)

                def emit(t, j, q):
                    b = j // G
                    if j % G == 0 and live(t, -G, TILES):
                        at_least(sp, matched, t, turn_s)
                        load_ids(2 * q + b + 1, 1 - b)
                    if j % G == 3 and live(t, 3 + G, TILES + G):
                        n = 2 * q + b - 1
                        at_least(sp, z_ready, t - 3, turn_s)
                        sp.dma_start(rows_v[bass.ds(n, 1), :, :, :].rearrange("q p k d -> (q p) k d"), XD[:, 1 - b, :, :]).then_inc(kept[1 - b], 16)
                    if j % G == 4 and live(t, -1, TILES):
                        at_least(sp, kept[1 - b], arrivals(j, q, U, G), turn_s)
                        load_rows(2 * q + b + 1, 1 - b)
                load_ids(0, 0)
                load_rows(0, 0)
                node.sync_start(own)
                steps(sp, own, 0, parts, (node.sync(own), emit))
                for b in range(2):
                    sp.wait_ge(kept[b], 16 * (QS // 2))

            @block.tensor
            def _(pe):
                own = Own(pe, turn_e, None)

                def emit(t, j, q):
                    if live(t, 0, TILES):
                        at_least(pe, made, t + 1)
                        at_least(pe, matched, t + 1)
                        at_least(pe, carried, t + 1)
                        at_least(pe, scaled, t)
                        pe.matmul(ps[:, 5, 0:HP], S[:, j % G, :], MSG[:, j % G, :], start=True, stop=True).then_inc(summed, 1)
                    if live(t, 1, TILES):
                        at_least(pe, scaled, t)
                        at_least(pe, at_ready, t - 1)
                        o = (j - 1) % 2
                        for h in range(2):
                            last = pe.transpose(ps[:, 6, h * P:(h + 1) * P], AG[:, o, h * P:(h + 1) * P], c.ident[:, :])
                        last.then_inc(e_turned, 1)
                    if live(t, 2, TILES):
                        at_least(pe, at_ready, t - 1)
                        at_least(pe, z_ready, t - 2)
                        for h in range(2):
                            last = pe.matmul(ps[:, 7, 0:D], AT[:, j % 2, h * P:(h + 1) * P], c.wo[:, h, :], start=(h == 0), stop=(h == 1))
                        last.then_inc(e_product, 1)
                steps(pe, own, 0, parts, (node.tensor(own), emit))

            @block.scalar
            def _(act):
                own = Own(act, turn_a, turn_a)

                def emit(t, j, q):
                    if live(t, 0, TILES - 1):
                        at_least(act, made, t + 2)
                        at_least(act, summed, t + 1)
                        act.activation(MSG[0:1, (j + 1) % G, :], ps[0:1, 5, 0:HP], ACT.Copy).then_inc(carried, 1)
                    if live(t, 1, TILES):
                        o = (j - 1) % 2
                        at_least(act, e_turned, t)
                        at_least(act, e_product, t - 2)
                        act.activation(AT[:, o, :], ps[:, 6, 0:D], ACT.Copy).then_inc(at_ready, 1)
                steps(act, own, 0, parts, (node.scalar(own), emit))
                node.scalar_end(act)

            @block.vector
            def _(dve):
                own = Own(dve, dve_own, turn_d)

                def match(t, j, arrived):
                    if j % G == 0:
                        at_least(dve, ids[j // G], arrived)
                    at_least(dve, summed, t - G + 1)
                    dve.tensor_scalar(S[:, j % G, :], MB[:, j // G, j % G, :], c.row_ids[:, bass.ds(t, 1)], None, ALU.is_equal).then_inc(matched, 1)

                def emit(t, j, q):
                    if live(t, 3, TILES):
                        n = (j - 3) % U
                        if n % G == 0:
                            at_least(dve, rows_in[n // G], arrivals(j, q, U, 3))
                        at_least(dve, e_product, t - 2)
                        dve.tensor_tensor(XD[:, n // G, n % G, :], ps[:, 7, 0:D], XD[:, n // G, n % G, :], ALU.add).then_inc(z_ready, 1)
                    if live(t, -2, TILES):
                        match(t + 2, (j + 2) % U, arrivals(j, q, U, -2))
                    if live(t, 0, TILES):
                        o = j % 2
                        if isinstance(t, int) and t == TILES - 1:
                            dve.wait_ge(summed, TILES)
                        else:
                            at_least(dve, carried, t + 2)
                        at_least(dve, e_turned, t - 1)
                        own(dve.tensor_scalar(rec[:, o, :], ps[:, 5, D:HP], 1e-8, None, ALU.add))
                        own.done()
                        own(dve.reciprocal(rec[:, o, :], rec[:, o, :]))
                        own.done()
                        dve.tensor_tensor(AG[:, o, :].rearrange("p (h d) -> p h d", h=H), ps[:, 5, 0:D].rearrange("p (h d) -> p h d", h=H),
                                          rec[:, o, :].unsqueeze(2).to_broadcast([P, H, HD]), ALU.mult).then_inc(scaled, 1)
                node.vector_start(own)
                for t in range(2):
                    match(t, t, 16)
                steps(dve, own, node.DVE + U * 2, parts, (node.vector(own), emit))


def message_pass(nc, c, io, out):
    R, AHEAD = 4, 2
    U = R * G
    c.passes += 1
    with ExitStack() as ctx:
        def sb(name, shape, dt=F32):
            return ctx.enter_context(nc.sbuf_tensor(c.name(name), shape, dt))

        def sem(name):
            return c.semaphore(nc, ctx, name)

        Z = sb("Z", [P, R, G, 2, D])
        AT = sb("AT", [P, R, G, RAD + 1])
        ZT = sb("ZT", [P, 2, 2 * D])
        ET = sb("ET", [RAD + 1, 2, P])
        st = sb("st", [P, G * 2, 6])
        mv = sb("mv", [P, G * 2, 2])
        vv = sb("vv", [P, G * 2])
        r = sb("r", [P, 2, G * 2])
        nm = sb("nm", [P, 2, G * 2])
        tmp = sb("tmp", [P, G * 2])
        QK = sb("QK", [P, 2, DM])
        icol = [[sb(f"icol{b}{n}", [P, G], I32) for n in range(2)] for b in range(R)]
        gathered = [sem(f"gathered{b}") for b in range(R)]
        attrs = [sem(f"attrs{b}") for b in range(R)]
        picked, padded, roots, e_normed, a_turned, et_ready, e_turned, zt_ready, e_product, scored, v_ready, copied, dve_own, turn_e, turn_a, turn_d, turn_s, turn_p = (
            sem(n) for n in ("picked", "padded", "roots", "e_normed", "a_turned", "et_ready", "e_turned", "zt_ready", "e_product", "scored", "v_ready", "copied", "dve_own",
                             "turn_e", "turn_a", "turn_d", "turn_s", "turn_p"))
        ps = c.psum
        attr_v = io["edge_attr_64"].rearrange("(q k e) a -> q e k a", k=G, e=EDGES)
        node = NodePart(nc, c, ctx, io["x"], out, NODE_PARTS[0] + NODE_PARTS[1], NODE_PARTS[2])
        parts = (node.part, Part(TILES, U, 2, AHEAD * G))
        TA = 3 * P
        with nc.Block() as block:
            @block.gpsimd
            def _(pool):
                own = Own(pool, copied, turn_p)

                def gather(n, b):
                    for k, col in enumerate((c.src_pos, c.last_pos)):
                        own(pool.tensor_copy(icol[b][k][:, :], col[:, bass.ds(G * n, G)]))
                    own.done(True)
                    for k in range(G):
                        for side in range(2):
                            pool.indirect_dma_start(out=Z[:, b, k, side, :], out_offset=None, in_=c.rows,
                                                    in_offset=bass.IndirectOffsetOnAxis(ap=icol[b][side][:, k:k + 1], axis=0)).then_inc(gathered[b], 16)

                def emit(t, j, q):
                    if j % G == 0 and live(t, -AHEAD * G, TILES):
                        at_least(pool, e_turned, t - (R - AHEAD) * G + G, turn_p)
                        gather(R * q + j // G + AHEAD, (j // G + AHEAD) % R)
                pool.wait_ge(picked, 2)
                for n in range(AHEAD):
                    gather(n, n)
                steps(pool, own, 2 * R, parts, (idle, emit))

            @block.sync
            def _(sp):
                own = Own(sp, turn_s, turn_s)

                def load(n, b):
                    sp.dma_start(AT[1:1 + EDGES, b, :, 0:RAD], attr_v[bass.ds(n, 1), :, :, :].rearrange("q e k a -> (q e) k a")).then_inc(attrs[b], 16)

                def emit(t, j, q):
                    if j % G == 0 and live(t, -AHEAD * G, TILES):
                        at_least(sp, e_turned, t - (R - AHEAD) * G + G, turn_s)
                        load(R * q + j // G + AHEAD, (j // G + AHEAD) % R)
                node.sync_start(own)
                sp.wait_ge(padded, 2)
                for n in range(AHEAD):
                    load(n, n)
                steps(sp, own, 0, parts, (node.sync(own), emit))

            @block.tensor
            def _(pe):
                own = Own(pe, turn_e, None)

                def emit(t, j, q):
                    if live(t, 0, TILES):
                        b, k = j // G, j % G
                        if k == 0:
                            at_least(pe, attrs[b], arrivals(j, q, U, 0))
                        at_least(pe, scored, t - 1)
                        at_least(pe, et_ready, t)
                        pe.transpose(ps[0:RAD + 1, 7, TA:TA + P], AT[:, b, k, :], c.ident[:, :]).then_inc(a_turned, 1)
                        at_least(pe, zt_ready, t)
                        at_least(pe, e_normed, t + 1)
                        for side in range(2):
                            for h in range(2):
                                last = pe.transpose(ps[:, 5, (2 * side + h) * P:(2 * side + h + 1) * P], Z[:, b, k, side, h * P:(h + 1) * P], c.ident[:, :])
                        last.then_inc(e_turned, 1)
                    if live(t, 1, TILES):
                        o = (j - 1) % 2
                        at_least(pe, zt_ready, t)
                        at_least(pe, v_ready, t - 1)
                        for h in range(2):
                            pe.matmul(ps[:, 6, 0:2 * DM], ZT[:, o, h * P:(h + 1) * P], c.w_kv[:, h, :], start=(h == 0), stop=False)
                        pe.matmul(ps[:, 6, 0:2 * DM], ET[:, o, :], c.we2[:, :], start=False, stop=True)
                        at_least(pe, et_ready, t + 1 if live(t, 0, TILES) else TILES)
                        for h in range(2):
                            last = pe.matmul(ps[:, 7, 0:2 * DM + 1], ZT[:, o, (2 + h) * P:(3 + h) * P], c.w_qs[:, h, :], start=(h == 0), stop=(h == 1))
                        last.then_inc(e_product, 1)
                steps(pe, own, 0, parts, (node.tensor(own), emit))

            @block.scalar
            def _(act):
                own = Own(act, turn_a, turn_a)

                N1 = G - 1

                def normalise(b, k, count):
                    at_least(act, roots, count)
                    for side in range(2):
                        n = 2 * k + side
                        last = act.activation(Z[:, b, k, side, :], Z[:, b, k, side, :], ACT.Identity, bias=nm[:, b % 2, n:n + 1], scale=r[:, b % 2, n:n + 1])
                    last.then_inc(e_normed, 1)

                def emit(t, j, q):
                    if live(t, 2, TILES):
                        at_least(act, scored, t - 1, turn_a)
                        act.activation(c.store[:, bass.ds(t - 2, 1), 0:DM].rearrange("p a d -> p (a d)"), ps[:, 6, DM:2 * DM], ACT.Copy).then_inc(v_ready, 1)
                    if live(t, 0, TILES):
                        o = j % 2
                        at_least(act, a_turned, t + 1)
                        at_least(act, e_product, t - 1)
                        act.activation(ET[:, o, :], ps[0:RAD + 1, 7, TA:TA + P], ACT.Copy).then_inc(et_ready, 1)
                    if live(t, -N1, TILES):
                        m = (j + N1) % U
                        normalise(m // G, m % G, R * q + (j + N1) // G + 1)
                    if live(t, 0, TILES):
                        at_least(act, e_turned, t + 1)
                        act.activation(ZT[:, o, :], ps[:, 5, :], ACT.Copy).then_inc(zt_ready, 1)
                for k in range(N1):
                    normalise(0, k, 1)
                steps(act, own, 0, parts, (node.scalar(own), emit))
                act.wait_ge(v_ready, TILES)
                node.scalar_end(act)

            @block.vector
            def _(dve):
                own = Own(dve, dve_own, turn_d)
                alt = c.own_pos[:, :]
                dve.tensor_scalar(alt, alt, ROWS, None, ALU.add).then_inc(picked, 1)
                dve.wait_ge(picked, 1)
                dve.tensor_tensor(c.src_pos[:, :], c.src_pos[:, :], alt, ALU.min).then_inc(picked, 1)
                own(dve.memset(AT[:, :, :, :], 0.0))
                own.done()
                dve.memset(AT[:, :, :, RAD:RAD + 1], 1.0).then_inc(padded, 2)

                def statistics(b, arrived, free):
                    at_least(dve, gathered[b], arrived)
                    for k in range(G):
                        for side in range(2):
                            own(dve.bn_stats(st[:, 2 * k + side, :], Z[:, b, k, side, :]))
                    own.done(True)
                    for n in range(2 * G):
                        own(dve.bn_aggr(mv[:, n, :], st[:, n, :]))
                    own.done()
                    own(dve.tensor_scalar(vv[:, :], mv[:, :, 1], EPS, None, ALU.add))
                    own.done()
                    at_least(dve, e_normed, free)
                    rsqrt(own, r[:, b % 2, :], vv[:, :], tmp[:, :])
                    dve.scalar_tensor_tensor(out=nm[:, b % 2, :], in0=mv[:, :, 0], scalar=-1.0, in1=r[:, b % 2, :], op0=ALU.mult, op1=ALU.mult).then_inc(roots, 1)

                def emit(t, j, q):
                    if live(t, -G, TILES) and j % G == 0:
                        at_least(dve, roots, R * q + j // G + 1, turn_d)
                        statistics(((j + G) % U) // G, arrivals(j, q, U, -G, 32 * G), t)
                    if live(t, 1, TILES):
                        n, o = t - 1, (j - 1) % 2
                        at_least(dve, e_product, t)
                        own(dve.tensor_tensor(c.store[:, bass.ds(n, 1), 0:2 * DM + 1].rearrange("p a d -> p (a d)"),
                                              ps[:, 7, 0:2 * DM + 1], c.bq_xr[:, :], ALU.add))
                        own.done()
                        own(dve.tensor_tensor(QK[:, o, :], c.store[:, bass.ds(n, 1), 0:DM].rearrange("p a d -> p (a d)"), ps[:, 6, 0:DM], ALU.mult))
                        own.done(True)
                        dve.tensor_reduce(c.scores[:, bass.ds(n, 1), :].rearrange("p a h -> p (a h)"), QK[:, o, :].rearrange("p (h d) -> p h d", h=H), AX.X, ALU.add).then_inc(scored, 1)
                node.vector_start(own)
                statistics(0, 32 * G, 0)
                steps(dve, own, node.DVE + U * 2 + R * (4 * G + 1 + 11), parts, (node.vector(own), emit))
                dve.wait_ge(scored, TILES)


def out_pass(nc, c, out):
    c.passes += 1
    R = 4
    U = R * G
    with ExitStack() as ctx:
        def sb(name, shape, dt=F32):
            return ctx.enter_context(nc.sbuf_tensor(c.name(name), shape, dt))

        def sem(name):
            return c.semaphore(nc, ctx, name)

        Z = sb("Z", [P, R, G, D])
        MB = sb("MB", [P, R, G, P])
        S = sb("S", [P, G, P])
        MSG = sb("MSG", [P, G, VP])
        O = sb("O", [P, 4, DM])
        DF = sb("DF", [P, 4, DM])
        OW = sb("OW", [P, 4, DM])
        MX = sb("MX", [P, 2, DM])
        MT = sb("MT", [P, 2, DM])
        rec = sb("rec", [P, 2, H])
        lg = sb("lg", [P, 4, 1])
        be = sb("be", [P, 4, 1])
        st = sb("st", [P, G, 6])
        mv = sb("mv", [P, G, 2])
        vv = sb("vv", [P, G])
        r = sb("r", [P, 2, 2, G])
        nm = sb("nm", [P, 2, 2, G])
        tmp = sb("tmp", [P, G])
        icol = [sb(f"icol{b}", [P, G], I32) for b in range(R)]
        rows = [sem(f"rows{b}") for b in range(R)]
        ids = [sem(f"ids{b}") for b in range(R)]
        scattered = [sem(f"scattered{b}") for b in range(R)]
        roots, x1_ready, made, matched, summed, carried, logit, beta_ready, mixed, turned, mt_ready, product, z_ready, z_roots, normed, copied, dve_own, turn_p, turn_e, turn_a, turn_d, turn_s = (
            sem(n) for n in ("roots", "x1_ready", "made", "matched", "summed", "carried", "logit", "beta_ready", "mixed", "turned", "mt_ready",
                             "product", "z_ready", "z_roots", "normed", "copied", "dve_own", "turn_p", "turn_e", "turn_a", "turn_d", "turn_s"))
        ps = c.psum
        tiles = Part(TILES, U, 7, G)
        ids_v = c.col_ids.rearrange("(q k) m -> q (k m)", k=G)
        rows_v = c.rows[0:ROWS, :].rearrange("(q k p) d -> q p k d", k=G, p=P)


        with nc.Block() as block:
            @block.sync
            def _(sp):
                own = Own(sp, turn_s, None)

                def load(n, b):
                    sp.dma_start(Z[:, b, :, :], rows_v[bass.ds(n, 1), :, :, :].rearrange("q p k d -> (q p) k d")).then_inc(rows[b], 16)
                    sp.dma_start(MB[:, b, :, :].rearrange("p k m -> p (k m)"), ids_v[bass.ds(n, 1), :].to_broadcast([P, G * P])).then_inc(ids[b], 16)

                def emit(t, j, q):
                    if j % G == 3 and live(t, -2 * G + 3, TILES):
                        b = (j // G + 2) % R
                        at_least(sp, scattered[b], arrivals(j // G, q, R, 2, 16 * G), turn_s)
                        at_least(sp, matched, t - 3 - G, turn_s)
                        load(R * q + j // G + 2, b)
                for n in range(2):
                    load(n, n)
                steps(sp, own, 0, (tiles,), (emit,))

            @block.gpsimd
            def _(pool):
                own = Own(pool, copied, turn_p)

                def make(t, j):
                    k = j % G
                    at_least(pool, summed, t - G + 1, turn_p)
                    w = c.weights[:, bass.ds(t, 1), :].rearrange("p a h -> p (a h)")
                    pool.tensor_tensor(MSG[:, k, 0:DM].rearrange("p (h d) -> p h d", h=H),
                                       c.store[:, bass.ds(t, 1), 0:DM].rearrange("p a (h d) -> p (a h) d", h=H),
                                       w.unsqueeze(2).to_broadcast([P, H, CH]), ALU.mult)
                    pool.tensor_copy(MSG[:, k, DM:VP], w).then_inc(made, 1)

                def emit(t, j, q):
                    if live(t, -2, TILES):
                        make(t + 2, (j + 2) % U)
                    if j % G == 1 and live(t, 2 * G + 1, TILES):
                        b, n = (j // G - 2) % R, R * q + j // G - 2
                        at_least(pool, scattered[b], arrivals(j // G, q, R, 2 + R, 16 * G), turn_p)
                        own(pool.tensor_copy(icol[b][:, :], c.last_col[:, bass.ds(G * n, G)]))
                        own.done(True)
                        at_least(pool, normed, n + 1, turn_p)
                        for k in range(G):
                            pool.indirect_dma_start(out=out, out_offset=bass.IndirectOffsetOnAxis(ap=icol[b][:, k:k + 1], axis=0),
                                                    in_=Z[:, b, k, :], in_offset=None, bounds_check=N - 1, oob_is_err=False).then_inc(scattered[b], 16)
                for t in range(2):
                    make(t, t)
                pool.wait_ge(made, 2)
                pool.memset(MSG[0:1, 0, :], 0.0).then_inc(carried, 1)
                steps(pool, own, R, (tiles,), (emit,))
                for b in range(R):
                    pool.wait_ge(scattered[b], 16 * G * QS // R)

            @block.tensor
            def _(pe):
                own = Own(pe, turn_e, None)

                def emit(t, j, q):
                    if live(t, 0, TILES):
                        at_least(pe, made, t + 1)
                        at_least(pe, matched, t + 1)
                        at_least(pe, carried, t + 1)
                        at_least(pe, logit, t - 1)
                        pe.matmul(ps[:, j % 2, 0:VP], S[:, j % G, :], MSG[:, j % G, :], start=True, stop=True).then_inc(summed, 1)
                    if live(t, 3, TILES):
                        at_least(pe, mixed, t - 2)
                        at_least(pe, mt_ready, t - 4)
                        pe.transpose(ps[:, 2 + (j - 3) % 2, 0:DM], MX[:, (j - 3) % 2, :], c.ident[:, :]).then_inc(turned, 1)
                    if live(t, 4, TILES):
                        at_least(pe, mt_ready, t - 3)
                        at_least(pe, z_ready, t - 5)
                        pe.matmul(ps[:, 4 + j % 2, 0:D], MT[:, j % 2, :], c.w_out1[:, 0:D], start=True, stop=True).then_inc(product, 1)
                steps(pe, own, 0, (tiles,), (emit,))

            @block.scalar
            def _(act):
                own = Own(act, turn_a, turn_a)

                def normalise(b, side, done, ready, count):
                    at_least(act, ready, count)
                    for k in range(G):
                        last = act.activation(Z[:, b, k, :], Z[:, b, k, :], ACT.Identity, bias=nm[:, side, b % 2, k:k + 1], scale=r[:, side, b % 2, k:k + 1])
                    last.then_inc(done, 1)

                def emit(t, j, q):
                    k = j % G
                    if k == 2 and live(t, 2 - G, TILES):
                        normalise(((j + G - 2) % U) // G, 0, x1_ready, roots, R * q + j // G + 2)
                    if live(t, 0, TILES - 1):
                        at_least(act, made, t + 2)
                        at_least(act, summed, t + 1)
                        act.activation(MSG[0:1, (j + 1) % G, :], ps[0:1, j % 2, 0:VP], ACT.Copy).then_inc(carried, 1)
                    if live(t, 1, TILES):
                        at_least(act, logit, t)
                        at_least(act, mixed, t - 4)
                        act.activation(be[:, (j - 1) % 4, :], lg[:, (j - 1) % 4, :], ACT.Sigmoid).then_inc(beta_ready, 1)
                    if k == 0 and live(t, 2 * G, TILES):
                        normalise((j // G - 2) % R, 1, normed, z_roots, R * q + j // G - 1)
                    if live(t, 3, TILES):
                        at_least(act, turned, t - 2)
                        at_least(act, product, t - 4)
                        act.activation(MT[:, (j - 3) % 2, :], ps[:, 2 + (j - 3) % 2, 0:DM], ACT.Copy).then_inc(mt_ready, 1)
                normalise(0, 0, x1_ready, roots, 1)
                steps(act, own, 0, (tiles,), (emit,))

            @block.vector
            def _(dve):
                own = Own(dve, dve_own, turn_d)

                def statistics(b, side, ready, used):
                    for k in range(G):
                        own(dve.bn_stats(st[:, k, :], Z[:, b, k, :]))
                    own.done(True)
                    for n in range(G):
                        own(dve.bn_aggr(mv[:, n, :], st[:, n, :]))
                    own.done()
                    own(dve.tensor_scalar(vv[:, :], mv[:, :, 1], EPS, None, ALU.add))
                    own.done()
                    at_least(dve, *used)
                    rsqrt(own, r[:, side, b % 2, :], vv[:, :], tmp[:, :])
                    dve.scalar_tensor_tensor(out=nm[:, side, b % 2, :], in0=mv[:, :, 0], scalar=-1.0, in1=r[:, side, b % 2, :], op0=ALU.mult, op1=ALU.mult).then_inc(ready, 1)

                def match(t, j, arrived):
                    if j % G == 0:
                        at_least(dve, ids[j // G], arrived)
                    at_least(dve, summed, t - G + 1)
                    dve.tensor_scalar(S[:, j % G, :], MB[:, j // G, j % G, :], c.row_ids[:, bass.ds(t, 1)], None, ALU.is_equal).then_inc(matched, 1)

                def emit(t, j, q):
                    k, o, w = j % G, j % 2, j % 4
                    if k == 0 and live(t, -G, TILES):
                        b = ((j + G) % U) // G
                        at_least(dve, rows[b], arrivals(j, q, U, -G))
                        n = R * q + j // G
                        at_least(dve, roots, n + 1)
                        statistics(b, 0, roots, (x1_ready, n))
                    if live(t, 2, TILES):
                        m = (j - 2) % 4
                        at_least(dve, beta_ready, t - 1)
                        at_least(dve, turned, t - 3)
                        dve.scalar_tensor_tensor(out=MX[:, o, :], in0=DF[:, m, :], scalar=be[:, m, :], in1=O[:, m, :], op0=ALU.mult, op1=ALU.add).then_inc(mixed, 1)
                    if live(t, 5, TILES):
                        b, n = ((j - 5) % U) // G, k
                        if n == 0:
                            at_least(dve, x1_ready, R * q + j // G)
                        at_least(dve, product, t - 4)
                        dve.tensor_tensor(Z[:, b, n, :], ps[:, 4 + (j - 5) % 2, 0:D], Z[:, b, n, :], ALU.add).then_inc(z_ready, 1)
                        if n == G - 1:
                            at_least(dve, z_ready, t - 4)
                            n = R * q + j // G - 1
                            at_least(dve, z_roots, n)
                            statistics(b, 1, z_roots, (normed, n - 1))
                    if live(t, -2, TILES):
                        match(t + 2, (j + 2) % U, arrivals(j, q, U, -2))
                    if live(t, 0, TILES):
                        if isinstance(t, int) and t == TILES - 1:
                            dve.wait_ge(summed, TILES)
                        else:
                            at_least(dve, carried, t + 2)
                        own(dve.tensor_scalar(rec[:, o, :], ps[:, o, DM:VP], 1e-16, None, ALU.add))
                        own.done()
                        own(dve.reciprocal(rec[:, o, :], rec[:, o, :]))
                        own.done()
                        own(dve.tensor_tensor(O[:, w, :].rearrange("p (h d) -> p h d", h=H), ps[:, o, 0:DM].rearrange("p (h d) -> p h d", h=H),
                                              rec[:, o, :].unsqueeze(2).to_broadcast([P, H, CH]), ALU.mult))
                        own.done()
                        own(dve.tensor_tensor(DF[:, w, :], c.store[:, bass.ds(t, 1), DM:2 * DM].rearrange("p a d -> p (a d)"), O[:, w, :], ALU.subtract))
                        own(dve.tensor_tensor(OW[:, w, :], O[:, w, :], c.wa_row[:, :], ALU.mult))
                        own.done()
                        at_least(dve, beta_ready, t - 3)
                        own(dve.tensor_reduce(lg[:, w, :], OW[:, w, :], AX.X, ALU.add))
                        own.done()
                        dve.tensor_tensor(lg[:, w, :], lg[:, w, :], c.store[:, bass.ds(t, 1), 2 * DM:XL + DM].rearrange("p a d -> p (a d)"), ALU.add).then_inc(logit, 1)
                dve.wait_ge(rows[0], 16)
                statistics(0, 0, roots, (x1_ready, 0))
                for t in range(2):
                    match(t, t, 16)
                steps(dve, own, U * (3 + 2 + 1) + R * 2 * (2 * G + 1 + 11), (tiles,), (emit,))


def build(nc, io, out):
    with ExitStack() as ctx:
        c = Core()

        def sb(name, shape, dt=F32):
            return ctx.enter_context(nc.sbuf_tensor(name, shape, dt))

        c.psum = ctx.enter_context(nc.psum_tensor("banks", [P, 8, 512], F32))
        c.ident = sb("ident", [P, P])
        c.ones_col = sb("ones_col", [P, 1])
        c.wh = sb("wh", [P, 2, HP])
        c.w_ad = sb("w_ad", [P, 2, H])
        c.wo = sb("wo", [P, 2, D])
        c.w_kv = sb("w_kv", [P, 2, 2 * DM])
        c.w_qs = sb("w_qs", [P, 2, 2 * DM + 1])
        c.bq_xr = sb("bq_xr", [P, 2 * DM + 1])
        c.we2 = sb("we2", [RAD + 1, 2 * DM])
        c.wa_row = sb("wa_row", [P, DM])
        c.wc_row = sb("wc_row", [P, DM])
        c.w_out1 = sb("w_out1", [P, D + 1])
        c.m_ext = sb("m_ext", [P, 2, D + 1])
        c.b_ext = sb("b_ext", [P, D + 1])
        c.src_col = sb("src_col", [P, TILES], I32)
        c.dst_col = sb("dst_col", [P, TILES], I32)
        c.last_col = sb("last_col", [P, TILES], I32)
        c.own_pos = sb("own_pos", [P, TILES], I32)
        c.last_pos = sb("last_pos", [P, TILES], I32)
        c.src_pos = sb("src_pos", [P, TILES], I32)
        c.row_ids = sb("row_ids", [P, TILES])
        c.cut = sb("cut", [TILES, 2, H, EDGES])
        c.open_ = sb("open_", [TILES, 2, EDGES])
        c.whole = sb("whole", [H, 2, TILES])
        c.pos_table = nc.dram_tensor("pos_table", (N, 1), I32, kind="Internal").ap()
        c.col_ids = nc.dram_tensor("col_ids", (TILES, P), F32, kind="Internal").ap()
        c.rows = nc.dram_tensor("rows", (2 * ROWS, D), F32, kind="Internal").ap()

        c.weights = sb("weights", [P, TILES, H])
        c.scores = sb("scores", [P, TILES, H])
        setup(nc, c, io)
        with ExitStack() as scratch:
            scratch_for_max(nc, c, scratch)
            index_pass(nc, c, io)
            position_pass(nc, c)
        c.store = sb("store", [P, TILES, HP])
        score_pass(nc, c, io, out)
        clear_semaphores(nc, c)
        weights_pass(nc, c, lambda h: c.store[:, :, D + h], True, c.weights[:, :, :])
        gather_pass(nc, c, io, out)
        clear_semaphores(nc, c)
        message_pass(nc, c, io, out)
        weights_pass(nc, c, lambda h: c.scores[:, :, h], False, c.weights[:, :, :])
        clear_semaphores(nc, c)
        out_pass(nc, c, out)


INS = ["x", "src", "dst", "edge_attr_64", "L0_gnn_W", "L0_gnn_attn", "L0_gnn_W_out", "L1_gnn_W_edge", "L1_gnn_W_n2m",
       "L1_gnn_Wq", "L1_gnn_bq", "L1_gnn_Wk", "L1_gnn_bk", "L1_gnn_Wv", "L1_gnn_bv", "L1_gnn_We", "L1_gnn_Wskip",
       "L1_gnn_bskip", "L1_gnn_Wbeta", "L1_gnn_W_m2n"]


def kernel(**inputs):
    import numpy as np
    import concourse.bacc as bacc
    from concourse.bass_utils import run_bass_kernel_spmd

    nc = bacc.Bacc("TRN2", target_bir_lowering=False, num_devices=1)
    arrays, io = {}, {}
    for name in INS:
        a = np.ascontiguousarray(inputs[name])
        arrays[f"in_{name}"] = a
        io[name] = nc.dram_tensor(f"in_{name}", a.shape, mybir.dt.from_np(a.dtype), kind="ExternalInput").ap()
    out = nc.dram_tensor("out", (N, D), F32, kind="ExternalOutput").ap()
    build(nc, io, out)
    return run_bass_kernel_spmd(nc, [arrays], core_ids=[0]).results[0]["out"]
```

```python
from contextlib import ExitStack

import concourse.bass as bass
from concourse import mybir

ALU = mybir.AluOpType
ACT = mybir.ActivationFunctionType
AX = mybir.AxisListType
F32 = mybir.dt.float32
I32 = mybir.dt.int32

P = 128
N, D = 50000, 256
E = 12500
H, HD = 4, 64
DM, RAD = 128, 64
CH = DM // H
EDGES, TILES = 125, 100
G = 5
QS = TILES // G
ROWS = TILES * P
HP = D + H
VP = DM + H
NT = 2
NROWS = NT * P
NFULL = N // NROWS
NSTEPS = NFULL + 1
BIG = 1.0e38
SKIP = 1 << 17
EPS = 1e-5
RSQRT_SEED = 0x5F3759DF


def at_least(eng, sem, value, turn=None):
    if isinstance(value, int):
        if value > 0:
            eng.wait_ge(sem, value)
    else:
        eng.wait_ge(sem, value)
        if turn is not None:
            eng.sem_inc(turn, 1)


class Own:

    def __init__(self, eng, sem, turn):
        self.eng, self.sem, self.turn, self.base, self.n = eng, sem, turn, 0, 0

    def __call__(self, ins):
        self.n += 1
        ins.then_inc(self.sem, 1)

    def upto(self, n, turn=False):
        at_least(self.eng, self.sem, self.base + n, self.turn if turn else None)

    def done(self, turn=False):
        at_least(self.eng, self.sem, self.base + self.n, self.turn if turn else None)

    def loop(self, i, per):
        self.at, self.per = self.n, per
        self.base = i * per

    def looped(self, times):
        assert self.n - self.at == self.per, (self.n - self.at, self.per)
        self.n, self.base = self.at + self.per * times, 0


def clear_semaphores(nc, c):
    with nc.Block() as block:
        @block.gpsimd
        def _(pool):
            pool.sem_clear(range(min(c.semaphores), max(c.semaphores) + 1))


class Part:

    def __init__(self, total, unroll, lag, ahead=0, rounds=1, per=1):
        self.total, self.unroll, self.lag, self.ahead, self.rounds, self.per = total, unroll, lag, ahead, rounds, per
        self.peeled = unroll * rounds
        self.loops = (total - self.peeled - ahead) // (unroll * per)


def blend(lists):
    spread = [((2 * k + 1) / (2 * len(x)), n, entry) for n, x in enumerate(lists) for k, entry in enumerate(x)]
    return [(n, entry) for _, n, entry in sorted(spread, key=lambda e: e[:2])]


def steps(eng, own, per, parts, emits, cuts=()):
    times = min(p.loops for p in parts)
    split = isinstance(per, (list, tuple))
    pers, emitted = (per, emits) if split else ([per], [emits])

    def perform(order, emit):
        for n, args in order:
            for _ in emit[n](*args) or ():
                pass

    def straight(entries, emit):
        perform([(n, (s, s % parts[n].unroll, s // parts[n].unroll)) for n, s in blend(entries)], emit)

    straight([list(range(p.peeled)) for p in parts], emitted[0])
    bounds = [0, *cuts, times]
    for lo, hi, count, emit in zip(bounds[:-1], bounds[1:], pers, emitted):
        with eng.Fori(lo, hi) as i:
            own.loop(i - lo if lo else i, count)
            order = []
            for n, j in blend([list(range(p.unroll * p.per)) for p in parts]):
                p = parts[n]
                q = p.per * i + (p.rounds + j // p.unroll)
                order.append((n, (p.unroll * p.per * i + (p.peeled + j), j % p.unroll, q)))
            perform(order, emit)
            own.looped(hi - lo)
    straight([list(range(p.peeled + times * p.unroll * p.per, p.total + p.lag)) for p in parts], emitted[-1])


def weave(*tasks):
    tasks = [t for t in tasks if t is not None]
    while tasks:
        for t in list(tasks):
            try:
                next(t)
                yield
            except StopIteration:
                tasks.remove(t)


def idle(s, j, q):
    pass


def live(s, lag, total):
    return not isinstance(s, int) or 0 <= s - lag < total


def arrivals(j, q, unroll, behind, unit=16):
    rounds = q + (1 + (j - behind) // unroll)
    return unit * (max(0, rounds) if isinstance(q, int) else rounds)


def rsqrt(own, y, v, t):
    dve = own.eng
    own(dve.tensor_scalar(t.bitcast(I32), v.bitcast(I32), 1, None, ALU.logical_shift_right))
    n = own.n
    yield
    own.upto(n)
    own(dve.tensor_scalar(y.bitcast(I32), t.bitcast(I32), -1.0, float(RSQRT_SEED), ALU.mult, ALU.add))
    for _ in range(3):
        n = own.n
        yield
        own.upto(n)
        own(dve.tensor_tensor(t, y, y, ALU.mult))
        n = own.n
        yield
        own.upto(n)
        own(dve.scalar_tensor_tensor(out=t, in0=t, scalar=-0.5, in1=v, op0=ALU.mult, op1=ALU.mult))
        n = own.n
        yield
        own.upto(n)
        own(dve.scalar_tensor_tensor(out=y, in0=t, scalar=1.5, in1=y, op0=ALU.add, op1=ALU.mult))
    n = own.n
    yield
    own.upto(n)


class Core:

    def __init__(self):
        self.passes = 0
        self.semaphores = set()

    def name(self, name):
        return f"{name}_{self.passes}"

    def semaphore(self, nc, ctx, name):
        sem = ctx.enter_context(nc.semaphore(self.name(name)))
        self.semaphores.add(sem.num)
        return sem


def setup(nc, c, io):
    c.passes += 1
    with ExitStack() as ctx:
        def sb(name, shape, dt=F32):
            return ctx.enter_context(nc.sbuf_tensor(c.name(name), shape, dt))

        def sem(name):
            return c.semaphore(nc, ctx, name)

        w_n2m = sb("w_n2m", [P, D])
        w_sq = sb("w_sq", [P, 4, DM])
        w_sqT = sb("w_sqT", [P, 4, DM])
        w_m2n = sb("w_m2n", [P, 2, DM])
        w_skipn = sb("w_skipn", [P, D])
        w_edge = sb("w_edge", [RAD, RAD])
        w_e = sb("w_e", [P, RAD])
        w_eT = sb("w_eT", [RAD, DM])
        attn = sb("attn", [P, H, 2 * HD])
        prod = sb("prod", [P, 2, H, HD])
        beta = sb("beta", [P, 3])
        wb = sb("wb", [P, 1])
        bs_cols = sb("bs_cols", [P, P])
        zero = sb("zero", [P, P])
        mean_w = sb("mean_w", [P, P])
        ldd = sem("ldd")
        ident_ready = sem("ident_ready")
        pool_done = sem("pool_done")
        pe_done = sem("pe_done")
        dve_done = sem("dve_done")
        ps = c.psum

        with nc.Block() as block:
            @block.sync
            def _(sp):
                with nc.allow_non_contiguous_dma(reason="a few short weight rows"):
                    sp.dma_start(w_n2m[:, :], io["L1_gnn_W_n2m"]).then_inc(ldd, 16)
                    for k, name in enumerate(("Wq", "Wk", "Wv", "Wskip")):
                        sp.dma_start(w_sq[:, k, :], io["L1_gnn_" + name]).then_inc(ldd, 16)
                    for k in range(2):
                        sp.dma_start(w_m2n[:, k, :], io["L1_gnn_W_m2n"][k * P:(k + 1) * P, :]).then_inc(ldd, 16)
                        sp.dma_start(c.wo[:, k, :], io["L0_gnn_W_out"][k * P:(k + 1) * P, :]).then_inc(ldd, 16)
                        sp.dma_start(c.wh[:, k, 0:D].rearrange("p (h d) -> p h d", h=H),
                                     io["L0_gnn_W"][:, k * P:(k + 1) * P, :].rearrange("h i d -> i h d")).then_inc(ldd, 16)
                    sp.dma_start(w_edge[:, :], io["L1_gnn_W_edge"]).then_inc(ldd, 16)
                    sp.dma_start(w_e[:, :], io["L1_gnn_We"]).then_inc(ldd, 16)
                    sp.dma_start(attn[:, :, :].rearrange("p h d -> p (h d)"),
                                 io["L0_gnn_attn"].rearrange("(a h) d -> a (h d)", a=1).to_broadcast([P, H * 2 * HD])).then_inc(ldd, 16)
                    for k in range(3):
                        sp.dma_start(beta[:, k:k + 1], io["L1_gnn_Wbeta"][:, k * DM:(k + 1) * DM].rearrange("a d -> d a")).then_inc(ldd, 16)

            @block.scalar
            def _(act):
                with nc.allow_non_contiguous_dma(reason="one bias column"):
                    act.dma_start(c.bq_xr[:, 0:DM], io["L1_gnn_bq"].rearrange("(a d) -> a d", a=1).to_broadcast([P, DM])).then_inc(ldd, 16)
                    act.dma_start(c.bq_xr[:, DM:2 * DM], io["L1_gnn_bskip"].rearrange("(a d) -> a d", a=1).to_broadcast([P, DM])).then_inc(ldd, 16)
                    act.dma_start(c.we2[RAD:RAD + 1, 0:DM], io["L1_gnn_bk"].rearrange("(a d) -> a d", a=1)).then_inc(ldd, 16)
                    act.dma_start(c.we2[RAD:RAD + 1, DM:2 * DM], io["L1_gnn_bv"].rearrange("(a d) -> a d", a=1)).then_inc(ldd, 16)
                    act.dma_start(c.wa_row[:, :], io["L1_gnn_Wbeta"][:, 0:DM].to_broadcast([P, DM])).then_inc(ldd, 16)
                    act.dma_start(c.wc_row[:, :], io["L1_gnn_Wbeta"][:, 2 * DM:3 * DM].to_broadcast([P, DM])).then_inc(ldd, 16)
                    act.dma_start(bs_cols[:, 0:1], io["L1_gnn_bskip"].rearrange("(d a) -> d a", a=1)).then_inc(ldd, 16)

            loads = 16 * (1 + 4 + 6 + 2 + 1 + 3 + 7)

            @block.gpsimd
            def _(pool):
                own = Own(pool, pool_done, None)
                own(pool.memset(c.ident[:, :], 0.0))
                own(pool.memset(zero[:, :], 0.0))
                own(pool.memset(mean_w[:, :], 1.0 / D))
                own.done()
                pool.affine_select(out=c.ident[:, :], in_=c.ident[:, :], compare_op=ALU.not_equal, fill=1.0,
                                   base=0, pattern=[[-1, P]], channel_multiplier=1).then_inc(ident_ready, 1)

            def bank(b, rows, cols):
                return ps[0:rows, b, 0:cols]

            @block.tensor
            def _(pe):
                pe.wait_ge(ident_ready, 1)
                pe.wait_ge(ldd, loads)
                for k in range(4):
                    pe.transpose(ps[:, 0, k * P:(k + 1) * P], w_sq[:, k, :], c.ident[:, :])
                for k in range(2):
                    pe.transpose(ps[:, 1, k * P:(k + 1) * P], w_m2n[:, k, :], c.ident[:, :])
                pe.transpose(ps[0:RAD, 2, 0:P], w_e[:, :], c.ident[:, :]).then_inc(pe_done, 1)
                pe.wait_ge(dve_done, 7)
                for k in range(2):
                    lhs = w_n2m[:, k * P:(k + 1) * P]
                    for n, w in enumerate((0, 3)):
                        pe.matmul(ps[:, 3, n * DM:(n + 1) * DM] if k == 0 else ps[:, 4, n * DM:(n + 1) * DM], lhs, w_sqT[:, w, :], start=True, stop=True)
                    for n, w in enumerate((1, 2)):
                        pe.matmul(ps[:, 5, n * DM:(n + 1) * DM] if k == 0 else ps[:, 6, n * DM:(n + 1) * DM], lhs, w_sqT[:, w, :], start=True, stop=True)
                pe.matmul(ps[:, 7, 0:D], w_sqT[:, 3, :], w_n2m[:, :], start=True, stop=True)
                pe.matmul(bank(2, RAD, DM), w_edge[:, :], w_eT[:, :], start=True, stop=True).then_inc(pe_done, 1)
                pe.wait_ge(dve_done, 14)
                for k in range(2):
                    pe.matmul(ps[:, 3 + k, 0:D + 1], w_skipn[:, k * P:(k + 1) * P], c.w_out1[:, :], start=True, stop=True)
                    pe.matmul(ps[:, 5 + k, 0:1], w_skipn[:, k * P:(k + 1) * P], wb[:, :], start=True, stop=True)
                pe.matmul(ps[:, 7, 0:D + 1], bs_cols[:, :], c.w_out1[:, :], start=True, stop=True).then_inc(pe_done, 1)
                pe.wait_ge(dve_done, 19)
                for k in range(2):
                    pe.matmul(ps[:, 0, 0:D + 1], mean_w[:, :], c.m_ext[:, k, :], start=(k == 0), stop=(k == 1))
                for k in range(2):
                    last = pe.matmul(ps[:, 1, 0:2 * DM + 1], mean_w[:, :], c.w_qs[:, k, :], start=(k == 0), stop=(k == 1))
                last.then_inc(pe_done, 1)

            @block.vector
            def _(dve):
                own = Own(dve, dve_done, None)
                dve.wait_ge(ldd, loads)
                dve.wait_ge(pool_done, 3)
                own(dve.tensor_tensor(wb[:, :], beta[:, 1:2], beta[:, 2:3], ALU.subtract))
                own(dve.tensor_tensor(c.wa_row[:, :], c.wa_row[:, :], c.wc_row[:, :], ALU.add))
                dve.wait_ge(pe_done, 1)
                own(dve.tensor_copy(w_sqT[:, :, :].rearrange("p k d -> p (k d)"), ps[:, 0, 0:512]))
                own(dve.tensor_copy(c.w_out1[:, 0:D], ps[:, 1, 0:D]))
                own(dve.tensor_copy(w_eT[:, :], ps[0:RAD, 2, 0:DM]))
                own.done()
                own(dve.tensor_copy(c.w_out1[:, D:D + 1], wb[:, :]))
                own(dve.tensor_scalar(bs_cols[:, 1:P], zero[:, 1:P], bs_cols[:, 0:1], None, ALU.add))
                dve.wait_ge(pe_done, 2)
                for k in range(2):
                    own(dve.tensor_copy(c.w_qs[:, k, 0:2 * DM], ps[:, 3 + k, 0:2 * DM]))
                    own(dve.tensor_copy(c.w_kv[:, k, :], ps[:, 5 + k, 0:2 * DM]))
                own(dve.tensor_copy(w_skipn[:, :], ps[:, 7, 0:D]))
                own(dve.tensor_copy(c.we2[0:RAD, 0:DM], ps[0:RAD, 2, 0:DM]))
                own(dve.tensor_copy(c.we2[0:RAD, DM:2 * DM], ps[0:RAD, 2, 0:DM]))
                dve.wait_ge(pe_done, 3)
                for k in range(2):
                    own(dve.tensor_copy(c.m_ext[:, k, :], ps[:, 3 + k, 0:D + 1]))
                    own(dve.tensor_copy(c.w_qs[:, k, 2 * DM:2 * DM + 1], ps[:, 5 + k, 0:1]))
                own(dve.tensor_copy(c.b_ext[:, :], ps[:, 7, 0:D + 1]))
                own.done()
                own(dve.tensor_copy(c.bq_xr[:, 2 * DM:2 * DM + 1], c.b_ext[:, D:D + 1]))
                dve.wait_ge(pe_done, 4)
                own.done()
                own(dve.scalar_tensor_tensor(out=c.b_ext[:, :], in0=c.b_ext[:, :], scalar=1.0 / D, in1=ps[:, 0, 0:D + 1], op0=ALU.mult, op1=ALU.subtract))
                own(dve.scalar_tensor_tensor(out=c.bq_xr[:, :], in0=c.bq_xr[:, :], scalar=1.0 / D, in1=ps[:, 1, 0:2 * DM + 1], op0=ALU.mult, op1=ALU.subtract))
                own.done()
                for k in range(2):
                    own(dve.tensor_tensor(c.m_ext[:, k, :], c.m_ext[:, k, :], c.b_ext[:, :], ALU.add))
                    own(dve.tensor_tensor(c.w_qs[:, k, :], c.w_qs[:, k, :], c.bq_xr[:, :], ALU.add))
                for half, out in ((0, c.wh[:, :, D:HP]), (1, c.w_ad[:, :, :])):
                    for k in range(2):
                        own.done()
                        own(dve.tensor_tensor(prod[:, k, :, :], c.wh[:, k, 0:D].rearrange("p (h d) -> p h d", h=H),
                                              attn[:, :, half * HD:(half + 1) * HD], ALU.mult))
                    own.done()
                    for k in range(2):
                        own(dve.tensor_reduce(out[:, k, :], prod[:, k, :, :], AX.X, ALU.add))
                own.done()


def index_pass(nc, c, io):
    c.passes += 1
    dst, src = io["dst"], io["src"]
    rows = dst.rearrange("(t e) -> t e", e=EDGES)
    with ExitStack() as ctx:
        def sb(name, shape, dt=F32):
            return ctx.enter_context(nc.sbuf_tensor(c.name(name), shape, dt))

        def sem(name):
            return c.semaphore(nc, ctx, name)

        dsti = sb("dsti", [TILES, EDGES], I32)
        srci = sb("srci", [TILES, EDGES], I32)
        previ = sb("previ", [TILES, 1], I32)
        nexti = sb("nexti", [TILES, 1], I32)
        edgei = sb("edgei", [H, 2, TILES], I32)
        edgef = sb("edgef", [H, 2, TILES])
        dstf = sb("dstf", [TILES, EDGES])
        prevf = sb("prevf", [TILES, 1])
        nextf = sb("nextf", [TILES, 1])
        row = sb("row", [TILES, 5, P])
        islast = sb("islast", [TILES, EDGES])
        posi = sb("posi", [TILES, EDGES], I32)
        posf = sb("posf", [TILES, EDGES])
        fill = sb("fill", [80, N // 80], I32)
        idx_loads = sem("idx_loads")
        own_sem = sem("own_sem")
        minus = sem("minus")
        table = sem("table")
        turned = sem("turned")
        pool_ready = sem("pool_ready")
        LD = 16 * 6
        with nc.Block() as block:
            @block.sync
            def _(sp):
                with nc.allow_non_contiguous_dma(reason="400 first and last dst of the tiles, once"):
                    sp.dma_start(dsti[:, :], rows).then_inc(idx_loads, 16)
                    sp.dma_start(srci[:, :], src.rearrange("(t e) -> t e", e=EDGES)).then_inc(idx_loads, 16)
                    sp.dma_start(edgei[:, 0, :], dst.rearrange("(a t e) -> a t e", a=1, e=EDGES)[:, :, 0].to_broadcast([H, TILES])).then_inc(idx_loads, 16)
                    sp.dma_start(edgei[:, 1, :], dst.rearrange("(a t e) -> a t e", a=1, e=EDGES)[:, :, EDGES - 1].to_broadcast([H, TILES])).then_inc(idx_loads, 16)
                    sp.wait_ge(minus, 1)
                    sp.dma_start(previ[1:TILES, :], rows[0:TILES - 1, EDGES - 1:EDGES]).then_inc(idx_loads, 16)
                    sp.dma_start(nexti[0:TILES - 1, :], rows[1:TILES, 0:1]).then_inc(idx_loads, 16)
                sp.wait_ge(pool_ready, 1)
                sp.dma_start(c.pos_table.rearrange("(p n) a -> p (n a)", p=80), fill[:, :]).then_inc(table, 16)
                sp.wait_ge(own_sem, 17)
                sp.dma_start(c.col_ids, row[:, 4, :]).then_inc(table, 16)
                sp.wait_ge(table, 32)

            @block.gpsimd
            def _(pool):
                pool.iota(posi[:, :], [[1, EDGES]], base=1, channel_multiplier=P).then_inc(pool_ready, 1)
                pool.iota(c.own_pos[:, :], [[P, TILES]], base=0, channel_multiplier=1).then_inc(pool_ready, 1)

            @block.vector
            def _(dve):
                own = Own(dve, own_sem, None)
                own(dve.memset(previ[:, :], -1))
                own(dve.memset(nexti[:, :], -1))
                own(dve.memset(row[:, 0:2, :], 0.0))
                own(dve.memset(row[:, 2, :], float(SKIP)))
                own(dve.memset(row[:, 3, :], -2.0))
                own(dve.memset(row[:, 4, :], -3.0))
                dve.memset(fill[:, :], SKIP).then_inc(minus, 1)
                dve.wait_ge(idx_loads, LD)
                dve.wait_ge(minus, 1)
                dve.wait_ge(pool_ready, 2)
                for out, into in ((dstf, dsti), (prevf, previ), (nextf, nexti), (posf, posi)):
                    own(dve.tensor_copy(out[:, :], into[:, :]))
                own(dve.tensor_copy(edgef[:, :, :], edgei[:, :, :]))
                own(dve.tensor_copy(row[:, 0, 1:1 + EDGES], srci[:, :]))
                own(dve.tensor_copy(row[:, 1, 1:1 + EDGES], dsti[:, :]))
                own.done()
                own(dve.tensor_copy(row[:, 3, 0:1], prevf[:, :]))
                own(dve.tensor_copy(row[:, 3, 1:1 + EDGES], dstf[:, :]))
                own(dve.tensor_copy(row[:, 4, 0:1], dstf[:, EDGES - 1:EDGES]))
                own(dve.tensor_copy(row[:, 4, 1:1 + EDGES], dstf[:, :]))
                own(dve.tensor_tensor(islast[:, 0:EDGES - 1], dstf[:, 0:EDGES - 1], dstf[:, 1:EDGES], ALU.not_equal))
                own(dve.tensor_tensor(islast[:, EDGES - 1:EDGES], dstf[:, EDGES - 1:EDGES], nextf[:, :], ALU.not_equal))
                own.done()
                own(dve.memset(c.cut[:, :, :, :], -BIG))
                own.done()
                for h in range(H):
                    own(dve.tensor_scalar(c.cut[:, 0, h, 1:EDGES], islast[:, 0:EDGES - 1], -BIG, None, ALU.mult))
                    own(dve.tensor_scalar(c.cut[:, 1, h, 0:EDGES - 1], islast[:, 0:EDGES - 1], -BIG, None, ALU.mult))
                for k, end in ((0, prevf), (1, nextf)):
                    own(dve.tensor_scalar(c.open_[:, k, :], dstf[:, :], end[:, :], None, ALU.is_equal))
                own.done()
                own(dve.tensor_scalar(c.open_[:, :, :], c.open_[:, :, :], -1.0, BIG, ALU.add, ALU.mult))
                own(dve.memset(c.whole[:, :, :], -BIG))
                own.done()
                own(dve.tensor_tensor(c.whole[:, 0, 1:TILES], edgef[:, 1, 0:TILES - 1], edgef[:, 1, 1:TILES], ALU.is_equal))
                own(dve.tensor_tensor(c.whole[:, 1, 0:TILES - 1], edgef[:, 0, 0:TILES - 1], edgef[:, 0, 1:TILES], ALU.is_equal))
                own.done()
                own(dve.tensor_scalar(c.whole[:, 0, 1:TILES], c.whole[:, 0, 1:TILES], -1.0, BIG, ALU.add, ALU.mult))
                own(dve.tensor_scalar(c.whole[:, 1, 0:TILES - 1], c.whole[:, 1, 0:TILES - 1], -1.0, BIG, ALU.add, ALU.mult))
                own(dve.tensor_scalar(row[:, 2, 1:1 + EDGES], dstf[:, :], -float(SKIP), None, ALU.add))
                own.done()
                own(dve.tensor_tensor(row[:, 2, 1:1 + EDGES], row[:, 2, 1:1 + EDGES], islast[:, :], ALU.mult))
                own.done()
                own(dve.tensor_scalar(row[:, 2, 1:1 + EDGES], row[:, 2, 1:1 + EDGES], float(SKIP), None, ALU.add))
                for h in range(H):
                    own(dve.tensor_copy(c.val[:, h, :], posf[:, :]))
                own.done()

            @block.tensor
            def _(pe):
                pe.wait_ge(own_sem, 43)
                for k in range(4):
                    last = pe.transpose(c.psum[:, k // 2, (k % 2) * 256:(k % 2) * 256 + TILES], row[:, k, :], c.ident[0:TILES, 0:TILES])
                last.then_inc(turned, 1)

            @block.scalar
            def _(act):
                act.wait_ge(turned, 1)
                for k, out in enumerate((c.src_col, c.dst_col, c.last_col, c.row_ids)):
                    act.activation(out[:, :], c.psum[:, k // 2, (k % 2) * 256:(k % 2) * 256 + TILES], ACT.Copy).then_inc(turned, 1)
                act.wait_ge(turned, 5)


def scratch_for_max(nc, c, ctx):
    def sb(name, shape):
        return ctx.enter_context(nc.sbuf_tensor(c.name(name), shape, F32))

    c.val, c.fwd, c.bwd, c.top = (sb(name, [TILES, H, EDGES]) for name in ("val", "fwd", "bwd", "top"))
    c.ends = sb("ends", [TILES, 2, H])
    c.run = sb("run", [H, 2, TILES])
    c.run2 = sb("run2", [H, 2, TILES + 1])
    c.carried = sb("carried", [TILES, 2, H])


def max_of_segments(nc, c, dve, own, asks, answers, n):
    flat = "p h e -> p (h e)"
    val, fwd, bwd = (x[:, :, :].rearrange(flat) for x in (c.val, c.fwd, c.bwd))
    own(dve.tensor_tensor_scan(fwd, c.cut[:, 0, :, :].rearrange(flat), val, -BIG, ALU.add, ALU.max))
    own(dve.tensor_tensor_scan(bwd[:, ::-1], c.cut[:, 1, :, :].rearrange(flat)[:, ::-1], val[:, ::-1], -BIG, ALU.add, ALU.max))
    own.done()
    own(dve.tensor_copy(c.ends[:, 0, :], c.fwd[:, :, EDGES - 1]))
    own(dve.tensor_copy(c.ends[:, 1, :], c.bwd[:, :, 0]))
    own.done()
    own(dve.tensor_tensor(c.top[:, :, :], c.fwd[:, :, :], c.bwd[:, :, :], ALU.max))
    own.done()
    dve.sem_inc(asks, 1)
    dve.wait_ge(answers, 2 * n + 1)
    own(dve.tensor_copy(c.run[:, 0, :], c.psum[0:H, 0, 0:TILES]))
    own(dve.tensor_copy(c.run[:, 1, :], c.psum[0:H, 0, 256:256 + TILES]))
    own.done()
    own(dve.tensor_tensor_scan(c.run2[:, 0, 1:TILES + 1], c.whole[:, 0, :], c.run[:, 0, :], -BIG, ALU.add, ALU.max))
    own(dve.tensor_tensor_scan(c.run2[:, 1, 0:TILES][:, ::-1], c.whole[:, 1, :][:, ::-1], c.run[:, 1, :][:, ::-1], -BIG, ALU.add, ALU.max))
    own(dve.memset(c.run2[:, 0, 0:1], -BIG))
    own(dve.memset(c.run2[:, 1, TILES:TILES + 1], -BIG))
    own.done()
    dve.sem_inc(asks, 1)
    dve.wait_ge(answers, 2 * n + 2)
    own(dve.tensor_copy(c.carried[:, 0, :], c.psum[0:TILES, 1, 0:H]))
    own(dve.tensor_copy(c.carried[:, 1, :], c.psum[0:TILES, 1, 256:256 + H]))
    for k in range(2):
        own.done()
        for h in range(H):
            own(dve.scalar_tensor_tensor(out=c.top[:, h, :], in0=c.open_[:, k, :], scalar=c.carried[:, k, h:h + 1],
                                         in1=c.top[:, h, :], op0=ALU.add, op1=ALU.max))
    own.done()


def turns_for_max(pe, c, asks, answers, n):
    pe.wait_ge(asks, 2 * n + 1)
    for k in range(2):
        last = pe.transpose(c.psum[0:H, 0, 256 * k:256 * k + TILES], c.ends[:, k, :], c.ident[0:TILES, 0:TILES])
    last.then_inc(answers, 1)
    pe.wait_ge(asks, 2 * n + 2)
    pe.transpose(c.psum[0:TILES, 1, 0:H], c.run2[:, 0, 0:TILES], c.ident[0:H, 0:H])
    pe.transpose(c.psum[0:TILES, 1, 256:256 + H], c.run2[:, 1, 1:TILES + 1], c.ident[0:H, 0:H]).then_inc(answers, 1)


def position_pass(nc, c):
    c.passes += 1
    with ExitStack() as ctx:
        own_sem, asks, answers, turned, ready = (c.semaphore(nc, ctx, n) for n in ("own_sem", "asks", "answers", "turned", "ready"))
        padded = ctx.enter_context(nc.sbuf_tensor(c.name("padded"), [TILES, P], F32))
        with nc.Block() as block:
            @block.vector
            def _(dve):
                own = Own(dve, own_sem, None)
                max_of_segments(nc, c, dve, own, asks, answers, 0)
                own(dve.memset(padded[:, :], 0.0))
                own.done()
                dve.tensor_copy(padded[:, 1:1 + EDGES], c.top[:, 0, :]).then_inc(ready, 1)

            @block.tensor
            def _(pe):
                turns_for_max(pe, c, asks, answers, 0)
                pe.wait_ge(ready, 1)
                pe.transpose(c.psum[:, 2, 0:TILES], padded[:, :], c.ident[0:TILES, 0:TILES]).then_inc(turned, 1)

            @block.scalar
            def _(act):
                act.wait_ge(turned, 1)
                act.activation(c.last_pos[:, :], c.psum[:, 2, 0:TILES], ACT.Copy).then_inc(ready, 1)
                act.wait_ge(ready, 2)


def weights_pass(nc, c, score_of, leaky, out):
    c.passes += 1
    with ExitStack() as ctx:
        own_sem, asks, answers, turned, ready, back = (c.semaphore(nc, ctx, n) for n in ("own_sem", "asks", "answers", "turned", "ready", "back"))
        scratch_for_max(nc, c, ctx)
        raw = ctx.enter_context(nc.sbuf_tensor(c.name("raw"), [TILES, H, EDGES], F32))
        weights = ctx.enter_context(nc.sbuf_tensor(c.name("weights"), [TILES, H, P], F32))
        with nc.Block() as block:
            @block.tensor
            def _(pe):
                for h in range(H):
                    last = pe.transpose(c.psum[0:TILES, 3, h * P:(h + 1) * P], score_of(h), c.ident[:, :])
                last.then_inc(turned, 1)
                turns_for_max(pe, c, asks, answers, 0)
                pe.wait_ge(ready, 2)
                for h in range(H):
                    last = pe.transpose(c.psum[:, 4, h * P:h * P + TILES], weights[:, h, :], c.ident[0:TILES, 0:TILES])
                last.then_inc(back, 1)

            @block.vector
            def _(dve):
                own = Own(dve, own_sem, None)
                dve.wait_ge(turned, 1)
                scores = c.psum[0:TILES, 3, :].rearrange("p (h e) -> p h e", h=H)[:, :, 1:1 + EDGES]
                own(dve.tensor_copy(raw[:, :, :], scores))
                own(dve.memset(weights[:, :, :], 0.0))
                own.done()
                if leaky:
                    own(dve.scalar_tensor_tensor(out=c.val[:, :, :].rearrange("p h e -> p (h e)"), in0=raw[:, :, :].rearrange("p h e -> p (h e)"), scalar=0.2,
                                                 in1=raw[:, :, :].rearrange("p h e -> p (h e)"), op0=ALU.mult, op1=ALU.max))
                else:
                    own(dve.tensor_scalar(c.val[:, :, :], raw[:, :, :], 1.0 / float(CH) ** 0.5, None, ALU.mult))
                own.done()
                max_of_segments(nc, c, dve, own, asks, answers, 0)
                own(dve.tensor_tensor(raw[:, :, :], c.val[:, :, :], c.top[:, :, :], ALU.subtract))
                own.done()
                dve.tensor_scalar(raw[:, :, :], raw[:, :, :], 20.0 if leaky else BIG, None, ALU.min).then_inc(ready, 1)

            @block.scalar
            def _(act):
                act.wait_ge(ready, 1)
                act.activation(weights[:, :, 1:1 + EDGES], raw[:, :, :], ACT.Exp).then_inc(ready, 1)
                act.wait_ge(back, 1)
                act.activation(out.rearrange("p t h -> p h t"), c.psum[:, 4, :].rearrange("p (h t) -> p h t", h=H)[:, :, 0:TILES], ACT.Copy).then_inc(ready, 1)
                act.wait_ge(ready, 3)


NODE_PARTS = (80, 80, NSTEPS - 160)


class NodePart:
    U = 8
    LAG = 6
    DVE = 8 * (2 * NT + (NT - 1) + 2 * NT + 1 + 11 + 1)

    def __init__(self, nc, c, ctx, x, out, first, count):
        U = self.U
        self.nc, self.c, self.x, self.out, self.first = nc, c, x, out, first
        self.xv = x[0:NFULL * NROWS, :].rearrange("(s p j) d -> s p (j d)", p=P, j=NT)
        self.ov = out[0:NFULL * NROWS, :].rearrange("(s p j) d -> s p (j d)", p=P, j=NT)
        self.part = Part(count, U, self.LAG, 2)

        def sb(name, shape, dt=F32):
            return ctx.enter_context(nc.sbuf_tensor(c.name("node_" + name), shape, dt))

        def sem(name):
            return c.semaphore(nc, ctx, "node_" + name)

        self.X = sb("X", [P, U, NT, D])
        self.Y = sb("Y", [P, 2, NT, D])
        self.XT = sb("XT", [P, 2, NT * D])
        self.st = sb("st", [P, 2, NT, 6])
        self.mv = sb("mv", [P, 2, 2, NT, 2])
        self.vv = sb("vv", [P, 2, NT])
        self.r = sb("r", [P, 4, 2, NT])
        self.nm = sb("nm", [P, 4, 2, NT])
        self.be = sb("be", [P, 4, NT])
        self.tmp = sb("tmp", [P, 2, NT])
        self.loaded = [sem(f"loaded{j}") for j in range(U)]
        self.stored = [sem(f"stored{j}") for j in range(U)]
        self.roots_ready, self.x1_ready, self.turned, self.xt_ready, self.product, self.beta_ready, self.updated, self.normed = (
            sem(n) for n in ("roots_ready", "x1_ready", "turned", "xt_ready", "product", "beta_ready", "updated", "normed"))

    def rows_of(self, view, whole, s):
        if isinstance(s, int) and s + self.first == NFULL:
            return whole[N - NROWS:N, :].rearrange("(p j) d -> p (j d)", j=NT)
        return view[bass.ds(s + self.first, 1), :, :].rearrange("s p n -> (s p) n")

    def load(self, sp, s, j):
        sp.dma_start(self.X[:, j, :, :].rearrange("p j d -> p (j d)"), self.rows_of(self.xv, self.x, s)).then_inc(self.loaded[j], 16)

    def sync_start(self, own):
        for s in range(2):
            self.load(own.eng, s, s)

    def sync(self, own):
        sp, U = own.eng, self.U

        def emit(s, j, q):
            if live(s, -2, self.part.total):
                at_least(sp, self.normed, s - U + 3, own.turn)
                self.load(sp, s + 2, (j + 2) % U)
        return emit

    def scalar(self, own):
        act, c, U, total, X = own.eng, self.c, self.U, self.part.total, self.X

        def emit(s, j, q):
            if live(s, 4, total):
                o, b = j % 4, NT * (j % 2)
                at_least(act, self.product, s - 3)
                at_least(act, self.updated, s - 7)
                act.activation(self.be[:, o, :], c.psum[:, b:b + NT, D], ACT.Sigmoid).then_inc(self.beta_ready, 1)
            if live(s, 1, total):
                o, w = (j - 1) % U, (j - 1) % 4
                at_least(act, self.roots_ready, s)
                for k in range(NT):
                    last = act.activation(X[:, o, k, :], X[:, o, k, :], ACT.Identity, bias=self.nm[:, w, 0, k:k + 1], scale=self.r[:, w, 0, k:k + 1])
                last.then_inc(self.x1_ready, 1)
            if live(s, 6, total):
                o, w = (j - 6) % U, (j - 1) % 4
                at_least(act, self.roots_ready, s)
                at_least(act, self.stored[(j - 8) % U], arrivals(j, q, U, 8))
                for k in range(NT):
                    last = act.activation(self.Y[:, j % 2, k, :], X[:, o, k, :], ACT.Identity, bias=self.nm[:, w, 1, k:k + 1], scale=self.r[:, w, 1, k:k + 1])
                last.then_inc(self.normed, 1)
            if live(s, 2, total):
                at_least(act, self.turned, s - 1)
                at_least(act, self.product, s - 3)
                act.activation(self.XT[:, j % 2, :], c.psum[:, 4, 0:NT * D], ACT.Copy).then_inc(self.xt_ready, 1)
            if live(s, 6, total):
                at_least(act, self.normed, s - 5, own.turn)
                if isinstance(s, int) and s - 6 + self.first == NFULL:
                    act.wait_ge(self.stored[(total - 2) % U], 16 * ((total - 2) // U + 1))
                act.dma_start(self.rows_of(self.ov, self.out, s - 6), self.Y[:, j % 2, :, :].rearrange("p j d -> p (j d)")).then_inc(self.stored[(j - 6) % U], 16)
        return emit

    def scalar_end(self, act):
        for j in range(self.U):
            act.wait_ge(self.stored[j], 16 * ((self.part.total - 1 - j) // self.U + 1))

    def tensor(self, own):
        pe, c, U, total, ps = own.eng, self.c, self.U, self.part.total, self.c.psum

        def emit(s, j, q):
            if live(s, 2, total):
                at_least(pe, self.x1_ready, s - 1)
                at_least(pe, self.xt_ready, s - 2)
                for k in range(NT):
                    for h in range(2):
                        last = pe.transpose(ps[:, 4, k * D + h * P:k * D + (h + 1) * P], self.X[:, (j - 2) % U, k, h * P:(h + 1) * P], c.ident[:, :])
                last.then_inc(self.turned, 1)
            if live(s, 3, total):
                at_least(pe, self.xt_ready, s - 2)
                at_least(pe, self.updated, s - 4)
                o = (j - 3) % 2
                for k in range(NT):
                    for h in range(2):
                        last = pe.matmul(ps[:, NT * o + k, 0:D + 1], self.XT[:, o, k * D + h * P:k * D + (h + 1) * P], c.m_ext[:, h, :],
                                         start=(h == 0), stop=(h == 1))
                last.then_inc(self.product, 1)
        return emit

    def vector(self, own):
        dve, c, U, total, ps = own.eng, self.c, self.U, self.part.total, self.c.psum
        X, st, mv, vv, tmp, r, nm = self.X, self.st, self.mv, self.vv, self.tmp, self.r, self.nm

        def emit(s, j, q):
            yield from weave(roots(s, j, q) if live(s, 0, total) or live(s, 5, total) else None, update(s, j, q))

        def update(s, j, q):
            w = (j + 1) % 2
            if live(s, -1, total):
                at_least(dve, self.loaded[(j + 1) % U], arrivals(j, q, U, -1))
                for k in range(NT):
                    own(dve.bn_stats(st[:, 0, k, :], X[:, (j + 1) % U, k, :]))
                    n = own.n
                    yield
            if live(s, 4, total):
                o, b = (j - 4) % U, NT * (j % 2)
                at_least(dve, self.beta_ready, s - 3)
                for k in range(NT):
                    ins = dve.scalar_tensor_tensor(out=X[:, o, k, :], in0=ps[:, b + k, 0:D], scalar=self.be[:, j % 4, k:k + 1],
                                                   in1=X[:, o, k, :], op0=ALU.mult, op1=ALU.add)
                    if k < NT - 1:
                        own(ins)
                    else:
                        ins.then_inc(self.updated, 1)
                    yield
            if live(s, -1, total):
                own.upto(n, True)
                for k in range(NT):
                    own(dve.bn_aggr(mv[:, w, 0, k, :], st[:, 0, k, :]))
                    yield
            if live(s, 4, total):
                at_least(dve, self.updated, s - 3)
                for k in range(NT):
                    own(dve.bn_stats(st[:, 1, k, :], X[:, o, k, :]))
                    n = own.n
                    yield
                own.upto(n, True)
                for k in range(NT):
                    own(dve.bn_aggr(mv[:, w, 1, k, :], st[:, 1, k, :]))
                    yield

        def roots(s, j, q):
            first, last = live(s, 0, total), live(s, 5, total)
            lo, hi = (0 if first else 1), (2 if last else 1)
            w = j % 4
            v, y, t = vv[:, lo:hi, :], r[:, w, lo:hi, :], tmp[:, lo:hi, :]
            own.done()
            own(dve.tensor_scalar(v, mv[:, j % 2, lo:hi, :, 1], EPS, None, ALU.add))
            n = own.n
            yield
            own.upto(n)
            at_least(dve, self.x1_ready, s - 2) if first else dve.wait_ge(self.normed, min(s - 8, total))
            yield from rsqrt(own, y, v, t)
            ins = dve.scalar_tensor_tensor(out=nm[:, w, lo:hi, :], in0=mv[:, j % 2, lo:hi, :, 0], scalar=-1.0, in1=y, op0=ALU.mult, op1=ALU.mult)
            if first:
                own(ins)
                n = own.n
                yield
                own.upto(n)
                ins = dve.tensor_scalar(nm[:, w, 0, :], nm[:, w, 0, :], 1.0, None, ALU.add)
            ins.then_inc(self.roots_ready, 1)
            n = s + 1
            yield
            at_least(dve, self.roots_ready, n, own.turn)
        return emit

    def vector_start(self, own):
        dve = own.eng
        dve.wait_ge(self.loaded[0], 16)
        for k in range(NT):
            own(dve.bn_stats(self.st[:, 0, k, :], self.X[:, 0, k, :]))
        own.done()
        for k in range(NT):
            own(dve.bn_aggr(self.mv[:, 0, 0, k, :], self.st[:, 0, k, :]))
        own.done()


def score_pass(nc, c, io, out):
    x, U = io["x"], 2 * G
    c.passes += 1
    with ExitStack() as ctx:
        def sb(name, shape, dt=F32):
            return ctx.enter_context(nc.sbuf_tensor(c.name(name), shape, dt))

        def sem(name):
            return c.semaphore(nc, ctx, name)

        XS = sb("XS", [P, 2, G, D])
        XD = sb("XD", [P, 2, G, D])
        ST = sb("ST", [P, 2, 2 * D])
        isrc = [sb(f"isrc{b}", [P, G], I32) for b in range(2)]
        idst = [sb(f"idst{b}", [P, G], I32) for b in range(2)]
        gathered = [sem(f"gathered{b}") for b in range(2)]
        kept = [sem(f"kept{b}") for b in range(2)]
        e_turned, st_ready, e_product, h_ready, copied, dve_own, turn_p, turn_e, turn_a, turn_d, turn_s = (
            sem(n) for n in ("e_turned", "st_ready", "e_product", "h_ready", "copied", "dve_own", "turn_p", "turn_e", "turn_a", "turn_d", "turn_s"))
        ps = c.psum
        dst_rows = c.rows[0:ROWS, :].rearrange("(q k p) d -> q p k d", k=G, p=P)
        src_rows = c.rows[ROWS:2 * ROWS, :].rearrange("(q k p) d -> q p k d", k=G, p=P)
        node = NodePart(nc, c, ctx, x, out, 0, NODE_PARTS[0])
        parts = (node.part, Part(TILES, U, 2))
        with nc.Block() as block:
            @block.gpsimd
            def _(pool):
                own = Own(pool, copied, turn_p)

                def gather(q, b):
                    own(pool.tensor_copy(isrc[b][:, :], c.src_col[:, bass.ds(G * q, G)]))
                    own(pool.tensor_copy(idst[b][:, :], c.dst_col[:, bass.ds(G * q, G)]))
                    own.done(True)
                    for k in range(G):
                        for rows, idx in ((XS, isrc), (XD, idst)):
                            pool.indirect_dma_start(out=rows[:, b, k, :], out_offset=None, in_=x,
                                                    in_offset=bass.IndirectOffsetOnAxis(ap=idx[b][:, k:k + 1], axis=0)).then_inc(gathered[b], 16)

                def emit(t, j, q):
                    if j % G == 0 and live(t, -G, TILES):
                        n, b = 2 * q + j // G, (j // G + 1) % 2
                        at_least(pool, e_turned, t, turn_p)
                        at_least(pool, kept[b], arrivals(j, q, U, G, 32), turn_p)
                        gather(n + 1, b)
                gather(0, 0)
                steps(pool, own, 4, parts, (idle, emit))

            @block.sync
            def _(sp):
                own = Own(sp, turn_s, turn_s)

                def emit(t, j, q):
                    if j % G == 0 and live(t, 0, TILES):
                        b = j // G
                        at_least(sp, gathered[b], arrivals(j, q, U, 0, 32 * G), turn_s)
                        for rows, into in ((XD, dst_rows), (XS, src_rows)):
                            sp.dma_start(into[bass.ds(2 * q + b, 1), :, :, :].rearrange("q p k d -> (q p) k d"), rows[:, b, :, :]).then_inc(kept[b], 16)
                node.sync_start(own)
                steps(sp, own, 0, parts, (node.sync(own), emit))
                for b in range(2):
                    sp.wait_ge(kept[b], 32 * QS // 2)

            @block.tensor
            def _(pe):
                own = Own(pe, turn_e, None)

                def emit(t, j, q):
                    if live(t, 0, TILES + 1):
                        at_least(pe, st_ready, t)
                    if live(t, 0, TILES):
                        if j % G == 0:
                            at_least(pe, gathered[j // G], arrivals(j, q, U, 0, 32 * G))
                        for side, rows in enumerate((XS, XD)):
                            for h in range(2):
                                last = pe.transpose(ps[:, 5, (2 * side + h) * P:(2 * side + h + 1) * P], rows[:, j // G, j % G, h * P:(h + 1) * P], c.ident[:, :])
                        last.then_inc(e_turned, 1)
                    if live(t, 1, TILES):
                        o = (j - 1) % 2
                        at_least(pe, h_ready, t - 2)
                        for h in range(2):
                            pe.matmul(ps[:, 6 + o, 0:HP], ST[:, o, h * P:(h + 1) * P], c.wh[:, h, :], start=(h == 0), stop=(h == 1))
                        for h in range(2):
                            last = pe.matmul(ps[:, 6 + o, D:HP], ST[:, o, (2 + h) * P:(3 + h) * P], c.w_ad[:, h, :], start=False, stop=(h == 1), skip_group_check=True)
                        last.then_inc(e_product, 1)
                steps(pe, own, 0, parts, (node.tensor(own), emit))

            @block.scalar
            def _(act):
                own = Own(act, turn_a, turn_a)

                def emit(t, j, q):
                    if live(t, 2, TILES):
                        at_least(act, e_product, t - 1, turn_a)
                        act.activation(c.store[:, bass.ds(t - 2, 1), 0:HP].rearrange("p a d -> p (a d)"), ps[:, 6 + j % 2, 0:HP], ACT.Copy).then_inc(h_ready, 1)
                    if live(t, 0, TILES):
                        at_least(act, e_turned, t + 1)
                        at_least(act, e_product, t - 1)
                        act.activation(ST[:, j % 2, :], ps[:, 5, :], ACT.Copy).then_inc(st_ready, 1)
                steps(act, own, 0, parts, (node.scalar(own), emit))
                act.wait_ge(h_ready, TILES)
                node.scalar_end(act)

            @block.vector
            def _(dve):
                own = Own(dve, dve_own, turn_d)

                node.vector_start(own)
                steps(dve, own, node.DVE, parts, (node.vector(own), idle))


def gather_pass(nc, c, io, out):
    U, Q = 2 * G, 4
    c.passes += 1
    with ExitStack() as ctx:
        def sb(name, shape, dt=F32):
            return ctx.enter_context(nc.sbuf_tensor(c.name(name), shape, dt))

        def sem(name):
            return c.semaphore(nc, ctx, name)

        XD = sb("XD", [P, 2, G, D])
        MB = sb("MB", [P, 2, G, P])
        S = sb("S", [P, G, P])
        MSG = sb("MSG", [P, G, HP])
        AG = sb("AG", [P, 2, D])
        AT = sb("AT", [P, 2, D])
        rec = sb("rec", [P, 2, H])
        idx = [sb(f"idx{b}", [P, G], I32) for b in range(Q)]
        val = [sb(f"val{b}", [P, G], I32) for b in range(Q)]
        moved = [sem(f"moved{b}") for b in range(Q)]
        found = [sem(f"found{b}") for b in range(Q)]
        rows_in = [sem(f"rows_in{b}") for b in range(2)]
        ids = [sem(f"ids{b}") for b in range(2)]
        kept = [sem(f"kept{b}") for b in range(2)]
        made, matched, summed, carried, scaled, e_turned, at_ready, e_product, z_ready, copied, dve_own, turn_p, turn_e, turn_a, turn_d, turn_s = (
            sem(n) for n in ("made", "matched", "summed", "carried", "scaled", "e_turned", "at_ready", "e_product", "z_ready", "copied", "dve_own",
                             "turn_p", "turn_e", "turn_a", "turn_d", "turn_s"))
        ps = c.psum
        ids_v = c.col_ids.rearrange("(q k) m -> q (k m)", k=G)
        rows_v = c.rows[0:ROWS, :].rearrange("(q k p) d -> q p k d", k=G, p=P)
        node = NodePart(nc, c, ctx, io["x"], out, NODE_PARTS[0], NODE_PARTS[1])
        tiles = Part(TILES, U, 4, 3)
        parts = (node.part, tiles)
        with nc.Block() as block:
            @block.gpsimd
            def _(pool):
                own = Own(pool, copied, turn_p)
                table = Part(2 * QS, Q, 0)
                half = (QS - Q) // Q

                def write(s, j, q):
                    at_least(pool, moved[j], arrivals(j, q, Q, Q, 16 * G), turn_p)
                    own(pool.tensor_copy(idx[j][:, :], c.last_col[:, bass.ds(G * s, G)]))
                    own(pool.tensor_copy(val[j][:, :], c.own_pos[:, bass.ds(G * s, G)]))
                    own.done(True)
                    for k in range(G):
                        pool.indirect_dma_start(out=c.pos_table, out_offset=bass.IndirectOffsetOnAxis(ap=idx[j][:, k:k + 1], axis=0),
                                                in_=val[j][:, k:k + 1], in_offset=None, bounds_check=N - 1, oob_is_err=False).then_inc(moved[j], 16)

                def read(s, j, q):
                    n = s - QS
                    if live(s, 0, 2 * QS):
                        if j == 0:
                            for b in range(Q):
                                pool.wait_ge(moved[b], 16 * G * QS // Q)
                        own(pool.tensor_copy(idx[j][:, :], c.src_col[:, bass.ds(G * n, G)]))
                        own.done(True)
                        for k in range(G):
                            pool.indirect_dma_start(out=val[j][:, k:k + 1], out_offset=None, in_=c.pos_table,
                                                    in_offset=bass.IndirectOffsetOnAxis(ap=idx[j][:, k:k + 1], axis=0)).then_inc(found[j], 16)
                    if j == Q - 1:
                        for b in range(Q):
                            at_least(pool, found[b], 16 * G * (q - QS // Q + 1), turn_p)
                            own(pool.tensor_copy(c.src_pos[:, bass.ds(G * (n - Q + 1 + b), G)], val[b][:, :]))
                        own.done(True)

                def make(t, j):
                    k = j % G
                    at_least(pool, summed, t - G + 1, turn_p)
                    w = c.weights[:, bass.ds(t, 1), :].rearrange("p a h -> p (a h)")
                    pool.tensor_tensor(MSG[:, k, 0:D].rearrange("p (h d) -> p h d", h=H),
                                       c.store[:, bass.ds(t, 1), 0:D].rearrange("p a (h d) -> p (a h) d", h=H),
                                       w.unsqueeze(2).to_broadcast([P, H, HD]), ALU.mult)
                    pool.tensor_copy(MSG[:, k, D:HP], w).then_inc(made, 1)

                def emit(t, j, q):
                    if live(t, -3, TILES):
                        make(t + 3, (j + 3) % U)

                for t in range(3):
                    make(t, t)
                pool.wait_ge(made, 3)
                pool.memset(MSG[0:1, 0, :], 0.0).then_inc(carried, 1)
                steps(pool, own, (2 * Q, 2 * Q), (node.part, tiles, table), ((idle, emit, write), (idle, emit, read)), (half,))

            @block.sync
            def _(sp):
                own = Own(sp, turn_s, turn_s)

                def load_ids(n, b):
                    sp.dma_start(MB[:, b, :, :].rearrange("p k m -> p (k m)"), ids_v[bass.ds(n, 1), :].to_broadcast([P, G * P])).then_inc(ids[b], 16)

                def load_rows(n, b):
                    sp.dma_start(XD[:, b, :, :], rows_v[bass.ds(n, 1), :, :, :].rearrange("q p k d -> (q p) k d")).then_inc(rows_in[b], 16)

                def emit(t, j, q):
                    b = j // G
                    if j % G == 0 and live(t, -G, TILES):
                        at_least(sp, matched, t, turn_s)
                        load_ids(2 * q + b + 1, 1 - b)
                    if j % G == 3 and live(t, 3 + G, TILES + G):
                        n = 2 * q + b - 1
                        at_least(sp, z_ready, t - 3, turn_s)
                        sp.dma_start(rows_v[bass.ds(n, 1), :, :, :].rearrange("q p k d -> (q p) k d"), XD[:, 1 - b, :, :]).then_inc(kept[1 - b], 16)
                    if j % G == 4 and live(t, -1, TILES):
                        at_least(sp, kept[1 - b], arrivals(j, q, U, G), turn_s)
                        load_rows(2 * q + b + 1, 1 - b)
                load_ids(0, 0)
                load_rows(0, 0)
                node.sync_start(own)
                steps(sp, own, 0, parts, (node.sync(own), emit))
                for b in range(2):
                    sp.wait_ge(kept[b], 16 * (QS // 2))

            @block.tensor
            def _(pe):
                own = Own(pe, turn_e, None)

                def emit(t, j, q):
                    if live(t, 0, TILES):
                        at_least(pe, made, t + 1)
                        at_least(pe, matched, t + 1)
                        at_least(pe, carried, t + 1)
                        at_least(pe, scaled, t)
                        pe.matmul(ps[:, 5, 0:HP], S[:, j % G, :], MSG[:, j % G, :], start=True, stop=True).then_inc(summed, 1)
                    if live(t, 1, TILES):
                        at_least(pe, scaled, t)
                        at_least(pe, at_ready, t - 1)
                        o = (j - 1) % 2
                        for h in range(2):
                            last = pe.transpose(ps[:, 6, h * P:(h + 1) * P], AG[:, o, h * P:(h + 1) * P], c.ident[:, :])
                        last.then_inc(e_turned, 1)
                    if live(t, 2, TILES):
                        at_least(pe, at_ready, t - 1)
                        at_least(pe, z_ready, t - 2)
                        for h in range(2):
                            last = pe.matmul(ps[:, 7, 0:D], AT[:, j % 2, h * P:(h + 1) * P], c.wo[:, h, :], start=(h == 0), stop=(h == 1))
                        last.then_inc(e_product, 1)
                steps(pe, own, 0, parts, (node.tensor(own), emit))

            @block.scalar
            def _(act):
                own = Own(act, turn_a, turn_a)

                def emit(t, j, q):
                    if live(t, 0, TILES - 1):
                        at_least(act, made, t + 2)
                        at_least(act, summed, t + 1)
                        act.activation(MSG[0:1, (j + 1) % G, :], ps[0:1, 5, 0:HP], ACT.Copy).then_inc(carried, 1)
                    if live(t, 1, TILES):
                        o = (j - 1) % 2
                        at_least(act, e_turned, t)
                        at_least(act, e_product, t - 2)
                        act.activation(AT[:, o, :], ps[:, 6, 0:D], ACT.Copy).then_inc(at_ready, 1)
                steps(act, own, 0, parts, (node.scalar(own), emit))
                node.scalar_end(act)

            @block.vector
            def _(dve):
                own = Own(dve, dve_own, turn_d)

                def match(t, j, arrived):
                    if j % G == 0:
                        at_least(dve, ids[j // G], arrived)
                    at_least(dve, summed, t - G + 1)
                    dve.tensor_scalar(S[:, j % G, :], MB[:, j // G, j % G, :], c.row_ids[:, bass.ds(t, 1)], None, ALU.is_equal).then_inc(matched, 1)

                def sums(t, j):
                    if not live(t, 0, TILES):
                        return
                    o = j % 2
                    if isinstance(t, int) and t == TILES - 1:
                        dve.wait_ge(summed, TILES)
                    else:
                        at_least(dve, carried, t + 2)
                    at_least(dve, e_turned, t - 1)
                    own(dve.tensor_scalar(rec[:, o, :], ps[:, 5, D:HP], 1e-8, None, ALU.add))
                    n = own.n
                    yield
                    own.upto(n)
                    own(dve.reciprocal(rec[:, o, :], rec[:, o, :]))
                    n = own.n
                    yield
                    own.upto(n)
                    dve.tensor_tensor(AG[:, o, :].rearrange("p (h d) -> p h d", h=H), ps[:, 5, 0:D].rearrange("p (h d) -> p h d", h=H),
                                      rec[:, o, :].unsqueeze(2).to_broadcast([P, H, HD]), ALU.mult).then_inc(scaled, 1)
                    yield

                def results(t, j, q):
                    if live(t, 3, TILES):
                        n = (j - 3) % U
                        if n % G == 0:
                            at_least(dve, rows_in[n // G], arrivals(j, q, U, 3))
                        at_least(dve, e_product, t - 2)
                        dve.tensor_tensor(XD[:, n // G, n % G, :], ps[:, 7, 0:D], XD[:, n // G, n % G, :], ALU.add).then_inc(z_ready, 1)
                        yield
                    if live(t, -2, TILES):
                        match(t + 2, (j + 2) % U, arrivals(j, q, U, -2))
                        yield

                def emit(t, j, q):
                    yield from weave(results(t, j, q), sums(t, j))

                for t in range(2):
                    match(t, t, 16)
                node.vector_start(own)
                steps(dve, own, node.DVE + U * 2, parts, (node.vector(own), emit))


def message_pass(nc, c, io, out):
    R, AHEAD = 4, 3
    U = R * G
    c.passes += 1
    with ExitStack() as ctx:
        def sb(name, shape, dt=F32):
            return ctx.enter_context(nc.sbuf_tensor(c.name(name), shape, dt))

        def sem(name):
            return c.semaphore(nc, ctx, name)

        Z = sb("Z", [P, R, G, 2, D])
        AT = sb("AT", [P, R, G, RAD + 1])
        ZT = sb("ZT", [P, 2, 2 * D])
        ET = sb("ET", [RAD + 1, 2, P])
        st = sb("st", [P, G * 2, 6])
        mv = sb("mv", [P, 2, G * 2, 2])
        vv = sb("vv", [P, G * 2])
        r = sb("r", [P, 2, G * 2])
        nm = sb("nm", [P, 2, G * 2])
        tmp = sb("tmp", [P, G * 2])
        Q = sb("Q", [P, 2, DM])
        K = sb("K", [P, 2, DM])
        QK = sb("QK", [P, 2, DM])
        icol = [[sb(f"icol{b}{n}", [P, G], I32) for n in range(2)] for b in range(R)]
        gathered = [sem(f"gathered{b}") for b in range(R)]
        attrs = [sem(f"attrs{b}") for b in range(R)]
        picked, padded, roots, e_normed, a_turned, et_ready, e_turned, zt_ready, e_product, x_kept, kept, k_used, scored, copied, dve_own, turn_e, turn_a, turn_d, turn_s, turn_p = (
            sem(n) for n in ("picked", "padded", "roots", "e_normed", "a_turned", "et_ready", "e_turned", "zt_ready", "e_product", "x_kept", "kept", "k_used", "scored", "copied", "dve_own",
                             "turn_e", "turn_a", "turn_d", "turn_s", "turn_p"))
        ps = c.psum
        attr_v = io["edge_attr_64"].rearrange("(q k e) a -> q e k a", k=G, e=EDGES)
        node = NodePart(nc, c, ctx, io["x"], out, NODE_PARTS[0] + NODE_PARTS[1], NODE_PARTS[2])
        parts = (node.part, Part(TILES, U, 3, AHEAD * G))
        TA = 3 * P
        with nc.Block() as block:
            @block.gpsimd
            def _(pool):
                own = Own(pool, copied, turn_p)

                def gather(n, b):
                    for k, col in enumerate((c.src_pos, c.last_pos)):
                        own(pool.tensor_copy(icol[b][k][:, :], col[:, bass.ds(G * n, G)]))
                    own.done(True)
                    for k in range(G):
                        for side in range(2):
                            pool.indirect_dma_start(out=Z[:, b, k, side, :], out_offset=None, in_=c.rows,
                                                    in_offset=bass.IndirectOffsetOnAxis(ap=icol[b][side][:, k:k + 1], axis=0)).then_inc(gathered[b], 16)

                def emit(t, j, q):
                    if j % G == 0 and live(t, -AHEAD * G, TILES):
                        at_least(pool, e_turned, t - (R - AHEAD) * G + G, turn_p)
                        gather(R * q + j // G + AHEAD, (j // G + AHEAD) % R)
                pool.wait_ge(picked, 2)
                for n in range(AHEAD):
                    gather(n, n)
                steps(pool, own, 2 * R, parts, (idle, emit))

            @block.sync
            def _(sp):
                own = Own(sp, turn_s, turn_s)

                def load(n, b):
                    sp.dma_start(AT[1:1 + EDGES, b, :, 0:RAD], attr_v[bass.ds(n, 1), :, :, :].rearrange("q e k a -> (q e) k a")).then_inc(attrs[b], 16)

                def emit(t, j, q):
                    if j % G == 0 and live(t, -AHEAD * G, TILES):
                        at_least(sp, e_turned, t - (R - AHEAD) * G + G, turn_s)
                        load(R * q + j // G + AHEAD, (j // G + AHEAD) % R)
                node.sync_start(own)
                sp.wait_ge(padded, 2)
                for n in range(AHEAD):
                    load(n, n)
                steps(sp, own, 0, parts, (node.sync(own), emit))

            @block.tensor
            def _(pe):
                own = Own(pe, turn_e, None)

                def emit(t, j, q):
                    if live(t, 0, TILES):
                        b, k = j // G, j % G
                        if k == 0:
                            at_least(pe, attrs[b], arrivals(j, q, U, 0))
                        at_least(pe, x_kept, t - 1)
                        at_least(pe, et_ready, t)
                        pe.transpose(ps[0:RAD + 1, 7, TA:TA + P], AT[:, b, k, :], c.ident[:, :]).then_inc(a_turned, 1)
                        at_least(pe, zt_ready, t)
                        at_least(pe, e_normed, t + 1)
                        for side in range(2):
                            for h in range(2):
                                last = pe.transpose(ps[:, 5, (2 * side + h) * P:(2 * side + h + 1) * P], Z[:, b, k, side, h * P:(h + 1) * P], c.ident[:, :])
                        last.then_inc(e_turned, 1)
                    if live(t, 1, TILES):
                        o = (j - 1) % 2
                        at_least(pe, zt_ready, t)
                        at_least(pe, kept, t - 1)
                        for h in range(2):
                            pe.matmul(ps[:, 6, 0:2 * DM], ZT[:, o, h * P:(h + 1) * P], c.w_kv[:, h, :], start=(h == 0), stop=False)
                        pe.matmul(ps[:, 6, 0:2 * DM], ET[:, o, :], c.we2[:, :], start=False, stop=True)
                        at_least(pe, et_ready, t + 1 if live(t, 0, TILES) else TILES)
                        for h in range(2):
                            last = pe.matmul(ps[:, 7, 0:2 * DM + 1], ZT[:, o, (2 + h) * P:(3 + h) * P], c.w_qs[:, h, :], start=(h == 0), stop=(h == 1))
                        last.then_inc(e_product, 1)
                steps(pe, own, 0, parts, (node.tensor(own), emit))

            @block.scalar
            def _(act):
                own = Own(act, turn_a, turn_a)

                N1 = G - 1

                def normalise(b, k, count):
                    at_least(act, roots, count)
                    for side in range(2):
                        n = 2 * k + side
                        last = act.activation(Z[:, b, k, side, :], Z[:, b, k, side, :], ACT.Identity, bias=nm[:, b % 2, n:n + 1], scale=r[:, b % 2, n:n + 1])
                    last.then_inc(e_normed, 1)

                def emit(t, j, q):
                    if live(t, 2, TILES):
                        o = j % 2
                        here = c.store[:, bass.ds(t - 2, 1), :].rearrange("p a d -> p (a d)")
                        at_least(act, e_product, t - 1, turn_a)
                        at_least(act, k_used, t - 3, turn_a)
                        act.activation(Q[:, o, :], ps[:, 7, 0:DM], ACT.Copy)
                        act.activation(here[:, DM:2 * DM + 1], ps[:, 7, DM:2 * DM + 1], ACT.Copy).then_inc(x_kept, 1)
                        act.activation(K[:, o, :], ps[:, 6, 0:DM], ACT.Copy)
                        act.activation(here[:, 0:DM], ps[:, 6, DM:2 * DM], ACT.Copy).then_inc(kept, 1)
                    if live(t, 0, TILES):
                        o = j % 2
                        at_least(act, a_turned, t + 1)
                        at_least(act, e_product, t - 1)
                        act.activation(ET[:, o, :], ps[0:RAD + 1, 7, TA:TA + P], ACT.Copy).then_inc(et_ready, 1)
                    if live(t, -N1, TILES):
                        m = (j + N1) % U
                        normalise(m // G, m % G, R * q + (j + N1) // G + 1)
                    if live(t, 0, TILES):
                        at_least(act, e_turned, t + 1)
                        act.activation(ZT[:, o, :], ps[:, 5, :], ACT.Copy).then_inc(zt_ready, 1)
                for k in range(N1):
                    normalise(0, k, 1)
                steps(act, own, 0, parts, (node.scalar(own), emit))
                act.wait_ge(kept, TILES)
                node.scalar_end(act)

            @block.vector
            def _(dve):
                own = Own(dve, dve_own, turn_d)
                alt = c.own_pos[:, :]
                dve.tensor_scalar(alt, alt, ROWS, None, ALU.add).then_inc(picked, 1)
                dve.wait_ge(picked, 1)
                dve.tensor_tensor(c.src_pos[:, :], c.src_pos[:, :], alt, ALU.min).then_inc(picked, 1)
                own(dve.memset(AT[:, :, :, :], 0.0))
                own.done()
                dve.memset(AT[:, :, :, RAD:RAD + 1], 1.0).then_inc(padded, 2)

                def statistics(t, j, q):
                    b, k = (j // G + 2) % R, j % G
                    if k == 0:
                        at_least(dve, gathered[b], arrivals(j, q, U, -2 * G, 32 * G))
                    for side in range(2):
                        own(dve.bn_stats(st[:, 2 * k + side, :], Z[:, b, k, side, :]))
                        m = own.n
                        yield
                    own.upto(m, True)
                    for side in range(2):
                        own(dve.bn_aggr(mv[:, b % 2, 2 * k + side, :], st[:, 2 * k + side, :]))
                    yield

                def roots_of(n, w):
                    own.done()
                    own(dve.tensor_scalar(vv[:, :], mv[:, w, :, 1], EPS, None, ALU.add))
                    m = own.n
                    yield
                    own.upto(m)
                    at_least(dve, roots, n)
                    at_least(dve, e_normed, G * (n - 1))
                    yield from rsqrt(own, r[:, w, :], vv[:, :], tmp[:, :])
                    own(dve.scalar_tensor_tensor(out=nm[:, w, :], in0=mv[:, w, :, 0], scalar=-1.0, in1=r[:, w, :], op0=ALU.mult, op1=ALU.mult))
                    m = own.n
                    yield
                    own.upto(m)
                    ones = nm[:, w, :].rearrange("p (k s) -> p k s", s=2)[:, :, 1]
                    dve.tensor_scalar(ones, ones, 1.0, None, ALU.add).then_inc(roots, 1)
                    yield

                def scores(t, j, q):
                    if live(t, -2 * G, TILES):
                        yield from statistics(t, j, q)
                    if live(t, 3, TILES):
                        n, o = t - 3, (j - 3) % 2
                        at_least(dve, kept, t - 2)
                        dve.tensor_tensor(QK[:, o, :], Q[:, o, :], K[:, o, :], ALU.mult).then_inc(k_used, 1)
                        yield
                        at_least(dve, k_used, t - 2, turn_d)
                        dve.tensor_reduce(c.scores[:, bass.ds(n, 1), :].rearrange("p a h -> p (a h)"), QK[:, o, :].rearrange("p (h d) -> p h d", h=H), AX.X, ALU.add).then_inc(scored, 1)
                        yield

                def emit(t, j, q):
                    chain = roots_of(R * q + j // G + 1, (j // G + 1) % 2) if j % G == 0 and live(t, -G, TILES) else None
                    yield from weave(chain, scores(t, j, q))

                node.vector_start(own)
                for t in range(2 * G):
                    for _ in statistics(t - 2 * G, (t - 2 * G) % U, -1):
                        pass
                for _ in roots_of(0, 0):
                    pass
                steps(dve, own, node.DVE + U * 4 + R * 13, parts, (node.vector(own), emit))
                dve.wait_ge(scored, TILES)


def out_pass(nc, c, out):
    c.passes += 1
    R = 4
    U = R * G
    with ExitStack() as ctx:
        def sb(name, shape, dt=F32):
            return ctx.enter_context(nc.sbuf_tensor(c.name(name), shape, dt))

        def sem(name):
            return c.semaphore(nc, ctx, name)

        Z = sb("Z", [P, R, G, D])
        MB = sb("MB", [P, R, G, P])
        S = sb("S", [P, G, P])
        MSG = sb("MSG", [P, G, VP])
        O = sb("O", [P, 4, DM])
        DF = sb("DF", [P, 4, DM])
        OW = sb("OW", [P, 4, DM])
        MX = sb("MX", [P, 2, DM])
        MT = sb("MT", [P, 2, DM])
        rec = sb("rec", [P, 2, H])
        lg = sb("lg", [P, 4, 1])
        be = sb("be", [P, 4, 1])
        st = sb("st", [P, 2, G, 6])
        mv = sb("mv", [P, 2, 2, G, 2])
        vv = sb("vv", [P, 2, G])
        r = sb("r", [P, 2, 2, G])
        nm = sb("nm", [P, 2, 2, G])
        tmp = sb("tmp", [P, 2, G])
        icol = [sb(f"icol{b}", [P, G], I32) for b in range(R)]
        rows = [sem(f"rows{b}") for b in range(R)]
        ids = [sem(f"ids{b}") for b in range(R)]
        scattered = [sem(f"scattered{b}") for b in range(R)]
        roots, finished, made, matched, summed, carried, scaled, logit, beta_ready, mixed, turned, mt_ready, product, z_ready, copied, dve_own, turn_p, turn_e, turn_a, turn_d, turn_s = (
            sem(n) for n in ("roots", "finished", "made", "matched", "summed", "carried", "scaled", "logit", "beta_ready", "mixed", "turned", "mt_ready",
                             "product", "z_ready", "copied", "dve_own", "turn_p", "turn_e", "turn_a", "turn_d", "turn_s"))
        ps = c.psum
        tiles = Part(TILES, U, 9, G)
        ids_v = c.col_ids.rearrange("(q k) m -> q (k m)", k=G)
        rows_v = c.rows[0:ROWS, :].rearrange("(q k p) d -> q p k d", k=G, p=P)


        with nc.Block() as block:
            @block.sync
            def _(sp):
                own = Own(sp, turn_s, None)

                def load(n, b):
                    sp.dma_start(Z[:, b, :, :], rows_v[bass.ds(n, 1), :, :, :].rearrange("q p k d -> (q p) k d")).then_inc(rows[b], 16)
                    sp.dma_start(MB[:, b, :, :].rearrange("p k m -> p (k m)"), ids_v[bass.ds(n, 1), :].to_broadcast([P, G * P])).then_inc(ids[b], 16)

                def emit(t, j, q):
                    if j % G == 3 and live(t, -2 * G + 3, TILES):
                        b = (j // G + 2) % R
                        at_least(sp, scattered[b], arrivals(j // G, q, R, 2, 16 * G), turn_s)
                        at_least(sp, matched, t - 3 - G, turn_s)
                        load(R * q + j // G + 2, b)
                for n in range(2):
                    load(n, n)
                steps(sp, own, 0, (tiles,), (emit,))

            @block.gpsimd
            def _(pool):
                own = Own(pool, copied, turn_p)

                def make(t, j):
                    k = j % G
                    at_least(pool, summed, t - G + 1, turn_p)
                    w = c.weights[:, bass.ds(t, 1), :].rearrange("p a h -> p (a h)")
                    pool.tensor_tensor(MSG[:, k, 0:DM].rearrange("p (h d) -> p h d", h=H),
                                       c.store[:, bass.ds(t, 1), 0:DM].rearrange("p a (h d) -> p (a h) d", h=H),
                                       w.unsqueeze(2).to_broadcast([P, H, CH]), ALU.mult)
                    pool.tensor_copy(MSG[:, k, DM:VP], w).then_inc(made, 1)

                def emit(t, j, q):
                    if live(t, -3, TILES):
                        make(t + 3, (j + 3) % U)
                    k = j % G
                    b, n = (j // G - 2) % R, R * q + j // G - 2
                    if k == 2 and live(t, 2 * G + 2, TILES):
                        at_least(pool, scattered[b], arrivals(j // G, q, R, 2 + R, 16 * G), turn_p)
                        own(pool.tensor_copy(icol[b][:, :], c.last_col[:, bass.ds(G * n, G)]))
                        own.done(True)
                        at_least(pool, finished, n + 3, turn_p)
                    if k in (2, 3) and live(t, 2 * G + k, TILES):
                        for m in range(3) if k == 2 else range(3, G):
                            pool.indirect_dma_start(out=out, out_offset=bass.IndirectOffsetOnAxis(ap=icol[b][:, m:m + 1], axis=0),
                                                    in_=Z[:, b, m, :], in_offset=None, bounds_check=N - 1, oob_is_err=False).then_inc(scattered[b], 16)
                for t in range(3):
                    make(t, t)
                pool.wait_ge(made, 3)
                pool.memset(MSG[0:1, 0, :], 0.0).then_inc(carried, 1)
                steps(pool, own, R, (tiles,), (emit,))
                for b in range(R):
                    pool.wait_ge(scattered[b], 16 * G * QS // R)

            @block.tensor
            def _(pe):
                own = Own(pe, turn_e, None)

                def emit(t, j, q):
                    if live(t, 0, TILES):
                        at_least(pe, made, t + 1)
                        at_least(pe, matched, t + 1)
                        at_least(pe, carried, t + 1)
                        at_least(pe, logit, t - 1)
                        pe.matmul(ps[:, j % 2, 0:VP], S[:, j % G, :], MSG[:, j % G, :], start=True, stop=True).then_inc(summed, 1)
                    if live(t, 3, TILES):
                        at_least(pe, mixed, t - 2)
                        at_least(pe, mt_ready, t - 4)
                        pe.transpose(ps[:, 2 + (j - 3) % 2, 0:DM], MX[:, (j - 3) % 2, :], c.ident[:, :]).then_inc(turned, 1)
                    if live(t, 4, TILES):
                        at_least(pe, mt_ready, t - 3)
                        at_least(pe, z_ready, t - 5)
                        pe.matmul(ps[:, 4 + j % 2, 0:D], MT[:, j % 2, :], c.w_out1[:, 0:D], start=True, stop=True).then_inc(product, 1)
                steps(pe, own, 0, (tiles,), (emit,))

            @block.scalar
            def _(act):
                own = Own(act, turn_a, turn_a)

                def normalise(b, side, w):
                    for k in range(G):
                        last = act.activation(Z[:, b, k, :], Z[:, b, k, :], ACT.Identity, bias=nm[:, w, side, k:k + 1], scale=r[:, w, side, k:k + 1])
                    return last

                def emit(t, j, q):
                    k = j % G
                    if live(t, 0, TILES - 1):
                        at_least(act, made, t + 2)
                        at_least(act, summed, t + 1)
                        act.activation(MSG[0:1, (j + 1) % G, :], ps[0:1, j % 2, 0:VP], ACT.Copy).then_inc(carried, 1)
                    if live(t, 1, TILES):
                        at_least(act, mixed, t - 4, turn_a)
                        at_least(act, logit, t, turn_a)
                        act.activation(be[:, (j - 1) % 4, :], lg[:, (j - 1) % 4, :], ACT.Sigmoid,
                                       bias=c.store[:, bass.ds(t - 1, 1), 2 * DM:2 * DM + 1].rearrange("p a d -> p (a d)")).then_inc(beta_ready, 1)
                    if k == 1 and live(t, 1, TILES + 2 * G):
                        n = R * q + j // G
                        at_least(act, roots, n + 1)
                        if live(t, 1, TILES):
                            last = normalise(j // G, 0, (j // G) % 2)
                        if live(t, 1 + 2 * G, TILES):
                            last = normalise((j // G - 2) % R, 1, (j // G) % 2)
                        last.then_inc(finished, 1)
                    if live(t, 3, TILES):
                        at_least(act, turned, t - 2)
                        at_least(act, product, t - 4)
                        act.activation(MT[:, (j - 3) % 2, :], ps[:, 2 + (j - 3) % 2, 0:DM], ACT.Copy).then_inc(mt_ready, 1)
                steps(act, own, 0, (tiles,), (emit,))

            @block.vector
            def _(dve):
                own = Own(dve, dve_own, turn_d)

                def match(t, j, arrived):
                    if j % G == 0:
                        at_least(dve, ids[j // G], arrived)
                    at_least(dve, summed, t - G + 1)
                    dve.tensor_scalar(S[:, j % G, :], MB[:, j // G, j % G, :], c.row_ids[:, bass.ds(t, 1)], None, ALU.is_equal).then_inc(matched, 1)

                def emit(t, j, q):
                    yield from weave(sums(t, j, q), results(t, j, q), roots_of(t, j, q))

                def sums(t, j, q):
                    o, w = j % 2, j % 4
                    if live(t, 0, TILES):
                        if isinstance(t, int) and t == TILES - 1:
                            dve.wait_ge(summed, TILES)
                        else:
                            at_least(dve, carried, t + 2)
                        own(dve.tensor_scalar(rec[:, o, :], ps[:, o, DM:VP], 1e-16, None, ALU.add))
                        n = own.n
                        yield
                        own.upto(n)
                        own(dve.reciprocal(rec[:, o, :], rec[:, o, :]))
                        n = own.n
                        yield
                        own.upto(n)
                        dve.tensor_tensor(O[:, w, :].rearrange("p (h d) -> p h d", h=H), ps[:, o, 0:DM].rearrange("p (h d) -> p h d", h=H),
                                          rec[:, o, :].unsqueeze(2).to_broadcast([P, H, CH]), ALU.mult).then_inc(scaled, 1)
                        yield
                        at_least(dve, scaled, t + 1)
                        at_least(dve, beta_ready, t - 3)
                        dve.scalar_tensor_tensor(out=OW[:, w, :], in0=O[:, w, :], scalar=1.0, in1=c.wa_row[:, :], op0=ALU.mult, op1=ALU.mult,
                                                 accum_out=lg[:, w, :]).then_inc(logit, 1)
                        yield
                        own(dve.tensor_tensor(DF[:, w, :], c.store[:, bass.ds(t, 1), DM:2 * DM].rearrange("p a d -> p (a d)"), O[:, w, :], ALU.subtract))
                        yield

                def results(t, j, q):
                    k, o, w = j % G, j % 2, (j // G + 1) % 2
                    if live(t, 2, TILES):
                        m = (j - 2) % 4
                        at_least(dve, beta_ready, t - 1)
                        at_least(dve, turned, t - 3)
                        dve.scalar_tensor_tensor(out=MX[:, o, :], in0=DF[:, m, :], scalar=be[:, m, :], in1=O[:, m, :], op0=ALU.mult, op1=ALU.add).then_inc(mixed, 1)
                        yield
                    if live(t, 5, TILES):
                        b = ((j - 5) % U) // G
                        if k == 0:
                            at_least(dve, finished, R * q + j // G)
                        at_least(dve, product, t - 4)
                        dve.tensor_tensor(Z[:, b, k, :], ps[:, 4 + (j - 5) % 2, 0:D], Z[:, b, k, :], ALU.add).then_inc(z_ready, 1)
                        yield
                    if live(t, -5, TILES):
                        b = ((j + G) % U) // G
                        if k == 0:
                            at_least(dve, rows[b], arrivals(j, q, U, -G))
                        own(dve.bn_stats(st[:, 0, k, :], Z[:, b, k, :]))
                        x_at = own.n
                        yield
                    if live(t, 5, TILES):
                        at_least(dve, z_ready, t - 4)
                        own(dve.bn_stats(st[:, 1, k, :], Z[:, ((j - 5) % U) // G, k, :]))
                        z_at = own.n
                        yield
                    if live(t, -2, TILES):
                        match(t + 2, (j + 2) % U, arrivals(j, q, U, -2))
                        yield
                    if live(t, -5, TILES):
                        own.upto(x_at, True)
                        own(dve.bn_aggr(mv[:, w, 0, k, :], st[:, 0, k, :]))
                        yield
                    if live(t, 5, TILES):
                        own.upto(z_at, True)
                        own(dve.bn_aggr(mv[:, w, 1, k, :], st[:, 1, k, :]))
                        yield

                def roots_of(t, j, q):
                    if j % G != 0 or not live(t, 0, TILES + 2 * G):
                        return
                    first, last = live(t, 0, TILES), live(t, 2 * G, TILES)
                    lo, hi = (0 if first else 1), (2 if last else 1)
                    w, n = (j // G) % 2, R * q + j // G
                    v, y, u = vv[:, lo:hi, :], r[:, w, lo:hi, :], tmp[:, lo:hi, :]
                    own.done()
                    own(dve.tensor_scalar(v, mv[:, w, lo:hi, :, 1], EPS, None, ALU.add))
                    m = own.n
                    yield
                    own.upto(m)
                    at_least(dve, roots, n)
                    at_least(dve, finished, n - 1)
                    yield from rsqrt(own, y, v, u)
                    dve.scalar_tensor_tensor(out=nm[:, w, lo:hi, :], in0=mv[:, w, lo:hi, :, 0], scalar=-1.0, in1=y, op0=ALU.mult, op1=ALU.mult).then_inc(roots, 1)
                    yield

                dve.wait_ge(rows[0], 16)
                for k in range(G):
                    own(dve.bn_stats(st[:, 0, k, :], Z[:, 0, k, :]))
                own.done()
                for k in range(G):
                    own(dve.bn_aggr(mv[:, 0, 0, k, :], st[:, 0, k, :]))
                own.done()
                for t in range(2):
                    match(t, t, 16)
                steps(dve, own, U * 7 + R * 12, (tiles,), (emit,))


def build(nc, io, out):
    with ExitStack() as ctx:
        c = Core()

        def sb(name, shape, dt=F32):
            return ctx.enter_context(nc.sbuf_tensor(name, shape, dt))

        c.psum = ctx.enter_context(nc.psum_tensor("banks", [P, 8, 512], F32))
        c.ident = sb("ident", [P, P])
        c.wh = sb("wh", [P, 2, HP])
        c.w_ad = sb("w_ad", [P, 2, H])
        c.wo = sb("wo", [P, 2, D])
        c.w_kv = sb("w_kv", [P, 2, 2 * DM])
        c.w_qs = sb("w_qs", [P, 2, 2 * DM + 1])
        c.bq_xr = sb("bq_xr", [P, 2 * DM + 1])
        c.we2 = sb("we2", [RAD + 1, 2 * DM])
        c.wa_row = sb("wa_row", [P, DM])
        c.wc_row = sb("wc_row", [P, DM])
        c.w_out1 = sb("w_out1", [P, D + 1])
        c.m_ext = sb("m_ext", [P, 2, D + 1])
        c.b_ext = sb("b_ext", [P, D + 1])
        c.src_col = sb("src_col", [P, TILES], I32)
        c.dst_col = sb("dst_col", [P, TILES], I32)
        c.last_col = sb("last_col", [P, TILES], I32)
        c.own_pos = sb("own_pos", [P, TILES], I32)
        c.last_pos = sb("last_pos", [P, TILES], I32)
        c.src_pos = sb("src_pos", [P, TILES], I32)
        c.row_ids = sb("row_ids", [P, TILES])
        c.cut = sb("cut", [TILES, 2, H, EDGES])
        c.open_ = sb("open_", [TILES, 2, EDGES])
        c.whole = sb("whole", [H, 2, TILES])
        c.pos_table = nc.dram_tensor("pos_table", (N, 1), I32, kind="Internal").ap()
        c.col_ids = nc.dram_tensor("col_ids", (TILES, P), F32, kind="Internal").ap()
        c.rows = nc.dram_tensor("rows", (2 * ROWS, D), F32, kind="Internal").ap()

        c.weights = sb("weights", [P, TILES, H])
        c.scores = sb("scores", [P, TILES, H])
        setup(nc, c, io)
        with ExitStack() as scratch:
            scratch_for_max(nc, c, scratch)
            index_pass(nc, c, io)
            position_pass(nc, c)
        c.store = sb("store", [P, TILES, HP])
        score_pass(nc, c, io, out)
        clear_semaphores(nc, c)
        weights_pass(nc, c, lambda h: c.store[:, :, D + h], True, c.weights[:, :, :])
        gather_pass(nc, c, io, out)
        clear_semaphores(nc, c)
        message_pass(nc, c, io, out)
        weights_pass(nc, c, lambda h: c.scores[:, :, h], False, c.weights[:, :, :])
        clear_semaphores(nc, c)
        out_pass(nc, c, out)


INS = ["x", "src", "dst", "edge_attr_64", "L0_gnn_W", "L0_gnn_attn", "L0_gnn_W_out", "L1_gnn_W_edge", "L1_gnn_W_n2m",
       "L1_gnn_Wq", "L1_gnn_bq", "L1_gnn_Wk", "L1_gnn_bk", "L1_gnn_Wv", "L1_gnn_bv", "L1_gnn_We", "L1_gnn_Wskip",
       "L1_gnn_bskip", "L1_gnn_Wbeta", "L1_gnn_W_m2n"]


def kernel(**inputs):
    import numpy as np
    import concourse.bacc as bacc
    from concourse.bass_utils import run_bass_kernel_spmd

    nc = bacc.Bacc("TRN2", target_bir_lowering=False, num_devices=1)
    arrays, io = {}, {}
    for name in INS:
        a = np.ascontiguousarray(inputs[name])
        arrays[f"in_{name}"] = a
        io[name] = nc.dram_tensor(f"in_{name}", a.shape, mybir.dt.from_np(a.dtype), kind="ExternalInput").ap()
    out = nc.dram_tensor("out", (N, D), F32, kind="ExternalOutput").ap()
    build(nc, io, out)
    return run_bass_kernel_spmd(nc, [arrays], core_ids=[0]).results[0]["out"]
```
